# Optimizing a Trainium2 kernel written in Bass

```python
import numpy as np
import jax
import jax.numpy as jnp

def _softmax(x, axis=-1):
    return jax.nn.softmax(x, axis=axis)

def _gelu(x):
    return jax.nn.gelu(x, approximate=True)

def _silu(x):
    return jax.nn.silu(x)

def _sigmoid(x):
    return jax.nn.sigmoid(x)

def _layernorm(x, axis=-1, eps=1e-05):
    m = jnp.mean(x, axis=axis, keepdims=True)
    v = jnp.var(x, axis=axis, keepdims=True)
    return (x - m) / jnp.sqrt(v + eps)

def _scatter_add(tgt, idx, src, axis=0):
    return tgt.at[idx].add(src)

def _segment_sum(src, seg, n):
    return jax.ops.segment_sum(src, seg, n)
kernel_name = 'mk_hybrid_d4_jaxref_r8_d95820'

def setup_inputs(seed: int=0):
    np.random.seed(seed)
    _w = jnp.asarray

    def _L0_attn_a_setup():
        import jax, jax.numpy as jnp
        import numpy as np
        from jax import lax
        D_MODEL = 128
        D_STATE = 16
        D_CONV = 4
        EXPAND = 2
        D_INNER = EXPAND * D_MODEL
        DT_RANK = -(-D_MODEL // 16)
        B, L = (2, 128)

        def _selective_scan(u, delta, a, b, c):
            deltaA = jnp.exp(jnp.einsum('bld,dn->bldn', delta, a))
            deltaBu = jnp.einsum('bld,bln,bld->bldn', delta, b, u)

            def step(h, inp):
                dA_t, dBu_t, c_t = inp
                h = dA_t * h + dBu_t
                y = jnp.einsum('bdn,bn->bd', h, c_t)
                return (h, y)
            h0 = jnp.zeros((u.shape[0], u.shape[2], a.shape[1]), dtype=u.dtype)
            xs = (jnp.moveaxis(deltaA, 1, 0), jnp.moveaxis(deltaBu, 1, 0), jnp.moveaxis(c, 1, 0))
            _, ys = lax.scan(step, h0, xs)
            return jnp.moveaxis(ys, 0, 1)
        key = jax.random.key(seed)
        ks = jax.random.split(key, 10)
        s = 0.02
        x = jax.random.normal(ks[0], (B, L, D_MODEL), dtype=jnp.float32)
        in_proj_w = jax.random.normal(ks[1], (2 * D_INNER, D_MODEL), dtype=jnp.float32) * s
        in_proj_b = jnp.zeros((2 * D_INNER,), dtype=jnp.float32)
        conv_w = jax.random.normal(ks[2], (D_INNER, 1, D_CONV), dtype=jnp.float32) * 0.1
        conv_b = jnp.zeros((D_INNER,), dtype=jnp.float32)
        x_proj_w = jax.random.normal(ks[3], (DT_RANK + 2 * D_STATE, D_INNER), dtype=jnp.float32) * s
        dt_proj_w = jax.random.normal(ks[4], (D_INNER, DT_RANK), dtype=jnp.float32) * s
        dt_proj_b = jnp.zeros((D_INNER,), dtype=jnp.float32)
        A_log = jnp.log(jnp.broadcast_to(jnp.arange(1, D_STATE + 1, dtype=jnp.float32), (D_INNER, D_STATE)))
        D_param = jnp.ones((D_INNER,), dtype=jnp.float32)
        out_proj_w = jax.random.normal(ks[5], (D_MODEL, D_INNER), dtype=jnp.float32) * s
        out_proj_b = jnp.zeros((D_MODEL,), dtype=jnp.float32)
        return dict(x=x, in_proj_w=in_proj_w, in_proj_b=in_proj_b, conv_w=conv_w, conv_b=conv_b, x_proj_w=x_proj_w, dt_proj_w=dt_proj_w, dt_proj_b=dt_proj_b, A_log=A_log, D_param=D_param, out_proj_w=out_proj_w, out_proj_b=out_proj_b)
    _L0_attn_a_in = _L0_attn_a_setup()

    def _L0_attn_b_setup():
        import jax, jax.numpy as jnp
        import numpy as np
        import math
        N_EMBD = 128
        N_HEAD = 16
        N_LAYER = 12
        key = jax.random.key(seed)
        kx, kw, kb = jax.random.split(key, 3)
        B, T, C = (4, 256, N_EMBD)
        x = jax.random.normal(kx, (B, T, C), dtype=jnp.float32)
        bound = 1.0 / math.sqrt(C)
        W = jax.random.uniform(kw, (3 * C, C), minval=-bound, maxval=bound, dtype=jnp.float32)
        W = W * (1.0 / math.sqrt(N_LAYER * 2))
        b = jax.random.uniform(kb, (3 * C,), minval=-bound, maxval=bound, dtype=jnp.float32)
        return {'x': x, 'W': W, 'b': b}
    _L0_attn_b_in = _L0_attn_b_setup()

    def _L0_ffn_setup():
        import jax, jax.numpy as jnp
        import numpy as np
        NQ, NK, H, DH = (128, 64, 8, 64)
        key = jax.random.key(seed)
        ks = jax.random.split(key, 8)
        b, n, d, g = (4, 512, 128, 4)
        di = H * DH
        s = lambda fan: 1.0 / np.sqrt(fan)
        return {'x': jax.random.normal(ks[0], (b, n, d), jnp.float32), 'w_qr': jax.random.normal(ks[1], (g, d), jnp.float32) * s(d), 'w_kvr': jax.random.normal(ks[2], (g, d), jnp.float32) * s(d), 'w_q': jax.random.normal(ks[3], (g, di, d), jnp.float32) * s(d), 'w_kv': jax.random.normal(ks[4], (g, 2 * di, d), jnp.float32) * s(d), 'w_out': jax.random.normal(ks[5], (g, d, di), jnp.float32) * s(di), 'null_kv': jax.random.normal(ks[6], (2, g, H, 1, DH), jnp.float32), 'null_token': jax.random.normal(ks[7], (1, 1, d), jnp.float32)}
    _L0_ffn_in = _L0_ffn_setup()

    def _L1_attn_a_setup():
        import jax, jax.numpy as jnp
        import numpy as np
        B, S, D = (4, 256, 128)
        SCALE = 1.0 / np.sqrt(D)
        key = jax.random.key(seed)
        k1, k2, k3 = jax.random.split(key, 3)
        x = jax.random.normal(k1, (B, S, D), dtype=jnp.float32)
        bound = 1.0 / np.sqrt(D)
        W_qk = jax.random.uniform(k2, (D, D), minval=-bound, maxval=bound, dtype=jnp.float32)
        W_v = jax.random.uniform(k3, (D, D), minval=-bound, maxval=bound, dtype=jnp.float32)
        alibi_slope = jnp.full((1,), 0.5, dtype=jnp.float32)
        return {'x': x, 'W_qk': W_qk, 'W_v': W_v, 'alibi_slope': alibi_slope}
    _L1_attn_a_in = _L1_attn_a_setup()

    def _L1_attn_b_setup():
        import jax, jax.numpy as jnp
        import numpy as np
        N_HEAD = 16
        CHUNK = 128

        def _phi(x):
            return jax.nn.elu(x) + 1.0

        def _causal_linear_attn(qp, kp, v):
            B, H, T, D = qp.shape
            NC = T // CHUNK

            def to_chunks(a):
                return a.reshape(B, H, NC, CHUNK, D).transpose(2, 0, 1, 3, 4)
            qc, kc, vc = (to_chunks(qp), to_chunks(kp), to_chunks(v))
            mask = jnp.tril(jnp.ones((CHUNK, CHUNK), dtype=bool))

            def step(carry, blk):
                S, z = carry
                q_c, k_c, v_c = blk
                scores = jnp.einsum('bhcd,bhkd->bhck', q_c, k_c)
                scores = jnp.where(mask, scores, 0.0)
                num = jnp.einsum('bhck,bhke->bhce', scores, v_c) + jnp.einsum('bhcd,bhde->bhce', q_c, S)
                den = scores.sum(-1) + jnp.einsum('bhcd,bhd->bhc', q_c, z)
                S = S + jnp.einsum('bhkd,bhke->bhde', k_c, v_c)
                z = z + k_c.sum(axis=2)
                return ((S, z), (num, den))
            S0 = jnp.zeros((B, H, D, D), dtype=qp.dtype)
            z0 = jnp.zeros((B, H, D), dtype=qp.dtype)
            _, (num, den) = jax.lax.scan(step, (S0, z0), (qc, kc, vc))
            y = num / (den[..., None] + 1e-06)
            y = y.transpose(1, 2, 0, 3, 4).reshape(B, H, T, D)
            return y
        key = jax.random.key(seed)
        k1, k2, k3 = jax.random.split(key, 3)
        B, T, E = (4, 256, 128)
        x = jax.random.normal(k1, (B, T, E), dtype=jnp.float32)
        w_attn = jax.random.normal(k2, (3 * E, E), dtype=jnp.float32) * 0.02
        w_proj = jax.random.normal(k3, (E, E), dtype=jnp.float32) * 0.02
        return {'x': x, 'w_attn': w_attn, 'w_proj': w_proj}
    _L1_attn_b_in = _L1_attn_b_setup()

    def _L1_ffn_setup():
        import jax, jax.numpy as jnp
        import numpy as np
        DIM = 128

        def _reference_tuple_inner(x, W_r, W_k, W_v, mu_r, mu_k):
            B, T, C = x.shape
            x_prev = jnp.concatenate([jnp.zeros((B, 1, C), x.dtype), x[:, :-1, :]], axis=1)
            xr = mu_r * x + (1.0 - mu_r) * x_prev
            xk = mu_k * x + (1.0 - mu_k) * x_prev
            r = jax.nn.sigmoid(jnp.einsum('btc,dc->btd', xr, W_r))
            k = jnp.einsum('btc,dc->btd', xk, W_k)
            k_act = jnp.square(jax.nn.relu(k))
            out = r * jnp.einsum('btc,dc->btd', k_act, W_v)
            new_state = x[:, -1, :]
            return (out, new_state)
        key = jax.random.key(seed)
        ks = jax.random.split(key, 6)
        B, T, C = (8, 256, DIM)
        x = jax.random.normal(ks[0], (B, T, C), dtype=jnp.float32)
        s = 1.0 / np.sqrt(C)
        W_r = jax.random.uniform(ks[1], (C, C), jnp.float32, -s, s)
        W_k = jax.random.uniform(ks[2], (C, C), jnp.float32, -s, s)
        W_v = jax.random.uniform(ks[3], (C, C), jnp.float32, -s, s)
        mu_r = jax.random.uniform(ks[4], (C,), jnp.float32)
        mu_k = jax.random.uniform(ks[5], (C,), jnp.float32)
        return {'x': x, 'W_r': W_r, 'W_k': W_k, 'W_v': W_v, 'mu_r': mu_r, 'mu_k': mu_k}
    _L1_ffn_in = _L1_ffn_setup()

    def _L2_attn_a_setup():
        import jax, jax.numpy as jnp
        import numpy as np
        import math
        DIM = 128
        NUM_HEADS = 16
        HEAD_DIM = DIM // NUM_HEADS
        BATCH = 4
        SEQ = 512

        def _feature_map(x, R):
            x = x / math.sqrt(HEAD_DIM)
            proj = jnp.einsum('bhnd,dm->bhnm', x, R)
            sq_norm = jnp.sum(x * x, axis=-1, keepdims=True)
            return jnp.exp(proj - 0.5 * sq_norm)
        key = jax.random.key(seed)
        ks = jax.random.split(key, 10)
        s = 1.0 / math.sqrt(DIM)
        return {'x': jax.random.normal(ks[0], (BATCH, SEQ, DIM), dtype=jnp.float32), 'Wq': jax.random.normal(ks[1], (DIM, DIM), dtype=jnp.float32) * s, 'bq': jax.random.normal(ks[2], (DIM,), dtype=jnp.float32) * 0.01, 'Wk': jax.random.normal(ks[3], (DIM, DIM), dtype=jnp.float32) * s, 'bk': jax.random.normal(ks[4], (DIM,), dtype=jnp.float32) * 0.01, 'Wv': jax.random.normal(ks[5], (DIM, DIM), dtype=jnp.float32) * s, 'bv': jax.random.normal(ks[6], (DIM,), dtype=jnp.float32) * 0.01, 'Wo': jax.random.normal(ks[7], (DIM, DIM), dtype=jnp.float32) * s, 'bo': jax.random.normal(ks[8], (DIM,), dtype=jnp.float32) * 0.01, 'R': jax.random.normal(ks[9], (HEAD_DIM, HEAD_DIM), dtype=jnp.float32) * 0.4}
    _L2_attn_a_in = _L2_attn_a_setup()

    def _L2_attn_b_setup():
        import jax, jax.numpy as jnp
        import numpy as np
        NUM_HEADS = 16
        DIM = 128
        key = jax.random.key(seed)
        kx, kwq, kbq, kwk, kbk = jax.random.split(key, 5)
        B, N, C = (2, 256, DIM)
        s = 1.0 / np.sqrt(C)
        return {'x': jax.random.normal(kx, (B, N, C), dtype=jnp.float32), 'Wq': jax.random.normal(kwq, (C, C), dtype=jnp.float32) * s, 'bq': jax.random.normal(kbq, (C,), dtype=jnp.float32) * 0.01, 'Wk': jax.random.normal(kwk, (C, C), dtype=jnp.float32) * s, 'bk': jax.random.normal(kbk, (C,), dtype=jnp.float32) * 0.01}
    _L2_attn_b_in = _L2_attn_b_setup()

    def _L2_ffn_setup():
        import jax, jax.numpy as jnp
        import numpy as np
        E = 8
        C = 160
        D = 128
        H = 512
        B, S = (4, 256)
        key = jax.random.key(seed)
        ks = jax.random.split(key, 12)
        sc = 0.02
        return {'input': jax.random.normal(ks[0], (B, S, D), jnp.float32), 'router_w': jax.random.normal(ks[1], (D, E), jnp.float32) * sc, 'router_b': jnp.zeros((E,), jnp.float32), 'w1': jax.random.normal(ks[2], (E, D, H), jnp.float32) * sc, 'b1': jnp.zeros((E, H), jnp.float32), 'w2': jax.random.normal(ks[3], (E, H, D), jnp.float32) * sc, 'b2': jnp.zeros((E, D), jnp.float32), 'ow1': jax.random.normal(ks[4], (D, H), jnp.float32) * sc, 'ob1': jnp.zeros((H,), jnp.float32), 'ow2': jax.random.normal(ks[5], (H, D), jnp.float32) * sc, 'ob2': jnp.zeros((D,), jnp.float32)}
    _L2_ffn_in = _L2_ffn_setup()

    def _L3_attn_a_setup():
        import jax, jax.numpy as jnp
        import numpy as np
        D_MODEL, D_K, D_V, H = (128, 64, 64, 16)
        B, N = (2, 256)
        key = jax.random.key(seed)
        ks = jax.random.split(key, 5)
        y = jax.random.normal(ks[0], (B, N, D_MODEL), dtype=jnp.float32)
        Wq = 0.001 * jax.random.normal(ks[1], (H * D_K, D_MODEL), dtype=jnp.float32)
        Wk = 0.001 * jax.random.normal(ks[2], (H * D_K, D_MODEL), dtype=jnp.float32)
        Wv = 0.001 * jax.random.normal(ks[3], (H * D_V, D_MODEL), dtype=jnp.float32)
        Wo = 0.001 * jax.random.normal(ks[4], (D_MODEL, H * D_V), dtype=jnp.float32)
        bq = jnp.zeros((H * D_K,), jnp.float32)
        bk = jnp.zeros((H * D_K,), jnp.float32)
        bv = jnp.zeros((H * D_V,), jnp.float32)
        bo = jnp.zeros((D_MODEL,), jnp.float32)
        return {'y': y, 'Wq': Wq, 'bq': bq, 'Wk': Wk, 'bk': bk, 'Wv': Wv, 'bv': bv, 'Wo': Wo, 'bo': bo}
    _L3_attn_a_in = _L3_attn_a_setup()

    def _L3_attn_b_setup():
        import math
        import jax, jax.numpy as jnp
        import numpy as np
        H = 16
        WIN = 64
        BS = 64

        def _sliding_window_attn(q, k, v):
            B, Hn, T, hd = q.shape
            nb = T // BS
            nw1 = WIN // BS + 1
            scale = 1.0 / math.sqrt(hd)
            qb = q.reshape(B, Hn, nb, BS, hd)
            kb = k.reshape(B, Hn, nb, BS, hd)
            vb = v.reshape(B, Hn, nb, BS, hd)
            offs = jnp.arange(-(WIN // BS), 1)
            idx_raw = jnp.arange(nb)[:, None] + offs[None, :]
            idx = jnp.clip(idx_raw, 0, nb - 1)
            kg = jnp.take(kb, idx, axis=2)
            vg = jnp.take(vb, idx, axis=2)
            scores = jnp.einsum('bhnqd,bhnwkd->bhnqwk', qb, kg) * scale
            qpos = (jnp.arange(nb) * BS)[:, None, None, None] + jnp.arange(BS)[None, :, None, None]
            kpos = (idx_raw * BS)[:, None, :, None] + jnp.arange(BS)[None, None, None, :]
            valid = (idx_raw[:, None, :, None] >= 0) & (kpos <= qpos) & (qpos - kpos < WIN)
            scores = jnp.where(valid[None, None], scores, -1000000000.0)
            p = jax.nn.softmax(scores.reshape(B, Hn, nb, BS, nw1 * BS), axis=-1)
            p = p.reshape(B, Hn, nb, BS, nw1, BS)
            out = jnp.einsum('bhnqwk,bhnwkd->bhnqd', p, vg)
            return out.reshape(B, Hn, T, hd)
        key = jax.random.key(seed)
        ks = jax.random.split(key, 5)
        B, T, D = (2, 512, 128)
        x = jax.random.normal(ks[0], (B, T, D), dtype=jnp.float32)
        init = 0.02
        Wq = jax.random.normal(ks[1], (D, D), dtype=jnp.float32) * init
        Wk = jax.random.normal(ks[2], (D, D), dtype=jnp.float32) * init
        Wv = jax.random.normal(ks[3], (D, D), dtype=jnp.float32) * init
        Wo = jax.random.normal(ks[4], (D, D), dtype=jnp.float32) * init
        return {'x': x, 'Wq': Wq, 'Wk': Wk, 'Wv': Wv, 'Wo': Wo}
    _L3_attn_b_in = _L3_attn_b_setup()

    def _L3_ffn_setup():
        import jax, jax.numpy as jnp
        import numpy as np
        B, S, D = (8, 64, 128)
        H = 16
        DFF = 512
        E = 4
        K = 2
        EPS = 1e-05

        def _layernorm(x, w, b):
            m = x.mean(-1, keepdims=True)
            v = ((x - m) ** 2).mean(-1, keepdims=True)
            return (x - m) / jnp.sqrt(v + EPS) * w + b

        def _encoder_layer(x, iw, ib, ow, ob, l1w, l1b, l2w, l2b, n1w, n1b, n2w, n2b):
            b, s, d = x.shape
            hd = d // H
            qkv = x @ iw.T + ib
            q, k, v = jnp.split(qkv, 3, axis=-1)
            rs = lambda t: t.reshape(b, s, H, hd).transpose(0, 2, 1, 3)
            q, k, v = (rs(q), rs(k), rs(v))
            scale = jnp.asarray(hd, x.dtype) ** 0.5
            scores = jnp.einsum('bhqd,bhkd->bhqk', q, k) / scale
            attn = jax.nn.softmax(scores, axis=-1)
            o = jnp.einsum('bhqk,bhkd->bhqd', attn, v).transpose(0, 2, 1, 3).reshape(b, s, d)
            o = o @ ow.T + ob
            x = _layernorm(x + o, n1w, n1b)
            ff = jax.nn.relu(x @ l1w.T + l1b) @ l2w.T + l2b
            return _layernorm(x + ff, n2w, n2b)
        key = jax.random.key(seed)
        ks = jax.random.split(key, 12)
        g = lambda k, shape: jax.random.normal(k, shape, dtype=jnp.float32) * 0.02
        return {'x': jax.random.normal(ks[0], (B, S, D), dtype=jnp.float32), 'in_proj_w': g(ks[1], (E, 3 * D, D)), 'in_proj_b': g(ks[2], (E, 3 * D)), 'out_proj_w': g(ks[3], (E, D, D)), 'out_proj_b': g(ks[4], (E, D)), 'ln1_w': jnp.ones((E, D), jnp.float32), 'ln1_b': jnp.zeros((E, D), jnp.float32), 'lin1_w': g(ks[5], (E, DFF, D)), 'lin1_b': g(ks[6], (E, DFF)), 'lin2_w': g(ks[7], (E, D, DFF)), 'lin2_b': g(ks[8], (E, D)), 'ln2_w': jnp.ones((E, D), jnp.float32), 'ln2_b': jnp.zeros((E, D), jnp.float32), 'gate_w': g(ks[9], (E, D)), 'gate_b': g(ks[10], (E,))}
    _L3_ffn_in = _L3_ffn_setup()
    _d = {'L0_attn_a_x': _L0_attn_a_in['x'], 'L0_attn_a_in_proj_w': _L0_attn_a_in['in_proj_w'], 'L0_attn_a_in_proj_b': _L0_attn_a_in['in_proj_b'], 'L0_attn_a_conv_w': _L0_attn_a_in['conv_w'], 'L0_attn_a_conv_b': _L0_attn_a_in['conv_b'], 'L0_attn_a_x_proj_w': _L0_attn_a_in['x_proj_w'], 'L0_attn_a_dt_proj_w': _L0_attn_a_in['dt_proj_w'], 'L0_attn_a_dt_proj_b': _L0_attn_a_in['dt_proj_b'], 'L0_attn_a_A_log': _L0_attn_a_in['A_log'], 'L0_attn_a_D_param': _L0_attn_a_in['D_param'], 'L0_attn_a_out_proj_w': _L0_attn_a_in['out_proj_w'], 'L0_attn_a_out_proj_b': _L0_attn_a_in['out_proj_b'], 'L0_attn_b_W': _L0_attn_b_in['W'], 'L0_attn_b_b': _L0_attn_b_in['b'], 'L0_ffn_w_qr': _L0_ffn_in['w_qr'], 'L0_ffn_w_kvr': _L0_ffn_in['w_kvr'], 'L0_ffn_w_q': _L0_ffn_in['w_q'], 'L0_ffn_w_kv': _L0_ffn_in['w_kv'], 'L0_ffn_w_out': _L0_ffn_in['w_out'], 'L0_ffn_null_kv': _L0_ffn_in['null_kv'], 'L0_ffn_null_token': _L0_ffn_in['null_token'], 'L1_attn_a_W_qk': _L1_attn_a_in['W_qk'], 'L1_attn_a_W_v': _L1_attn_a_in['W_v'], 'L1_attn_a_alibi_slope': _L1_attn_a_in['alibi_slope'], 'L1_attn_b_w_attn': _L1_attn_b_in['w_attn'], 'L1_attn_b_w_proj': _L1_attn_b_in['w_proj'], 'L1_ffn_W_r': _L1_ffn_in['W_r'], 'L1_ffn_W_k': _L1_ffn_in['W_k'], 'L1_ffn_W_v': _L1_ffn_in['W_v'], 'L1_ffn_mu_r': _L1_ffn_in['mu_r'], 'L1_ffn_mu_k': _L1_ffn_in['mu_k'], 'L2_attn_a_Wq': _L2_attn_a_in['Wq'], 'L2_attn_a_bq': _L2_attn_a_in['bq'], 'L2_attn_a_Wk': _L2_attn_a_in['Wk'], 'L2_attn_a_bk': _L2_attn_a_in['bk'], 'L2_attn_a_Wv': _L2_attn_a_in['Wv'], 'L2_attn_a_bv': _L2_attn_a_in['bv'], 'L2_attn_a_Wo': _L2_attn_a_in['Wo'], 'L2_attn_a_bo': _L2_attn_a_in['bo'], 'L2_attn_a_R': _L2_attn_a_in['R'], 'L2_attn_b_Wq': _L2_attn_b_in['Wq'], 'L2_attn_b_bq': _L2_attn_b_in['bq'], 'L2_attn_b_Wk': _L2_attn_b_in['Wk'], 'L2_attn_b_bk': _L2_attn_b_in['bk'], 'L2_ffn_router_w': _L2_ffn_in['router_w'], 'L2_ffn_router_b': _L2_ffn_in['router_b'], 'L2_ffn_w1': _L2_ffn_in['w1'], 'L2_ffn_b1': _L2_ffn_in['b1'], 'L2_ffn_w2': _L2_ffn_in['w2'], 'L2_ffn_b2': _L2_ffn_in['b2'], 'L2_ffn_ow1': _L2_ffn_in['ow1'], 'L2_ffn_ob1': _L2_ffn_in['ob1'], 'L2_ffn_ow2': _L2_ffn_in['ow2'], 'L2_ffn_ob2': _L2_ffn_in['ob2'], 'L3_attn_a_Wq': _L3_attn_a_in['Wq'], 'L3_attn_a_bq': _L3_attn_a_in['bq'], 'L3_attn_a_Wk': _L3_attn_a_in['Wk'], 'L3_attn_a_bk': _L3_attn_a_in['bk'], 'L3_attn_a_Wv': _L3_attn_a_in['Wv'], 'L3_attn_a_bv': _L3_attn_a_in['bv'], 'L3_attn_a_Wo': _L3_attn_a_in['Wo'], 'L3_attn_a_bo': _L3_attn_a_in['bo'], 'L3_attn_b_Wq': _L3_attn_b_in['Wq'], 'L3_attn_b_Wk': _L3_attn_b_in['Wk'], 'L3_attn_b_Wv': _L3_attn_b_in['Wv'], 'L3_attn_b_Wo': _L3_attn_b_in['Wo'], 'L3_ffn_in_proj_w': _L3_ffn_in['in_proj_w'], 'L3_ffn_in_proj_b': _L3_ffn_in['in_proj_b'], 'L3_ffn_out_proj_w': _L3_ffn_in['out_proj_w'], 'L3_ffn_out_proj_b': _L3_ffn_in['out_proj_b'], 'L3_ffn_ln1_w': _L3_ffn_in['ln1_w'], 'L3_ffn_ln1_b': _L3_ffn_in['ln1_b'], 'L3_ffn_lin1_w': _L3_ffn_in['lin1_w'], 'L3_ffn_lin1_b': _L3_ffn_in['lin1_b'], 'L3_ffn_lin2_w': _L3_ffn_in['lin2_w'], 'L3_ffn_lin2_b': _L3_ffn_in['lin2_b'], 'L3_ffn_ln2_w': _L3_ffn_in['ln2_w'], 'L3_ffn_ln2_b': _L3_ffn_in['ln2_b'], 'L3_ffn_gate_w': _L3_ffn_in['gate_w'], 'L3_ffn_gate_b': _L3_ffn_in['gate_b']}
    _x0 = _d['L0_attn_a_x']
    _d['L0_attn_a_x'] = jax.random.normal(jax.random.fold_in(jax.random.key(seed), 1), (8, 256, 128), dtype=_x0.dtype)
    del _x0
    return _d

def reference(L0_attn_a_x, L0_attn_a_in_proj_w, L0_attn_a_in_proj_b, L0_attn_a_conv_w, L0_attn_a_conv_b, L0_attn_a_x_proj_w, L0_attn_a_dt_proj_w, L0_attn_a_dt_proj_b, L0_attn_a_A_log, L0_attn_a_D_param, L0_attn_a_out_proj_w, L0_attn_a_out_proj_b, L0_attn_b_W, L0_attn_b_b, L0_ffn_w_qr, L0_ffn_w_kvr, L0_ffn_w_q, L0_ffn_w_kv, L0_ffn_w_out, L0_ffn_null_kv, L0_ffn_null_token, L1_attn_a_W_qk, L1_attn_a_W_v, L1_attn_a_alibi_slope, L1_attn_b_w_attn, L1_attn_b_w_proj, L1_ffn_W_r, L1_ffn_W_k, L1_ffn_W_v, L1_ffn_mu_r, L1_ffn_mu_k, L2_attn_a_Wq, L2_attn_a_bq, L2_attn_a_Wk, L2_attn_a_bk, L2_attn_a_Wv, L2_attn_a_bv, L2_attn_a_Wo, L2_attn_a_bo, L2_attn_a_R, L2_attn_b_Wq, L2_attn_b_bq, L2_attn_b_Wk, L2_attn_b_bk, L2_ffn_router_w, L2_ffn_router_b, L2_ffn_w1, L2_ffn_b1, L2_ffn_w2, L2_ffn_b2, L2_ffn_ow1, L2_ffn_ob1, L2_ffn_ow2, L2_ffn_ob2, L3_attn_a_Wq, L3_attn_a_bq, L3_attn_a_Wk, L3_attn_a_bk, L3_attn_a_Wv, L3_attn_a_bv, L3_attn_a_Wo, L3_attn_a_bo, L3_attn_b_Wq, L3_attn_b_Wk, L3_attn_b_Wv, L3_attn_b_Wo, L3_ffn_in_proj_w, L3_ffn_in_proj_b, L3_ffn_out_proj_w, L3_ffn_out_proj_b, L3_ffn_ln1_w, L3_ffn_ln1_b, L3_ffn_lin1_w, L3_ffn_lin1_b, L3_ffn_lin2_w, L3_ffn_lin2_b, L3_ffn_ln2_w, L3_ffn_ln2_b, L3_ffn_gate_w, L3_ffn_gate_b):

    def _L0_attn_a_ref(x, in_proj_w, in_proj_b, conv_w, conv_b, x_proj_w, dt_proj_w, dt_proj_b, A_log, D_param, out_proj_w, out_proj_b):
        import jax, jax.numpy as jnp
        import numpy as np
        from jax import lax
        D_MODEL = 128
        D_STATE = 16
        D_CONV = 4
        EXPAND = 2
        D_INNER = EXPAND * D_MODEL
        DT_RANK = -(-D_MODEL // 16)
        B, L = (2, 128)

        def _selective_scan(u, delta, a, b, c):
            deltaA = jnp.exp(jnp.einsum('bld,dn->bldn', delta, a))
            deltaBu = jnp.einsum('bld,bln,bld->bldn', delta, b, u)

            def step(h, inp):
                dA_t, dBu_t, c_t = inp
                h = dA_t * h + dBu_t
                y = jnp.einsum('bdn,bn->bd', h, c_t)
                return (h, y)
            h0 = jnp.zeros((u.shape[0], u.shape[2], a.shape[1]), dtype=u.dtype)
            xs = (jnp.moveaxis(deltaA, 1, 0), jnp.moveaxis(deltaBu, 1, 0), jnp.moveaxis(c, 1, 0))
            _, ys = lax.scan(step, h0, xs)
            return jnp.moveaxis(ys, 0, 1)
        x_and_res = x @ in_proj_w.T + in_proj_b
        x_b, res = jnp.split(x_and_res, [D_INNER], axis=-1)
        xc = jnp.transpose(x_b, (0, 2, 1))
        xc = lax.conv_general_dilated(xc, conv_w, window_strides=(1,), padding=[(D_CONV - 1, 0)], dimension_numbers=('NCH', 'OIH', 'NCH'), feature_group_count=D_INNER)
        xc = xc + conv_b[None, :, None]
        x_b = jax.nn.silu(jnp.transpose(xc, (0, 2, 1)))
        x_dbl = x_b @ x_proj_w.T
        delta, b, c = jnp.split(x_dbl, [DT_RANK, DT_RANK + D_STATE], axis=-1)
        delta = jax.nn.softplus(delta @ dt_proj_w.T + dt_proj_b)
        a = -jnp.exp(A_log)
        y = _selective_scan(x_b, delta, a, b, c)
        y = y + x_b * D_param
        y = y * jax.nn.silu(res)
        return y @ out_proj_w.T + out_proj_b

    def _L0_attn_b_ref(x, W, b):
        import jax, jax.numpy as jnp
        import numpy as np
        import math
        N_EMBD = 128
        N_HEAD = 16
        N_LAYER = 12
        B, T, C = x.shape
        H = N_HEAD
        D = C // H
        qkv = jnp.einsum('btc,oc->bto', x, W) + b
        q, k, v = jnp.split(qkv, 3, axis=-1)
        q = q.reshape(B, T, H, D).transpose(0, 2, 1, 3)
        k = k.reshape(B, T, H, D).transpose(0, 2, 1, 3)
        v = v.reshape(B, T, H, D).transpose(0, 2, 1, 3)
        att = jnp.einsum('bhtd,bhsd->bhts', q, k) / math.sqrt(D)
        causal = jnp.tril(jnp.ones((T, T), dtype=bool))
        att = jnp.where(causal, att, -jnp.inf)
        att = jax.nn.softmax(att, axis=-1)
        y = jnp.einsum('bhts,bhsd->bhtd', att, v)
        return y.transpose(0, 2, 1, 3).reshape(B, T, C)

    def _L0_ffn_ref(x, w_qr, w_kvr, w_q, w_kv, w_out, null_kv, null_token):
        import jax, jax.numpy as jnp
        import numpy as np
        NQ, NK, H, DH = (128, 64, 8, 64)
        b, n, d = x.shape
        g = w_qr.shape[0]
        bidx = jnp.arange(b)[:, None, None]
        q_logits = jnp.einsum('bnd,gd->bgn', x, w_qr)
        q_top, q_idx = jax.lax.top_k(q_logits, NQ)
        q_scores = jax.nn.sigmoid(q_top)[..., None]
        queries = x[bidx, q_idx]
        kv_logits = jnp.einsum('bnd,gd->bgn', x, w_kvr)
        kv_top, kv_idx = jax.lax.top_k(kv_logits, NK)
        kv_scores = jax.nn.sigmoid(kv_top)[:, :, None, :, None]
        key_values = x[bidx, kv_idx]
        q = jnp.einsum('bgnd,ged->bgne', queries, w_q)
        kv = jnp.einsum('bgnd,ged->bgne', key_values, w_kv)
        k, v = jnp.split(kv, 2, axis=-1)
        heads = lambda t: t.reshape(b, g, -1, H, DH).transpose(0, 1, 3, 2, 4)
        q, k, v = (heads(q), heads(k), heads(v))
        v = v * kv_scores
        nk = jnp.broadcast_to(null_kv[0][None], (b, g, H, 1, DH))
        nv = jnp.broadcast_to(null_kv[1][None], (b, g, H, 1, DH))
        k = jnp.concatenate([nk, k], axis=-2)
        v = jnp.concatenate([nv, v], axis=-2)
        attn = jax.nn.softmax(jnp.einsum('bghid,bghjd->bghij', q, k) * DH ** (-0.5), axis=-1)
        o = jnp.einsum('bghij,bghjd->bghid', attn, v)
        o = o.transpose(0, 1, 3, 2, 4).reshape(b, g, NQ, H * DH)
        o = jnp.einsum('bgne,gde->bgnd', o, w_out)
        o = o * q_scores
        flat_idx = q_idx.reshape(b, g * NQ)
        flat_o = o.reshape(b, g * NQ, d)
        b2 = jnp.arange(b)[:, None]
        summed = jnp.zeros_like(x).at[b2, flat_idx].add(flat_o)
        counts = jnp.zeros((b, n), x.dtype).at[b2, flat_idx].add(1.0)[..., None]
        meaned = summed / jnp.clip(counts, 1e-05)
        return jnp.where(counts > 0, meaned, null_token)

    def _L1_attn_a_ref(x, W_qk, W_v, alibi_slope):
        import jax, jax.numpy as jnp
        import numpy as np
        B, S, D = (4, 256, 128)
        SCALE = 1.0 / np.sqrt(D)
        seq_len = x.shape[1]
        scores = jnp.einsum('bqe,bke->bqk', x @ W_qk, x) * SCALE
        kpos = jnp.arange(seq_len, dtype=x.dtype)[None, :]
        qpos = jnp.arange(seq_len, dtype=x.dtype)[:, None]
        scores = scores + (kpos - qpos) * alibi_slope[0]
        causal = qpos >= kpos
        scores = jnp.where(causal, scores, -jnp.inf)
        attn = jax.nn.softmax(scores, axis=-1)
        v = x @ W_v.T
        return jnp.einsum('bqk,bkd->bqd', attn, v)

    def _L1_attn_b_ref(x, w_attn, w_proj):
        import jax, jax.numpy as jnp
        import numpy as np
        N_HEAD = 16
        CHUNK = 128

        def _phi(x):
            return jax.nn.elu(x) + 1.0

        def _causal_linear_attn(qp, kp, v):
            B, H, T, D = qp.shape
            NC = T // CHUNK

            def to_chunks(a):
                return a.reshape(B, H, NC, CHUNK, D).transpose(2, 0, 1, 3, 4)
            qc, kc, vc = (to_chunks(qp), to_chunks(kp), to_chunks(v))
            mask = jnp.tril(jnp.ones((CHUNK, CHUNK), dtype=bool))

            def step(carry, blk):
                S, z = carry
                q_c, k_c, v_c = blk
                scores = jnp.einsum('bhcd,bhkd->bhck', q_c, k_c)
                scores = jnp.where(mask, scores, 0.0)
                num = jnp.einsum('bhck,bhke->bhce', scores, v_c) + jnp.einsum('bhcd,bhde->bhce', q_c, S)
                den = scores.sum(-1) + jnp.einsum('bhcd,bhd->bhc', q_c, z)
                S = S + jnp.einsum('bhkd,bhke->bhde', k_c, v_c)
                z = z + k_c.sum(axis=2)
                return ((S, z), (num, den))
            S0 = jnp.zeros((B, H, D, D), dtype=qp.dtype)
            z0 = jnp.zeros((B, H, D), dtype=qp.dtype)
            _, (num, den) = jax.lax.scan(step, (S0, z0), (qc, kc, vc))
            y = num / (den[..., None] + 1e-06)
            y = y.transpose(1, 2, 0, 3, 4).reshape(B, H, T, D)
            return y
        B, T, E = x.shape
        H = N_HEAD
        D = E // H
        qkv = x @ w_attn.T
        q, k, v = jnp.split(qkv, 3, axis=2)

        def heads(a):
            return a.reshape(B, T, H, D).transpose(0, 2, 1, 3)
        y = _causal_linear_attn(_phi(heads(q)), _phi(heads(k)), heads(v))
        y = y.transpose(0, 2, 1, 3).reshape(B, T, E)
        return y @ w_proj.T

    def _L1_ffn_ref(x, W_r, W_k, W_v, mu_r, mu_k):
        import jax, jax.numpy as jnp
        import numpy as np
        DIM = 128

        def _reference_tuple_inner(x, W_r, W_k, W_v, mu_r, mu_k):
            B, T, C = x.shape
            x_prev = jnp.concatenate([jnp.zeros((B, 1, C), x.dtype), x[:, :-1, :]], axis=1)
            xr = mu_r * x + (1.0 - mu_r) * x_prev
            xk = mu_k * x + (1.0 - mu_k) * x_prev
            r = jax.nn.sigmoid(jnp.einsum('btc,dc->btd', xr, W_r))
            k = jnp.einsum('btc,dc->btd', xk, W_k)
            k_act = jnp.square(jax.nn.relu(k))
            out = r * jnp.einsum('btc,dc->btd', k_act, W_v)
            new_state = x[:, -1, :]
            return (out, new_state)
        return _reference_tuple_inner(x, W_r, W_k, W_v, mu_r, mu_k)[0]

    def _L2_attn_a_ref(x, Wq, bq, Wk, bk, Wv, bv, Wo, bo, R):
        import jax, jax.numpy as jnp
        import numpy as np
        import math
        DIM = 128
        NUM_HEADS = 16
        HEAD_DIM = DIM // NUM_HEADS
        BATCH = 4
        SEQ = 512

        def _feature_map(x, R):
            x = x / math.sqrt(HEAD_DIM)
            proj = jnp.einsum('bhnd,dm->bhnm', x, R)
            sq_norm = jnp.sum(x * x, axis=-1, keepdims=True)
            return jnp.exp(proj - 0.5 * sq_norm)
        b, n, _ = x.shape
        h, d = (NUM_HEADS, HEAD_DIM)

        def split_heads(t):
            return t.reshape(b, n, h, d).transpose(0, 2, 1, 3)
        q = split_heads(x @ Wq.T + bq)
        k = split_heads(x @ Wk.T + bk)
        v = split_heads(x @ Wv.T + bv)
        q_prime = _feature_map(q, R)
        k_prime = _feature_map(k, R)
        kv = jnp.einsum('bhnd,bhne->bhde', k_prime, v)
        z = 1.0 / (jnp.sum(q_prime, axis=-1) + 1e-08)
        out = jnp.einsum('bhnd,bhde,bhn->bhne', q_prime, kv, z)
        out = out.transpose(0, 2, 1, 3).reshape(b, n, DIM)
        return out @ Wo.T + bo

    def _L2_attn_b_ref(x, Wq, bq, Wk, bk):
        import jax, jax.numpy as jnp
        import numpy as np
        NUM_HEADS = 16
        DIM = 128
        B, N, C = x.shape
        H = NUM_HEADS
        Dh = C // H
        q = (x @ Wq + bq).reshape(B, N, H, Dh).transpose(0, 2, 1, 3)
        k = (x @ Wk + bk).reshape(B, N, H, Dh).transpose(0, 2, 1, 3)
        v = k
        scale = C ** (-0.5)
        attn = jnp.einsum('bhnd,bhmd->bhnm', q, k) * scale
        attn = jax.nn.softmax(attn, axis=-1)
        out = jnp.einsum('bhnm,bhmd->bhnd', attn, v)
        return out.transpose(0, 2, 1, 3).reshape(B, N, C)

    def _L2_ffn_ref(input, router_w, router_b, w1, b1, w2, b2, ow1, ob1, ow2, ob2):
        import jax, jax.numpy as jnp
        import numpy as np
        E = 8
        C = 160
        D = 128
        H = 512
        B, S = (4, 256)
        Bq, Sq, Dq = input.shape
        N = Bq * Sq
        xf = input.reshape(N, Dq)
        probs = jax.nn.softmax(xf @ router_w + router_b, axis=-1)
        eid = jnp.argmax(probs, axis=-1)
        onehot = jax.nn.one_hot(eid, E, dtype=xf.dtype)
        rank = (jnp.cumsum(onehot, axis=0)[jnp.arange(N), eid] - 1.0).astype(jnp.int32)
        valid = rank < C
        pos = jnp.where(valid, rank, 0)
        vmask = valid.astype(xf.dtype)[:, None]
        buf = jnp.zeros((E, C, Dq), xf.dtype).at[eid, pos].add(xf * vmask)
        h = jax.nn.relu(jnp.einsum('ecd,edh->ech', buf, w1) + b1[:, None, :])
        y = jnp.einsum('ech,ehd->ecd', h, w2) + b2[:, None, :]
        y_tok = y[eid, pos] * vmask
        yov = jax.nn.relu(xf @ ow1 + ob1) @ ow2 + ob2
        out = y_tok + yov * (1.0 - vmask)
        return out.reshape(Bq, Sq, Dq)

    def _L3_attn_a_ref(y, Wq, bq, Wk, bk, Wv, bv, Wo, bo):
        import jax, jax.numpy as jnp
        import numpy as np
        D_MODEL, D_K, D_V, H = (128, 64, 64, 16)
        B, N = (2, 256)
        b_s, n, _ = y.shape
        scale = 1.0 / np.sqrt(D_K).astype(np.float32)
        q = (jnp.einsum('bnd,ed->bne', y, Wq) + bq).reshape(b_s, n, H, D_K).transpose(0, 2, 1, 3)
        k = (jnp.einsum('bnd,ed->bne', y, Wk) + bk).reshape(b_s, n, H, D_K).transpose(0, 2, 1, 3)
        v = (jnp.einsum('bnd,ed->bne', y, Wv) + bv).reshape(b_s, n, H, D_V).transpose(0, 2, 1, 3)
        att = jnp.einsum('bhqd,bhkd->bhqk', q, k) * scale
        att = jax.nn.softmax(att, axis=-1)
        out = jnp.einsum('bhqk,bhkd->bhqd', att, v)
        out = out.transpose(0, 2, 1, 3).reshape(b_s, n, H * D_V)
        out = jnp.einsum('bne,de->bnd', out, Wo) + bo
        return out

    def _L3_attn_b_ref(x, Wq, Wk, Wv, Wo):
        import math
        import jax, jax.numpy as jnp
        import numpy as np
        H = 16
        WIN = 64
        BS = 64

        def _sliding_window_attn(q, k, v):
            B, Hn, T, hd = q.shape
            nb = T // BS
            nw1 = WIN // BS + 1
            scale = 1.0 / math.sqrt(hd)
            qb = q.reshape(B, Hn, nb, BS, hd)
            kb = k.reshape(B, Hn, nb, BS, hd)
            vb = v.reshape(B, Hn, nb, BS, hd)
            offs = jnp.arange(-(WIN // BS), 1)
            idx_raw = jnp.arange(nb)[:, None] + offs[None, :]
            idx = jnp.clip(idx_raw, 0, nb - 1)
            kg = jnp.take(kb, idx, axis=2)
            vg = jnp.take(vb, idx, axis=2)
            scores = jnp.einsum('bhnqd,bhnwkd->bhnqwk', qb, kg) * scale
            qpos = (jnp.arange(nb) * BS)[:, None, None, None] + jnp.arange(BS)[None, :, None, None]
            kpos = (idx_raw * BS)[:, None, :, None] + jnp.arange(BS)[None, None, None, :]
            valid = (idx_raw[:, None, :, None] >= 0) & (kpos <= qpos) & (qpos - kpos < WIN)
            scores = jnp.where(valid[None, None], scores, -1000000000.0)
            p = jax.nn.softmax(scores.reshape(B, Hn, nb, BS, nw1 * BS), axis=-1)
            p = p.reshape(B, Hn, nb, BS, nw1, BS)
            out = jnp.einsum('bhnqwk,bhnwkd->bhnqd', p, vg)
            return out.reshape(B, Hn, T, hd)
        B, T, D = x.shape
        hd = D // H

        def proj(W):
            return (x @ W.T).reshape(B, T, H, hd).transpose(0, 2, 1, 3)
        q, k, v = (proj(Wq), proj(Wk), proj(Wv))
        out = _sliding_window_attn(q, k, v)
        out = out.transpose(0, 2, 1, 3).reshape(B, T, D)
        return out @ Wo.T

    def _L3_ffn_ref(x, in_proj_w, in_proj_b, out_proj_w, out_proj_b, ln1_w, ln1_b, lin1_w, lin1_b, lin2_w, lin2_b, ln2_w, ln2_b, gate_w, gate_b):
        import jax, jax.numpy as jnp
        import numpy as np
        B, S, D = (8, 64, 128)
        H = 16
        DFF = 512
        E = 4
        K = 2
        EPS = 1e-05

        def _layernorm(x, w, b):
            m = x.mean(-1, keepdims=True)
            v = ((x - m) ** 2).mean(-1, keepdims=True)
            return (x - m) / jnp.sqrt(v + EPS) * w + b

        def _encoder_layer(x, iw, ib, ow, ob, l1w, l1b, l2w, l2b, n1w, n1b, n2w, n2b):
            b, s, d = x.shape
            hd = d // H
            qkv = x @ iw.T + ib
            q, k, v = jnp.split(qkv, 3, axis=-1)
            rs = lambda t: t.reshape(b, s, H, hd).transpose(0, 2, 1, 3)
            q, k, v = (rs(q), rs(k), rs(v))
            scale = jnp.asarray(hd, x.dtype) ** 0.5
            scores = jnp.einsum('bhqd,bhkd->bhqk', q, k) / scale
            attn = jax.nn.softmax(scores, axis=-1)
            o = jnp.einsum('bhqk,bhkd->bhqd', attn, v).transpose(0, 2, 1, 3).reshape(b, s, d)
            o = o @ ow.T + ob
            x = _layernorm(x + o, n1w, n1b)
            ff = jax.nn.relu(x @ l1w.T + l1b) @ l2w.T + l2b
            return _layernorm(x + ff, n2w, n2b)
        gate_logits = x.mean(axis=1) @ gate_w.T + gate_b
        _, top_idx = jax.lax.top_k(gate_logits, K)
        gate_weights = jax.nn.softmax(gate_logits, axis=-1)
        mask = jnp.zeros_like(gate_weights).at[jnp.arange(x.shape[0])[:, None], top_idx].set(1.0)
        expert_outs = jax.vmap(_encoder_layer, in_axes=(None, 0, 0, 0, 0, 0, 0, 0, 0, 0, 0, 0, 0))(x, in_proj_w, in_proj_b, out_proj_w, out_proj_b, lin1_w, lin1_b, lin2_w, lin2_b, ln1_w, ln1_b, ln2_w, ln2_b)
        return jnp.einsum('be,ebsd->bsd', gate_weights * mask, expert_outs)
    x = L0_attn_a_x
    x = x + _L0_attn_a_ref(_layernorm(x, axis=-1), L0_attn_a_in_proj_w, L0_attn_a_in_proj_b, L0_attn_a_conv_w, L0_attn_a_conv_b, L0_attn_a_x_proj_w, L0_attn_a_dt_proj_w, L0_attn_a_dt_proj_b, L0_attn_a_A_log, L0_attn_a_D_param, L0_attn_a_out_proj_w, L0_attn_a_out_proj_b)
    x = x + _L0_ffn_ref(_layernorm(x, axis=-1), L0_ffn_w_qr, L0_ffn_w_kvr, L0_ffn_w_q, L0_ffn_w_kv, L0_ffn_w_out, L0_ffn_null_kv, L0_ffn_null_token)
    x = x + _L0_attn_b_ref(_layernorm(x, axis=-1), L0_attn_b_W, L0_attn_b_b)
    x = x + _L0_ffn_ref(_layernorm(x, axis=-1), L0_ffn_w_qr, L0_ffn_w_kvr, L0_ffn_w_q, L0_ffn_w_kv, L0_ffn_w_out, L0_ffn_null_kv, L0_ffn_null_token)
    x = x + _L1_attn_a_ref(_layernorm(x, axis=-1), L1_attn_a_W_qk, L1_attn_a_W_v, L1_attn_a_alibi_slope)
    x = x + _L1_ffn_ref(_layernorm(x, axis=-1), L1_ffn_W_r, L1_ffn_W_k, L1_ffn_W_v, L1_ffn_mu_r, L1_ffn_mu_k)
    x = x + _L1_attn_b_ref(_layernorm(x, axis=-1), L1_attn_b_w_attn, L1_attn_b_w_proj)
    x = x + _L1_ffn_ref(_layernorm(x, axis=-1), L1_ffn_W_r, L1_ffn_W_k, L1_ffn_W_v, L1_ffn_mu_r, L1_ffn_mu_k)
    x = x + _L2_attn_a_ref(_layernorm(x, axis=-1), L2_attn_a_Wq, L2_attn_a_bq, L2_attn_a_Wk, L2_attn_a_bk, L2_attn_a_Wv, L2_attn_a_bv, L2_attn_a_Wo, L2_attn_a_bo, L2_attn_a_R)
    x = x + _L2_ffn_ref(_layernorm(x, axis=-1), L2_ffn_router_w, L2_ffn_router_b, L2_ffn_w1, L2_ffn_b1, L2_ffn_w2, L2_ffn_b2, L2_ffn_ow1, L2_ffn_ob1, L2_ffn_ow2, L2_ffn_ob2)
    x = x + _L2_attn_b_ref(_layernorm(x, axis=-1), L2_attn_b_Wq, L2_attn_b_bq, L2_attn_b_Wk, L2_attn_b_bk)
    x = x + _L2_ffn_ref(_layernorm(x, axis=-1), L2_ffn_router_w, L2_ffn_router_b, L2_ffn_w1, L2_ffn_b1, L2_ffn_w2, L2_ffn_b2, L2_ffn_ow1, L2_ffn_ob1, L2_ffn_ow2, L2_ffn_ob2)
    x = x + _L3_attn_a_ref(_layernorm(x, axis=-1), L3_attn_a_Wq, L3_attn_a_bq, L3_attn_a_Wk, L3_attn_a_bk, L3_attn_a_Wv, L3_attn_a_bv, L3_attn_a_Wo, L3_attn_a_bo)
    x = x + _L3_ffn_ref(_layernorm(x, axis=-1), L3_ffn_in_proj_w, L3_ffn_in_proj_b, L3_ffn_out_proj_w, L3_ffn_out_proj_b, L3_ffn_ln1_w, L3_ffn_ln1_b, L3_ffn_lin1_w, L3_ffn_lin1_b, L3_ffn_lin2_w, L3_ffn_lin2_b, L3_ffn_ln2_w, L3_ffn_ln2_b, L3_ffn_gate_w, L3_ffn_gate_b)
    x = x + _L3_attn_b_ref(_layernorm(x, axis=-1), L3_attn_b_Wq, L3_attn_b_Wk, L3_attn_b_Wv, L3_attn_b_Wo)
    x = x + _L3_ffn_ref(_layernorm(x, axis=-1), L3_ffn_in_proj_w, L3_ffn_in_proj_b, L3_ffn_out_proj_w, L3_ffn_out_proj_b, L3_ffn_ln1_w, L3_ffn_ln1_b, L3_ffn_lin1_w, L3_ffn_lin1_b, L3_ffn_lin2_w, L3_ffn_lin2_b, L3_ffn_ln2_w, L3_ffn_ln2_b, L3_ffn_gate_w, L3_ffn_gate_b)
    return x

_drawn_inputs = setup_inputs


def setup_inputs(seed=0):
    import zlib

    import numpy as np

    out = dict(_drawn_inputs(seed))
    spreads = {'L0_attn_a_in_proj_b': (0.0, 0.8),
     'L0_attn_a_conv_b': (0.0, 0.536),
     'L0_attn_a_dt_proj_b': (0.0, 0.8),
     'L0_attn_a_D_param': (1.0, 0.6),
     'L0_attn_a_out_proj_b': (0.0, 0.1),
     'L2_ffn_router_b': (0.0, 0.362),
     'L2_ffn_b1': (0.0, 0.8),
     'L2_ffn_b2': (0.0, 2.0),
     'L2_ffn_ob1': (0.0, 0.8),
     'L2_ffn_ob2': (0.0, 0.8),
     'L3_attn_a_bq': (0.0, 2.0),
     'L3_attn_a_bk': (0.0, 2.0),
     'L3_attn_a_bv': (0.0, 2.0),
     'L3_attn_a_bo': (0.0, 2.0),
     'L3_ffn_ln1_w': (1.0, 0.6),
     'L3_ffn_ln1_b': (0.0, 0.8),
     'L3_ffn_ln2_w': (1.0, 0.6),
     'L3_ffn_ln2_b': (0.0, 0.8)}
    factors = {'L0_attn_a_in_proj_w': 3.536,
     'L0_attn_a_conv_w': 4.851,
     'L0_attn_a_x_proj_w': 8.0,
     'L0_attn_a_dt_proj_w': 8.0,
     'L0_attn_a_A_log': 8.0,
     'L0_attn_a_out_proj_w': 3.784,
     'L1_ffn_W_r': 2.854,
     'L1_ffn_mu_r': 22.727,
     'L2_attn_a_bq': 22.792,
     'L2_attn_a_bk': 8.0,
     'L2_attn_a_bo': 49.917,
     'L2_attn_b_Wq': 95.521,
     'L2_attn_b_bq': 200.0,
     'L2_attn_b_bk': 180.013,
     'L2_ffn_router_w': 8.0,
     'L2_ffn_w1': 8.0,
     'L2_ffn_w2': 8.0,
     'L2_ffn_ow1': 8.0,
     'L2_ffn_ow2': 8.0,
     'L3_attn_a_Wq': 200.0,
     'L3_attn_a_Wk': 200.0,
     'L3_attn_a_Wv': 64.0,
     'L3_attn_a_Wo': 64.0,
     'L3_attn_b_Wq': 8.0,
     'L3_attn_b_Wk': 8.0,
     'L3_attn_b_Wv': 8.0,
     'L3_attn_b_Wo': 8.0,
     'L3_ffn_in_proj_w': 8.0,
     'L3_ffn_in_proj_b': 64.0,
     'L3_ffn_out_proj_w': 8.0,
     'L3_ffn_out_proj_b': 190.927,
     'L3_ffn_lin1_w': 8.0,
     'L3_ffn_lin1_b': 64.0,
     'L3_ffn_lin2_w': 8.0,
     'L3_ffn_lin2_b': 200.0,
     'L3_ffn_gate_w': 22.46,
     'L3_ffn_gate_b': 177.882,
     'L1_attn_b_w_proj': 4.549}
    for name, (base, spread) in spreads.items():
        noise = np.random.default_rng([zlib.crc32(name.encode()), seed]).standard_normal(out[name].shape)
        drawn = base * np.exp(spread * noise) if base else spread * noise
        out[name] = jnp.asarray(drawn.astype(out[name].dtype))
    for name, factor in factors.items():
        out[name] = (out[name] * factor).astype(out[name].dtype)
    return out
```

```python
from contextlib import ExitStack

import concourse.bass as bass
import numpy as np
from concourse import mybir

F32 = mybir.dt.float32
BF16 = mybir.dt.bfloat16
ALU = mybir.AluOpType
ACT = mybir.ActivationFunctionType
AX_X = mybir.AxisListType.X

P = 128
B, T, D = 8, 256, 128
TT = T // P
NT = B * TT
NTOK = B * T
LN_EPS = 1e-5
NEG = -1.0e30
DT_RANK, STATE = 8, 16
HEAD = 8


class Stage:

    def __init__(self, nc, name):
        self.nc, self.name, self.stack, self.sems = nc, name, ExitStack(), []

    def sb(self, name, shape, dt=F32):
        return self.stack.enter_context(self.nc.sbuf_tensor(f"{self.name}_{name}", shape, dt))

    def ps(self, name, shape, dt=F32):
        return self.stack.enter_context(self.nc.psum_tensor(f"{self.name}_{name}", shape, dt))

    def sem(self, name):
        s = self.nc.alloc_semaphore(f"{self.name}_{name}")
        self.sems.append(s)
        return s

    def __enter__(self):
        return self

    def __exit__(self, *a):
        if a[0] is None:
            self.nc.clear_and_free_semaphores(self.sems)
            self.nc.all_engine_barrier()
        self.stack.close()


class Steps:

    def __init__(self, eng, sem):
        self.eng, self.sem, self.n = eng, sem, 0

    def mark(self, ins):
        self.n += 1
        ins.then_inc(self.sem, 1)

    def wait(self):
        self.eng.wait_ge(self.sem, self.n)

    def done(self, ins):
        self.mark(ins)
        self.wait()

    def restart(self):
        self.wait()
        self.eng.sem_clear(self.sem)
        self.n = 0


def layer_norm_stage(nc, g, name):
    with Stage(nc, name) as st:
        stats = st.sb("stats", [P, NT, 6])
        mv = st.sb("mean_var", [P, NT, 2])
        veps = st.sb("veps", [P, NT])
        rstd = st.sb("rstd", [P, NT])
        hTp = st.ps("hTp", [P, 4, 512])
        stats_done, aggr_done, veps_done = st.sem("stats"), st.sem("aggr"), st.sem("veps")
        rstd_done, h_done, turned = st.sem("rstd"), st.sem("h"), st.sem("turned")

        with nc.Block() as block:
            @block.vector
            def _(dve):
                for t in range(NT):
                    dve.bn_stats(stats[:, t, :], g.x[:, t, :]).then_inc(stats_done, 1)
                for t in range(NT):
                    dve.wait_ge(stats_done, t + 1)
                    dve.bn_aggr(mv[:, t, :], stats[:, t, :]).then_inc(aggr_done, 1)
                dve.wait_ge(rstd_done, 1)
                for t in range(NT):
                    dve.tensor_scalar(g.h[:, t, :], g.x[:, t, :], mv[:, t, 0:1], rstd[:, t:t + 1],
                                      ALU.subtract, ALU.mult).then_inc(h_done, 1)

            @block.gpsimd
            def _(pool):
                pool.wait_ge(aggr_done, NT)
                pool.tensor_scalar(veps[:], mv[:, :, 1], LN_EPS, None, ALU.add).then_inc(veps_done, 1)
                pool.wait_ge(veps_done, 1)
                pool.tensor_tensor(rstd[:], veps[:], g.neg_half[:, 0:NT], ALU.pow).then_inc(rstd_done, 1)

            @block.tensor
            def _(pe):
                for t in range(NT):
                    pe.wait_ge(h_done, t + 1)
                    pe.transpose(hTp[:, t // 4, (t % 4) * P:(t % 4 + 1) * P], g.h[:, t, :],
                                 g.ident[:]).then_inc(turned, 1)

            @block.scalar
            def _(act):
                for c in range(4):
                    act.wait_ge(turned, 4 * c + 4)
                    act.activation(g.hT[:, c * 512:(c + 1) * 512], hTp[:, c, :], ACT.Copy)


class Weights:

    def __init__(self):
        self.at, self.n, self.parts = {}, 0, []

    def add(self, name, a):
        a = np.asarray(a)
        assert a.ndim == 2 and a.shape[0] <= P, (name, a.shape)
        self.at[name] = (self.n, a.shape[1], a.shape[0])
        self.n += a.shape[1]
        self.parts.append(a)

    def packed(self):
        out = np.zeros((P, self.n), self.parts[0].dtype)
        c = 0
        for a in self.parts:
            out[:a.shape[0], c:c + a.shape[1]] = a
            c += a.shape[1]
        return out


def linear_attention_stage(nc, g, name, W, hd, scale, mask=None, wo=False, linear=False):
    H = 16
    HP = P // (32 if hd <= 32 else 64)
    HS = P // HP
    NC = H // HP
    NV = H * hd // P
    G = P // hd
    NG = H // G
    NF = 2 * NC + NV
    per = -(-NF // 12)
    NH = 2 * H
    HV = hd + 1 if linear else hd
    keys = {0: (0, P if mask or linear else T), 1: (0, T)}
    with Stage(nc, name) as st:
        hTs = st.sb("hTs", [P, 2, T])
        qT = st.sb("qT", [P, 2, NC, T])
        kT = st.sb("kT", [P, 2, NC, T])
        v = st.sb("v", [P, 2, TT, H, HV])
        ex = st.sb("ex", [P, T]) if linear else None
        bqs = st.sb("bqs", [P, NC])
        negmax = st.sb("negmax", [P, NH, TT])
        sums = st.sb("sums", [P, NH, TT])
        rinv = st.sb("rinv", [P, NH, TT])
        pr = st.sb("pr", [P, 3, TT, T])
        prT = st.sb("prT", [P, 2, 512])
        o = st.sb("o", [P, 2, TT, P])
        oT = st.sb("oT", [P, TT, P])
        S = st.ps("S", [P, 2, 512])
        PT = st.ps("PT", [P, 2, 512])
        FR = st.ps("FR", [P, 512])[:, 0:T]
        Ob = st.ps("O", [P, 2, 512])
        O = [Ob[:, n, 0:TT * G * HV].rearrange("p (t h d) -> p t h d", t=TT, h=G) for n in range(2)]
        Y = st.ps("Y", [P, 2, TT, P])
        OT = [Ob[:, n, T:2 * T].rearrange("p (t n) -> p t n", t=TT) if NG > 1 else Y[:, 0, :, :]
              for n in range(2)]
        names = ["h_copied", "front_mm", "front_cp", "scored", "maxed", "expd", "turned",
                 "prT_cp", "pv", "o_norm", "oT_ps", "oT_cp", "y_ps", "resid", "steps_done", "bias", "phi"]
        (h_copied, front_mm, front_cp, scored, maxed, expd, turned, prT_cp, pv, o_norm,
         oT_ps, oT_cp, y_ps, resid, steps_done, bias, phi) = [st.sem(n) for n in names]
        wq, wk, wv = g.w(W + "wq"), g.w(W + "wk"), g.w(W + "wv")
        bq, bk, bv = (g.w(W + n) if g.has(W + n) else None for n in ("bq", "bk", "bv"))

        def grp(i):
            return i // G

        def body(eng, step):
            with eng.Fori(0, B // 2) as pair:
                for i in range(NH + 6):
                    step(pair, i)

        def fronts(i):
            first = {1: 1, 20: 0}
            for at, par in first.items():
                if at <= i < at + 12:
                    return [(par, s) for s in range((i - at) * per, min((i - at + 1) * per, NF))]
            return []

        with nc.Block() as block:
            @block.gpsimd
            def _(pool):
                pool.sem_inc(h_copied, HEAD)
                pool.tensor_copy(hTs[:, 0, :], g.hT[:, 0:T]).then_inc(h_copied, 1)
                with pool.Fori(0, B // 2) as pair:
                    for par in (1, 0):
                        if par == 1:
                            pool.wait_ge(front_mm, 2 * NF * pair + HEAD)
                        else:
                            pool.wait_ge(front_mm, 2 * NF * pair + HEAD + NF)
                        pool.tensor_copy(hTs[:, par, :], g.hT[:, bass.ds(pair * (2 * T) + (T if par else 2 * T), T)])\
                            .then_inc(h_copied, 1)

            @block.tensor
            def _(pe):
                for s in (front_mm, scored, turned, pv, oT_ps, y_ps):
                    pe.sem_inc(s, HEAD)

                def front(f0, b0, par, s):
                    if s == 0:
                        pe.wait_ge(h_copied, b0 + 1 + HEAD)
                    pe.wait_ge(front_cp, f0 + s + HEAD)
                    out = FR
                    if s < 2 * NC:
                        w = (wq if s < NC else wk)[:, (s % NC) * P:(s % NC + 1) * P]
                        last = pe.matmul(out, w, hTs[:, par, :], start=True, stop=True)
                    else:
                        c = s - 2 * NC
                        for t in range(TT):
                            last = pe.matmul(out[:, t * P:(t + 1) * P], hTs[:, par, t * P:(t + 1) * P],
                                             wv[:, c * P:(c + 1) * P], start=True, stop=bv is None)
                            if bv is not None:
                                last = pe.matmul(out[:, t * P:(t + 1) * P], g.ones[0:1, :],
                                                 bv[0:1, c * P:(c + 1) * P], start=False, stop=True)
                    last.then_inc(front_mm, 1)

                for s in range(NF):
                    front(0, 0, 0, s)

                def step(pair, i):
                    n = pair * NH + (i + HEAD)
                    par, hh = i // H, i % H
                    if i < NH:
                        if hh == 0:
                            pe.wait_ge(front_cp, pair * (2 * NF) + (par + 1) * NF + HEAD)
                            if linear:
                                pe.wait_ge(phi, pair * (4 * NC) + (par + 1) * 2 * NC + HEAD)
                        pe.wait_ge(prT_cp if linear else expd, n - 1)
                        rows = slice(HS * (hh % HP), HS * (hh % HP) + hd)
                        for k in range(TT if linear else 0):
                            last = pe.matmul(S[:, i % 2, k * T + k * P:(k + 1) * T],
                                             kT[rows, par, hh // HP, k * P:(k + 1) * P],
                                             qT[rows, par, hh // HP, k * P:T], start=True, stop=True)
                        for t in range(0 if linear else TT):
                            lo, hi = keys[t]
                            last = pe.matmul(S[:, i % 2, t * T + lo:t * T + hi],
                                             qT[rows, par, hh // HP, t * P:(t + 1) * P],
                                             kT[rows, par, hh // HP, lo:hi], start=True, stop=mask is None)
                            if mask is not None:
                                last = pe.matmul(S[:, i % 2, t * T + lo:t * T + hi], g.ident_bf[:],
                                                 g.masks[mask][:, t, lo:hi], start=False, stop=True)
                        last.then_inc(scored, 1)
                    j = i - 2
                    if 0 <= j < NH and not linear:
                        pe.wait_ge(expd, n - 2 + 1)
                        pe.wait_ge(prT_cp, n - 2 - 1)
                        for t in range(TT):
                            for k in range(keys[t][1] // P):
                                last = pe.transpose(PT[:, j % 2, (2 * k + t) * P:(2 * k + t + 1) * P],
                                                    pr[:, j % 3, t, k * P:(k + 1) * P], g.ident[:])
                        last.then_inc(turned, 1)
                    j = i - 3
                    if 0 <= j < NH:
                        pe.wait_ge(prT_cp, n - 3 + 1)
                        if j % G == 0:
                            pe.wait_ge(o_norm, pair * (2 * NG) + grp(j) - 1 + HEAD)
                            if NG > 1:
                                pe.wait_ge(oT_cp, pair * (2 * NG) + grp(j) - 1 + HEAD)
                        jh = j % H
                        for t in range(TT):
                            nk = keys[t][1] // P
                            for k in range(nk):
                                last = pe.matmul(O[grp(j) % 2][:, t, j % G, :],
                                                 prT[:, j % 2, (2 * k + t) * P:(2 * k + t + 1) * P],
                                                 v[:, j // H, k, jh, :],
                                                 start=(k == 0), stop=(k == nk - 1))
                        last.then_inc(pv, 1)
                    j = i - 4
                    if wo and 0 <= j < NH and j % G == G - 1:
                        gabs = pair * (2 * NG) + grp(j) + HEAD
                        pe.wait_ge(o_norm, gabs + 1)
                        pe.wait_ge(oT_cp, gabs)
                        if grp(j) % NG == 0:
                            pe.wait_ge(resid, pair * 2 + j // H + HEAD)
                        for t in range(TT):
                            last = pe.transpose(OT[grp(j) % 2][:, t, :], o[:, grp(j) % 2, t, :], g.ident[:])
                        last.then_inc(oT_ps, 1)
                    j = i - 5
                    if wo and 0 <= j < NH and j % G == G - 1:
                        gb = grp(j) % NG
                        pe.wait_ge(oT_cp, pair * (2 * NG) + grp(j) + 1 + HEAD)
                        for t in range(TT):
                            last = pe.matmul(Y[:, 1, t, :], oT[:, t, :],
                                             g.w(W + "wo")[:, gb * P:(gb + 1) * P],
                                             start=(gb == 0 and t == 0), stop=(gb == NG - 1),
                                             skip_group_check=True)
                        last.then_inc(y_ps, 1)
                    for fp, s in fronts(i):
                        front(pair * (2 * NF) + (NF if fp else 2 * NF),
                              pair * 2 + (1 if fp else 2), fp, s)

                body(pe, step)

            @block.scalar
            def _(act):
                for s in (front_cp, expd, oT_cp):
                    act.sem_inc(s, HEAD)
                if bq is not None:
                    act.activation(bqs[:], bq, ACT.Copy, scale=scale).then_inc(bias, 1)
                    act.wait_ge(bias, 1)

                def front(b0, pv_before, par, s):
                    if s == 0 and pv_before is not None:
                        act.wait_ge(pv, pv_before)
                    act.wait_ge(front_mm, b0 * NF + s + 1 + HEAD)
                    c = s % NC
                    if linear and s < 2 * NC:
                        act.wait_ge(phi, b0 * (2 * NC) + s + HEAD)
                        act.activation(ex[:], FR, ACT.Exp)
                        ins = act.activation((qT if s < NC else kT)[:, par, c, :], FR, ACT.Relu)
                    elif s < NC:
                        ins = act.activation(qT[:, par, c, :], FR, ACT.Identity,
                                             bias=bqs[:, c:c + 1] if bq is not None else 0.0, scale=scale)
                    elif s < 2 * NC:
                        ins = act.activation(kT[:, par, c, :], FR, ACT.Identity,
                                             bias=bk[:, c:c + 1] if bk is not None else 0.0)
                    else:
                        c = s - 2 * NC
                        ins = act.activation(v[:, par, :, c * G:(c + 1) * G, 0:hd],
                                             FR.rearrange("p (t h d) -> p t h d", t=TT, h=G), ACT.Copy)
                    ins.then_inc(front_cp, 1)

                for s in range(NF):
                    front(0, None, 0, s)

                def step(pair, i):
                    n = pair * NH + (i + HEAD)
                    if i < NH and not linear:
                        act.wait_ge(maxed, n + 1)
                        act.wait_ge(turned, n - 2 if i >= 3 else pair * NH + HEAD)
                        for t in range(TT):
                            lo, hi = keys[t]
                            ins = act.activation(pr[:, i % 3, t, lo:hi], S[:, i % 2, t * T + lo:t * T + hi],
                                                 ACT.Exp, bias=negmax[:, i, t:t + 1],
                                                 accum_out=sums[:, i, t:t + 1])
                        ins.then_inc(expd, 1)
                    j = i - 4
                    if wo and 0 <= j < NH and j % G == G - 1:
                        gabs = pair * (2 * NG) + grp(j) + HEAD
                        act.wait_ge(oT_ps, gabs + 1)
                        act.wait_ge(y_ps, gabs)
                        act.activation(oT[:], OT[grp(j) % 2], ACT.Copy).then_inc(oT_cp, 1)
                    for fp, s in fronts(i):
                        front(pair * 2 + (1 if fp else 2),
                              pair * NH + (0 if fp else H) + HEAD, fp, s)

                body(act, step)

            @block.vector
            def _(dve):
                for s in (maxed, prT_cp, o_norm, resid, phi):
                    dve.sem_inc(s, HEAD)
                steps = Steps(dve, steps_done)
                if linear:
                    dve.memset(v[:, :, :, :, hd:HV], 1.0)

                def front(b0, par, s):
                    if linear and s < 2 * NC:
                        dve.wait_ge(front_cp, b0 * NF + s + 1 + HEAD)
                        to = (qT if s < NC else kT)[:, par, s % NC, :]
                        dve.scalar_tensor_tensor(out=to, in0=ex[:], scalar=1.0, in1=to,
                                                 op0=ALU.min, op1=ALU.add).then_inc(phi, 1)

                for s in range(NF):
                    front(0, 0, s)

                def step(pair, i):
                    n = pair * NH + (i + HEAD)
                    if i < NH and not linear:
                        dve.wait_ge(scored, n + 1)
                        if mask is None:
                            dve.tensor_reduce(negmax[:, i, :], S[:, i % 2, :].rearrange("p (t k) -> p t k", t=TT),
                                              AX_X, ALU.max, negate=True).then_inc(maxed, 1)
                        else:
                            for t in range(TT):
                                ins = dve.tensor_reduce(negmax[:, i, t:t + 1],
                                                        S[:, i % 2, t * T:t * T + keys[t][1]],
                                                        AX_X, ALU.max, negate=True)
                            ins.then_inc(maxed, 1)
                    j = i - 2
                    if 0 <= j < NH and linear:
                        dve.wait_ge(scored, n - 2 + 1)
                        dve.wait_ge(pv, n - 2 - 1)
                        dve.tensor_tensor(prT[:, j % 2, 0:T], S[:, j % 2, 0:T], g.causal01[:], ALU.mult)
                        dve.tensor_tensor(prT[:, j % 2, 3 * P:4 * P], S[:, j % 2, 3 * P:4 * P],
                                          g.causal01[:, 0:P], ALU.mult).then_inc(prT_cp, 1)
                    elif 0 <= j < NH:
                        dve.wait_ge(turned, n - 2 + 1)
                        dve.wait_ge(pv, n - 2 - 1)
                        if mask is None:
                            dve.tensor_copy(prT[:, j % 2, :], PT[:, j % 2, :]).then_inc(prT_cp, 1)
                        else:
                            dve.tensor_copy(prT[:, j % 2, 0:2 * P], PT[:, j % 2, 0:2 * P])
                            dve.tensor_copy(prT[:, j % 2, 3 * P:4 * P],
                                            PT[:, j % 2, 3 * P:4 * P]).then_inc(prT_cp, 1)
                    j = i - 3
                    if 0 <= j < NH and j % G == G - 1:
                        gi = grp(j)
                        gabs = pair * (2 * NG) + gi + HEAD
                        rg = rinv[:, j - G + 1:j + 1, :]
                        if linear:
                            dve.wait_ge(pv, n - 3 + 1)
                            steps.done(dve.tensor_scalar(rg.rearrange("p h t -> p t h"), O[gi % 2][:, :, :, hd],
                                                         1e-6, None, ALU.add))
                            steps.done(dve.reciprocal(rg, rg))
                        else:
                            steps.done(dve.reciprocal(rg, sums[:, j - G + 1:j + 1, :]))
                            dve.wait_ge(pv, n - 3 + 1)
                        if wo:
                            dve.wait_ge(oT_ps, gabs - 1)
                        ins = dve.tensor_tensor(
                            o[:, gi % 2, :, :].rearrange("p t (h d) -> p t h d", h=G),
                            O[gi % 2][:, :, :, 0:hd],
                            rg.rearrange("p h t -> p t h").unsqueeze(3)
                                .to_broadcast([P, TT, G, hd]), ALU.mult)
                        ins.then_inc(o_norm, 1)
                        xb = g.x[:, bass.ds(pair * (2 * TT) + TT * (j // H), TT), :]
                        if not wo and gi % NG == NG - 1:
                            dve.wait_ge(o_norm, gabs + 1)
                            dve.tensor_tensor(xb, xb, o[:, gi % 2, :, :], ALU.add)
                    for fp, s in fronts(i):
                        front(pair * 2 + (1 if fp else 2), fp, s)
                    j = i - 5
                    if wo and 0 <= j < NH and j % H == H - 1:
                        dve.wait_ge(y_ps, pair * (2 * NG) + (j // H + 1) * NG + HEAD)
                        xb = g.x[:, bass.ds(pair * (2 * TT) + TT * (j // H), TT), :]
                        ins = dve.tensor_tensor(xb, xb, Y[:, 1, :, :], ALU.add)
                        if g.has(W + "bo"):
                            steps.done(ins)
                            ins = dve.tensor_tensor(
                                xb, xb, g.w(W + "bo").unsqueeze(1).to_broadcast([P, TT, P]), ALU.add)
                        ins.then_inc(resid, 1)
                    if i == NH + 5:
                        steps.restart()

                body(dve, step)


class AttentionPlan:
    H = 16
    SCORES, NORM, TURN, PV, PROJ, RESID = 7, 6, 4, 3, 2, 1
    NH = 2 * H

    def __init__(self, hd, masked):
        self.hd = hd
        self.HS = 32 if hd <= 32 else 64
        self.HP = P // self.HS
        self.NC = self.H // self.HP
        self.NV = self.H * hd // P
        self.NF = 2 * self.NC + self.NV
        self.per = -(-self.NF // 10)
        self.width = [P, T] if masked else [T, T]

    def head(self, i, offset):
        return i + offset if i + offset >= 0 else None

    def fronts(self, i):
        for rel in (1, 2, 3):
            first = self.H * (rel - 1) - self.PV + 1
            if first <= i < first + 10:
                s0 = (i - first) * self.per
                return [(rel, s) for s in range(s0, min(s0 + self.per, self.NF))]
        return []

    def copies(self, i):
        return {self.H * (rel - 1) - self.PV - 1: rel for rel in (2, 3)}.get(i)

    def steps(self, eng, step):
        for i in range(-self.SCORES, 0):
            step(0, i)
        with eng.Fori(0, B // 2) as pair:
            for i in range(self.NH):
                step(pair, i)


def attention_stage(nc, g, name, W, hd, scale, mask=None):
    a = AttentionPlan(hd, mask is not None)
    H, NH, HS, HP, NC, NF = a.H, a.NH, a.HS, a.HP, a.NC, a.NF
    with Stage(nc, name) as st:
        b = AttentionBuffers(st, a)
        s = b.sems
        with nc.Block() as block:
            @block.gpsimd
            def _(pool):
                attention_pool_setup(pool, b)
                a.steps(pool, lambda pair, i: attention_pool_step(pool, a, b, pair, i))

            @block.tensor
            def _(pe):
                for x in (s.front_mm, s.scored, s.turned, s.pv, s.y_ps):
                    pe.sem_inc(x, HEAD)
                wq, wk, wv, wo = (g.w(W + n) for n in ("wq", "wk", "wv", "wo"))
                bv = g.w(W + "bv") if g.has(W + "bv") else None

                def front(pair, rel, t):
                    if t == 0:
                        pe.wait_ge(s.h_copied, pair * 2 + rel + 1 + HEAD)
                    attention_front_pe(pe, g, a, b, pair, rel, t, wq, wk, wv, bv)

                for t in range(NF):
                    front(0, 0, t)

                def step(pair, i):
                    attention_scores_pe(pe, g, a, b, pair, i, mask)
                    attention_output_pe(pe, g, a, b, pair, i)
                    j = a.head(i, a.PROJ)
                    if j is not None and j % HP == HP - 1:
                        chunk = j // HP
                        pe.wait_ge(s.oT_cp, pair * (2 * NC) + chunk + 1 + HEAD)
                        if chunk % NC == 0:
                            pe.wait_ge(s.resid, pair * 2 + chunk // NC + HEAD)
                        for t in range(TT):
                            last = pe.matmul(b.Y[:, t, :], b.oT[:, chunk % 2, t * P:(t + 1) * P],
                                             wo[:, (chunk % NC) * P:(chunk % NC + 1) * P],
                                             start=(chunk % NC == 0 and t == 0), stop=(chunk % NC == NC - 1),
                                             skip_group_check=True)
                        last.then_inc(s.y_ps, 1)
                    for rel, t in a.fronts(i):
                        front(pair, rel, t)

                a.steps(pe, step)

            @block.scalar
            def _(act):
                for x in (s.front_cp, s.expd, s.oT_cp):
                    act.sem_inc(x, HEAD)
                bq, bk = (g.w(W + n) if g.has(W + n) else None for n in ("bq", "bk"))
                if bq is not None:
                    act.activation(b.bqs[:], bq, ACT.Copy, scale=scale).then_inc(s.bias, 1)
                    act.wait_ge(s.bias, 1)
                    bq = b.bqs
                for t in range(NF):
                    attention_front_act(act, a, b, 0, 0, t, bq, bk, scale)

                def step(pair, i):
                    attention_exp_act(act, a, b, pair, i)
                    for rel, t in a.fronts(i):
                        attention_front_act(act, a, b, pair, rel, t, bq, bk, scale)

                a.steps(act, step)

            @block.vector
            def _(dve):
                for x in (s.maxed, s.recip, s.prT_cp, s.resid, s.h_copied):
                    dve.sem_inc(x, HEAD)

                for n in range(2):
                    attention_copy_h(dve, g, a, b, 0, n, n)

                def step(pair, i):
                    attention_dve_step(dve, a, b, pair, i)
                    if (rel := a.copies(i)) is not None:
                        attention_copy_h(dve, g, a, b, pair, rel, pair * 2 + rel)
                    j = a.head(i, a.RESID)
                    if j is not None and j % H == H - 1:
                        rel = j // H
                        dve.wait_ge(s.y_ps, pair * (2 * NC) + (rel + 1) * NC + HEAD)
                        xb = g.x[:, bass.ds(pair * (2 * TT) + TT * rel, TT), :]
                        ins = dve.tensor_tensor(xb, xb, b.Y[:], ALU.add)
                        if g.has(W + "bo"):
                            ins.then_inc(s.bias_add, 1)
                            dve.wait_ge(s.bias_add, pair * 2 + rel + 1)
                            ins = dve.tensor_tensor(
                                xb, xb, g.w(W + "bo").unsqueeze(1).to_broadcast([P, TT, P]), ALU.add)
                        ins.then_inc(s.resid, 1)

                a.steps(dve, step)


class AttentionSems:

    def __init__(self, st):
        self.h_copied = st.sem("h_copied")
        self.front_mm = st.sem("front_mm")
        self.front_cp = st.sem("front_cp")
        self.scored = st.sem("scored")
        self.maxed = st.sem("maxed")
        self.expd = st.sem("expd")
        self.recip = st.sem("recip")
        self.normed = st.sem("normed")
        self.turned = st.sem("turned")
        self.prT_cp = st.sem("prT_cp")
        self.pv = st.sem("pv")
        self.oT_cp = st.sem("oT_cp")
        self.y_ps = st.sem("y_ps")
        self.resid = st.sem("resid")
        self.bias = st.sem("bias")
        self.bias_add = st.sem("bias_add")
        self.zeroed = st.sem("zeroed")


class AttentionBuffers:
    def __init__(self, st, a):
        self.hTs = st.sb("hTs", [P, 2, T])
        self.qT = st.sb("qT", [P, 2, a.NC, T])
        self.kT = st.sb("kT", [P, 2, a.NC, T])
        self.v = st.sb("v", [P, 2, TT, a.H, a.HS])
        self.bqs = st.sb("bqs", [P, a.NC])
        self.negmax = st.sb("negmax", [P, a.NH, TT])
        self.sums = st.sb("sums", [P, a.NH, TT])
        self.rinv = st.sb("rinv", [P, a.NH, TT])
        self.pr = st.sb("pr", [P, 4, TT, T])
        self.prT = st.sb("prT", [P, 2 * a.HP, 512])
        self.oT = st.sb("oT", [P, 2, T])
        self.S = st.ps("S", [P, 2, 512])
        self.PT = st.ps("PT", [P, 2, 512])
        self.FR = st.ps("FR", [P, 2, 512])
        self.O = st.ps("O", [P, 512])[:, 0:T]
        self.Y = st.ps("Y", [P, 4, P])[:, 0:TT, :]
        self.sems = AttentionSems(st)


def attention_pool_setup(pool, b):
    pool.memset(b.v[:], 0.0).then_inc(b.sems.zeroed, 1)
    pool.memset(b.pr[:], 0.0).then_inc(b.sems.zeroed, 1)
    pool.sem_inc(b.sems.normed, HEAD)


def attention_pool_step(pool, a, b, pair, i):
    s = b.sems
    j = a.head(i, a.NORM)
    if j is None:
        return
    pool.wait_ge(s.recip, pair * a.NH + j + 1 + HEAD)
    p = b.pr[:, j % 4, :, :]
    pool.tensor_tensor(p, p, b.rinv[:, j % a.NH, :].unsqueeze(2).to_broadcast([P, TT, T]), ALU.mult)\
        .then_inc(s.normed, 1)


def attention_front_pe(pe, g, a, b, pair, rel, t, wq, wk, wv, bv, banks=2):
    s = b.sems
    f = a.NF * rel + t
    pe.wait_ge(s.front_cp, pair * (2 * a.NF) + f + 1 - banks + HEAD)
    out = b.FR[:, f % banks, 0:T]
    src = b.hTs[:, rel % 2, :]
    if t < 2 * a.NC:
        w = (wq if t < a.NC else wk)[:, (t % a.NC) * P:(t % a.NC + 1) * P]
        last = pe.matmul(out, w, src, start=True, stop=True)
    else:
        c = slice((t - 2 * a.NC) * P, (t - 2 * a.NC + 1) * P)
        for k in range(TT):
            tile = slice(k * P, (k + 1) * P)
            last = pe.matmul(out[:, tile], src[:, tile], wv[:, c], start=True, stop=bv is None)
            if bv is not None:
                last = pe.matmul(out[:, tile], g.ones[0:1, :], bv[0:1, c], start=False, stop=True)
    last.then_inc(s.front_mm, 1)


def attention_front_act(act, a, b, pair, rel, t, bq, bk, scale, banks=2):
    s = b.sems
    f = a.NF * rel + t
    if t == 0 and rel == 0:
        act.wait_ge(s.zeroed, 2)
    if t == 0 and rel >= 2:
        act.wait_ge(s.pv, pair * (2 * a.NC) + (rel - 1) * a.NC + HEAD)
    act.wait_ge(s.front_mm, pair * (2 * a.NF) + f + 1 + HEAD)
    src = b.FR[:, f % banks, 0:T]
    c = t % a.NC
    if t < a.NC:
        ins = act.activation(b.qT[:, rel % 2, c, :], src, ACT.Identity,
                             bias=bq[:, c:c + 1] if bq is not None else 0.0, scale=scale)
    elif t < 2 * a.NC:
        ins = act.activation(b.kT[:, rel % 2, c, :], src, ACT.Identity,
                             bias=bk[:, c:c + 1] if bk is not None else 0.0)
    else:
        n = P // a.hd
        c = t - 2 * a.NC
        ins = act.activation(b.v[:, rel % 2, :, c * n:(c + 1) * n, 0:a.hd],
                             src.rearrange("p (t h d) -> p t h d", t=TT, h=n), ACT.Copy)
    ins.then_inc(s.front_cp, 1)


def attention_scores_pe(pe, g, a, b, pair, i, mask):
    s = b.sems
    j = a.head(i, a.SCORES)
    if j is None:
        return
    rel, hh = j // a.H, j % a.H
    if hh == 0:
        pe.wait_ge(s.front_cp, pair * (2 * a.NF) + (rel + 1) * a.NF + HEAD)
    pe.wait_ge(s.expd, pair * a.NH + j - 1 + HEAD)
    rows = slice(a.HS * (hh % a.HP), a.HS * (hh % a.HP) + a.hd)
    for t in range(TT):
        n = a.width[t]
        out = b.S[:, j % 2, t * T:t * T + n]
        last = pe.matmul(out, b.qT[rows, rel % 2, hh // a.HP, t * P:(t + 1) * P],
                         b.kT[rows, rel % 2, hh // a.HP, 0:n], start=True, stop=mask is None)
        if mask is not None:
            last = pe.matmul(out, g.ident_bf[:], g.masks[mask][:, t, 0:n], start=False, stop=True)
    last.then_inc(s.scored, 1)


def attention_output_pe(pe, g, a, b, pair, i):
    s = b.sems
    j = a.head(i, a.TURN)
    if j is not None:
        n = pair * a.NH + j + HEAD
        pe.wait_ge(s.normed, n + 1)
        pe.wait_ge(s.prT_cp, n - 1)
        for t in range(TT):
            for k in range(a.width[t] // P):
                last = pe.transpose(b.PT[:, j % 2, (2 * k + t) * P:(2 * k + t + 1) * P],
                                    b.pr[:, j % 4, t, k * P:(k + 1) * P], g.ident[:])
        last.then_inc(s.turned, 1)
    j = a.head(i, a.PV)
    if j is not None and j % a.HP == a.HP - 1:
        chunk = j // a.HP
        pe.wait_ge(s.prT_cp, pair * a.NH + j + 1 + HEAD)
        pe.wait_ge(s.oT_cp, pair * (2 * a.NC) + chunk + HEAD)
        for k in range(TT):
            lo = k * P if a.width[0] == P else 0
            for h in range(a.HP):
                jh = j - a.HP + 1 + h
                last = pe.matmul(b.O[a.HS * h:a.HS * (h + 1), lo:T],
                                 b.v[:, (jh // a.H) % 2, k, jh % a.H, :],
                                 b.prT[:, jh % (2 * a.HP), k * T + lo:(k + 1) * T],
                                 start=(k == 0), stop=(k == TT - 1), skip_group_check=True)
        last.then_inc(s.pv, 1)


def attention_exp_act(act, a, b, pair, i):
    s = b.sems
    j = a.head(i, a.SCORES)
    act.wait_ge(s.maxed, pair * a.NH + j + 1 + HEAD)
    act.wait_ge(s.turned, pair * a.NH + j - 3 + HEAD)
    for t in range(TT):
        n = a.width[t]
        ins = act.activation(b.pr[:, j % 4, t, 0:n], b.S[:, j % 2, t * T:t * T + n], ACT.Exp,
                             bias=b.negmax[:, j % a.NH, t:t + 1], accum_out=b.sums[:, j % a.NH, t:t + 1])
    ins.then_inc(s.expd, 1)
    j = a.head(i, a.PV)
    if j is not None and j % a.HP == a.HP - 1:
        chunk = j // a.HP
        act.wait_ge(s.pv, pair * (2 * a.NC) + chunk + 1 + HEAD)
        act.wait_ge(s.y_ps, pair * (2 * a.NC) + chunk - 1 + HEAD)
        act.activation(b.oT[:, chunk % 2, :], b.O, ACT.Copy).then_inc(s.oT_cp, 1)


def attention_copy_h(dve, g, a, b, pair, rel, batch):
    s = b.sems
    if rel >= 2:
        dve.wait_ge(s.front_mm, pair * (2 * a.NF) + (rel - 1) * a.NF + HEAD)
    src = g.hT[:, batch * T:(batch + 1) * T] if isinstance(batch, int) else g.hT[:, bass.ds(batch * T, T)]
    dve.tensor_scalar(b.hTs[:, rel % 2, :], src, 1.0, None, ALU.mult).then_inc(s.h_copied, 1)


def attention_dve_step(dve, a, b, pair, i):
    s = b.sems
    j = a.head(i, a.SCORES)
    dve.wait_ge(s.scored, pair * a.NH + j + 1 + HEAD)
    m = b.negmax[:, j % a.NH, :]
    if a.width[0] == T:
        ins = dve.tensor_reduce(m, b.S[:, j % 2, :].rearrange("p (t k) -> p t k", t=TT), AX_X, ALU.max,
                                negate=True)
    else:
        for t in range(TT):
            ins = dve.tensor_reduce(m[:, t:t + 1], b.S[:, j % 2, t * T:t * T + a.width[t]], AX_X, ALU.max,
                                    negate=True)
    ins.then_inc(s.maxed, 1)
    j = a.head(i, a.NORM)
    if j is not None:
        dve.wait_ge(s.expd, pair * a.NH + j + 1 + HEAD)
        dve.reciprocal(b.rinv[:, j % a.NH, :], b.sums[:, j % a.NH, :]).then_inc(s.recip, 1)
    j = a.head(i, a.TURN)
    if j is not None:
        dve.wait_ge(s.turned, pair * a.NH + j + 1 + HEAD)
        dve.wait_ge(s.pv, pair * (2 * a.NC) + j // a.HP - 1 + HEAD)
        to, of = b.prT[:, j % (2 * a.HP), :], b.PT[:, j % 2, :]
        if a.width[0] == T:
            dve.tensor_copy(to, of).then_inc(s.prT_cp, 1)
        else:
            dve.tensor_copy(to[:, 0:2 * P], of[:, 0:2 * P])
            dve.tensor_copy(to[:, 3 * P:4 * P], of[:, 3 * P:4 * P]).then_inc(s.prT_cp, 1)


class EncoderPlan(AttentionPlan):
    K = 9
    SCORES, NORM, TURN, PV, PROJ = (7 + K, 6 + K, 4 + K, 3 + K, 2 + K)
    LN1, POW1, NORM1, AFFINE1, X1T, FF1, FF2, LN2, POW2, NORM2 = (K + 1, K, K - 1, K - 2, K - 3, K - 4,
                                                                  K - 6, K - 7, K - 8, K - 9)
    E, DFF = 4, 512

    def ends(self, i, offset):
        j = self.head(i, offset)
        return j // self.H if j is not None and j % self.H == self.H - 1 else None

    def steps(self, eng, step):
        for i in range(-self.SCORES, 0):
            step(0, i)
        with eng.Fori(0, B) as pair:
            for i in range(self.NH):
                step(pair, i)


ENC_A = ["wq", "wk", "wv", "bq", "bk", "bv"]
ENC_B = ["wo", "w1", "w2", "b1", "ob", "b2", "n1w", "n1b", "n2w", "n2b"]


def expert_gates(nc, g, name, gates, experts):
    E = EncoderPlan.E
    with Stage(nc, name) as st:
        hsum = st.sb("hsum", [P, B])
        z = st.sb("z", [B, 4, E])
        onehot = st.sb("onehot", [B, 2, E])
        cand = st.sb("cand", [B, E])
        small = st.sb("small", [B, 8])
        picked = st.sb("picked", [B, 2])
        gk = st.sb("gk", [B, 2])
        spread = st.sb("spread", [B, B, 2])
        expert_i = st.sb("expert_i", [B, 2], mybir.dt.int32)
        psg = st.ps("psg", [P, 512])
        psb = st.ps("psb", [P, 512])
        steps_done, summed, logits, expd, spread_done, gates_ps, numbers, moved, zeroed = [
            st.sem(n) for n in ("steps", "summed", "logits", "expd", "spread", "gates_ps", "numbers", "moved",
                                "zeroed")]
        lg, ex, gate, masked = (z[:, n, :] for n in range(4))
        iota = g.w("enc_iota")

        with nc.Block() as block:
            @block.vector
            def _(dve):
                d = Steps(dve, steps_done)
                dve.tensor_reduce(hsum[:], g.hT[:, 0:NTOK].rearrange("p (b t) -> p b t", b=B), AX_X, ALU.add)\
                    .then_inc(summed, 1)
                dve.wait_ge(logits, 1)
                d.done(dve.tensor_scalar(lg, psg[0:B, 0:E], 1.0 / T, None, ALU.mult))
                d.done(dve.tensor_tensor(lg, lg, g.w("enc_gate_b"), ALU.add))
                d.done(dve.tensor_reduce(small[:, 0:1], lg, AX_X, ALU.max))
                dve.tensor_scalar(small[:, 1:2], small[:, 0:1], -1.0, None, ALU.mult).then_inc(summed, 1)
                dve.wait_ge(expd, 1)
                d.done(dve.reciprocal(small[:, 3:4], small[:, 2:3]))
                d.done(dve.tensor_scalar(gate, ex, small[:, 3:4], None, ALU.mult))
                d.done(dve.tensor_copy(masked, lg))
                for k in range(2):
                    d.done(dve.tensor_reduce(small[:, 4:5], masked, AX_X, ALU.max))
                    d.done(dve.tensor_scalar(cand[:], masked, small[:, 4:5], float(E), ALU.is_lt, ALU.mult))
                    d.done(dve.tensor_tensor(cand[:], cand[:], iota, ALU.add))
                    d.done(dve.tensor_reduce(picked[:, k:k + 1], cand[:], AX_X, ALU.min))
                    d.done(dve.tensor_scalar(onehot[:, k, :], iota, picked[:, k:k + 1], None, ALU.is_equal))
                    if k == 0:
                        d.done(dve.scalar_tensor_tensor(out=masked, in0=onehot[:, 0, :], scalar=NEG, in1=masked,
                                                        op0=ALU.mult, op1=ALU.add))
                d.done(dve.tensor_tensor(onehot[:], onehot[:], gate.unsqueeze(1).to_broadcast([B, 2, E]),
                                         ALU.mult))
                d.done(dve.tensor_reduce(gk[:], onehot[:], AX_X, ALU.add))
                dve.tensor_tensor(spread[:], g.ident[0:B, 0:B].unsqueeze(2).to_broadcast([B, B, 2]),
                                  gk[:].unsqueeze(1).to_broadcast([B, B, 2]), ALU.mult).then_inc(spread_done, 1)
                dve.tensor_copy(expert_i[:], picked[:]).then_inc(numbers, 1)
                dve.wait_ge(gates_ps, 1)
                dve.tensor_copy(gates[:, 0:2 * B], psb[:, 0:2 * B])

            @block.tensor
            def _(pe):
                pe.wait_ge(summed, 1)
                pe.matmul(psg[0:B, 0:E], hsum[:], g.w("enc_gate_w"), start=True, stop=True).then_inc(logits, 1)
                pe.wait_ge(spread_done, 1)
                pe.matmul(psb[:, 0:2 * B], g.ones[0:B, :], spread[:].rearrange("p b k -> p (b k)"),
                          start=True, stop=True).then_inc(gates_ps, 1)

            @block.scalar
            def _(act):
                act.wait_ge(summed, 2)
                act.activation(ex, lg, ACT.Exp, bias=small[:, 1:2], accum_out=small[:, 2:3]).then_inc(expd, 1)

            @block.gpsimd
            def _(pool):
                pool.memset(experts[:], 0).then_inc(zeroed, 1)

            @block.sync
            def _(sp):
                sp.wait_ge(numbers, 1)
                sp.wait_ge(zeroed, 1)
                sp.dma_start(experts[0:1, 0:2 * B], expert_i[:]).then_inc(moved, 16)
                sp.wait_ge(moved, 16)


def encoder_stage(nc, g, name):
    a = EncoderPlan(8, False)
    H, NH, HP, NC, NF = a.H, a.NH, a.HP, a.NC, a.NF
    scale = a.hd ** -0.5
    with Stage(nc, name) as st:
        gates = st.sb("gates", [P, 2 * B])
        experts = st.sb("experts", [1, 2 * B + 4], mybir.dt.int32)
        expert_gates(nc, g, name + "g", gates, experts)
        b = AttentionBuffers(st, a)
        s = b.sems
        b.gates, b.experts = gates, experts
        atA, nA, atB, nB = g.enc_layout
        wA = st.sb("wA", [P, 2, nA])
        wB = st.sb("wB", [P, 2, nB])
        r = st.sb("r", [P, 2, TT, D])
        stats = st.sb("stats", [P, 2, TT, 6])
        mv = st.sb("mv", [P, 2, TT, 2])
        veps = st.sb("veps", [P, 2, TT])
        rstd = st.sb("rstd", [P, 2, TT])
        x1 = st.sb("x1", [P, TT, D])
        x1b = st.sb("x1b", [P, TT, D])
        x1T = st.sb("x1T", [P, T])
        hid = st.sb("hid", [P, 4, T])
        TL = b.FR[:, 1, 0:T]
        (tl_mm, tl_cp, var_ready, rstd_ready, x1_norm, x1_ready, dve_steps, pool_steps, a_in, b_in, unit_done) = [
            st.sem(n) for n in ("tl_mm", "tl_cp", "var", "rstd", "x1_norm", "x1_ready", "dve_steps",
                                "pool_steps", "a_in0", "b_in0", "unit_done")]
        a_in, b_in = [a_in, st.sem("a_in1")], [b_in, st.sem("b_in1")]
        NT_ = 6

        def part(par, key):
            at, w = (atA, wA) if key in atA else (atB, wB)
            c, n, rows = at[key]
            return w[0:rows, par, c:c + n]

        with nc.Block() as block:
            @block.sync
            def _(sp):
                def expert(pair, rel):
                    return sp.value_load(b.experts[0:1, bass.ds(pair * 2 + rel, 1)], min_val=0, max_val=a.E - 1)

                def load(e, rel, group):
                    if group == "a":
                        sp.dma_start(wA[:, rel % 2, :], g.a["enc_a"][bass.ds(e, 1), :, :]
                                     .rearrange("e p n -> p (e n)")).then_inc(a_in[rel % 2], 16)
                    else:
                        sp.dma_start(wB[:, rel % 2, :], g.a["enc_b"][bass.ds(e, 1), :, :]
                                     .rearrange("e p n -> p (e n)")).then_inc(b_in[rel % 2], 16)

                for rel in range(2):
                    e = expert(0, rel)
                    load(e, rel, "a")
                    load(e, rel, "b")
                with sp.Fori(0, B) as pair:
                    for rel in (2, 3):
                        e = expert(pair, rel)
                        sp.wait_ge(s.front_cp, pair * (2 * NF) + (rel - 1) * NF + HEAD)
                        load(e, rel, "a")
                        sp.wait_ge(unit_done, pair * 2 + rel - 1)
                        load(e, rel, "b")
                for x in a_in + b_in:
                    sp.wait_ge(x, 16 * (B + 1))

            @block.gpsimd
            def _(pool):
                attention_pool_setup(pool, b)
                pool.sem_inc(rstd_ready, HEAD)
                ps = Steps(pool, pool_steps)

                def power(pair, rel, n):
                    pool.wait_ge(var_ready, pair * 4 + rel * 2 + n + 1)
                    ps.done(pool.tensor_tensor(veps[:, n, :], mv[:, n, :, 1], g.eps[:, 0:TT], ALU.add))
                    pool.tensor_tensor(rstd[:, n, :], veps[:, n, :], g.neg_half[:, 0:TT], ALU.pow)\
                        .then_inc(rstd_ready, 1)

                def step(pair, i):
                    attention_pool_step(pool, a, b, pair, i)
                    if (rel := a.ends(i, a.POW1)) is not None:
                        power(pair, rel, 0)
                    if (rel := a.ends(i, a.AFFINE1)) is not None:
                        pool.wait_ge(x1_norm, pair * 2 + rel + 1)
                        for key, op in (("n1w", ALU.mult), ("n1b", ALU.add)):
                            ps.mark(pool.tensor_tensor(x1[:], x1[:], part(rel % 2, key).unsqueeze(1)
                                                       .to_broadcast([P, TT, D]), op))
                            ps.wait()
                        pool.tensor_tensor(x1b[:], x1[:], part(rel % 2, "b2").unsqueeze(1)
                                           .to_broadcast([P, TT, D]), ALU.add).then_inc(x1_ready, 1)
                    if (rel := a.ends(i, a.POW2)) is not None:
                        power(pair, rel, 1)
                    if i == NH - 1:
                        ps.restart()

                a.steps(pool, step)

            @block.tensor
            def _(pe):
                for x in (s.front_mm, s.scored, s.turned, s.pv, s.y_ps, tl_mm):
                    pe.sem_inc(x, HEAD)

                def front(pair, rel, t):
                    if t == 0:
                        pe.wait_ge(s.h_copied, pair * 2 + rel + 1 + HEAD)
                        pe.wait_ge(a_in[rel % 2], pair * 16 + 16 * (rel // 2 + 1))
                    par = rel % 2
                    attention_front_pe(pe, g, a, b, pair, rel, t, part(par, "wq"), part(par, "wk"),
                                       part(par, "wv"), part(par, "bv"), banks=1)

                def tail(pair, rel, t):
                    n = pair * (2 * NT_) + rel * NT_ + t + HEAD
                    pe.wait_ge(tl_cp, n)
                    par = rel % 2
                    if t == 0:
                        pe.wait_ge(x1_ready, pair * 2 + rel + 1)
                        for k in range(TT):
                            last = pe.transpose(TL[:, k * P:(k + 1) * P], x1[:, k, :], g.ident[:])
                    elif t < 5:
                        last = pe.matmul(TL, part(par, "w1")[:, (t - 1) * P:t * P], x1T[:], start=True, stop=True)
                    else:
                        for k in range(TT):
                            for c in range(4):
                                last = pe.matmul(TL[:, k * P:(k + 1) * P], hid[:, c, k * P:(k + 1) * P],
                                                 part(par, "w2")[:, c * P:(c + 1) * P],
                                                 start=(c == 0), stop=(c == 3))
                    last.then_inc(tl_mm, 1)

                for t in range(NF):
                    front(0, 0, t)

                def step(pair, i):
                    attention_scores_pe(pe, g, a, b, pair, i, None)
                    attention_output_pe(pe, g, a, b, pair, i)
                    j = a.head(i, a.PROJ)
                    if j is not None and j % HP == HP - 1:
                        chunk = j // HP
                        pe.wait_ge(s.oT_cp, pair * (2 * NC) + chunk + 1 + HEAD)
                        if chunk % NC == 0:
                            pe.wait_ge(s.resid, pair * 2 + chunk // NC + HEAD)
                            rel = chunk // NC
                            pe.wait_ge(b_in[rel % 2], pair * 16 + 16 * (rel // 2 + 1))
                        for t in range(TT):
                            last = pe.matmul(b.Y[:, t, :], b.oT[:, chunk % 2, t * P:(t + 1) * P],
                                             part((chunk // NC) % 2, "wo")[:, (chunk % NC) * P:(chunk % NC + 1) * P],
                                             start=(chunk % NC == 0 and t == 0), stop=(chunk % NC == NC - 1),
                                             skip_group_check=True)
                        last.then_inc(s.y_ps, 1)
                    for rel, t in a.fronts(i):
                        front(pair, rel, t)
                    for off, ts in ((a.X1T, [0]), (a.FF1, [1, 2]), (a.FF1 - 1, [3, 4]), (a.FF2, [5])):
                        if (rel := a.ends(i, off)) is not None:
                            for t in ts:
                                tail(pair, rel, t)

                a.steps(pe, step)

            @block.scalar
            def _(act):
                for x in (s.front_cp, s.expd, s.oT_cp, tl_cp):
                    act.sem_inc(x, HEAD)

                def front(pair, rel, t):
                    if t == 0:
                        act.wait_ge(a_in[rel % 2], pair * 16 + 16 * (rel // 2 + 1))
                        act.activation(b.bqs[:], part(rel % 2, "bq"), ACT.Copy, scale=scale).then_inc(s.bias, 1)
                        act.wait_ge(s.bias, pair * 2 + rel + 1)
                    attention_front_act(act, a, b, pair, rel, t, b.bqs, part(rel % 2, "bk"), scale, banks=1)

                def tail(pair, rel, t):
                    n = pair * (2 * NT_) + rel * NT_ + t + HEAD
                    act.wait_ge(tl_mm, n + 1)
                    if t == 0:
                        act.activation(x1T[:], TL, ACT.Copy).then_inc(tl_cp, 1)
                    else:
                        act.activation(hid[:, t - 1, :], TL, ACT.Relu,
                                       bias=part(rel % 2, "b1")[:, t - 1:t]).then_inc(tl_cp, 1)

                for t in range(NF):
                    front(0, 0, t)

                def step(pair, i):
                    attention_exp_act(act, a, b, pair, i)
                    for rel, t in a.fronts(i):
                        front(pair, rel, t)
                    for off, ts in ((a.X1T, [0]), (a.FF1, [1, 2]), (a.FF1 - 1, [3, 4])):
                        if (rel := a.ends(i, off)) is not None:
                            for t in ts:
                                tail(pair, rel, t)

                a.steps(act, step)

            @block.vector
            def _(dve):
                for x in (s.maxed, s.recip, s.prT_cp, s.resid, s.h_copied):
                    dve.sem_inc(x, HEAD)
                d = Steps(dve, dve_steps)
                attention_copy_h(dve, g, a, b, 0, 0, 0)
                attention_copy_h(dve, g, a, b, 0, 1, 0)

                def moments(n):
                    for t in range(TT):
                        d.mark(dve.bn_stats(stats[:, n, t, :], r[:, n, t, :]))
                    for t in range(TT):
                        d.wait()
                        ins = dve.bn_aggr(mv[:, n, t, :], stats[:, n, t, :])
                    ins.then_inc(var_ready, 1)

                def step(pair, i):
                    attention_dve_step(dve, a, b, pair, i)
                    if (rel := a.copies(i)) is not None:
                        attention_copy_h(dve, g, a, b, pair, rel, pair + rel // 2)
                    if (rel := a.ends(i, a.LN1)) is not None:
                        dve.wait_ge(s.y_ps, pair * (2 * NC) + (rel + 1) * NC + HEAD)
                        dve.tensor_tensor(r[:, 0, :, :], b.Y, g.h[:, bass.ds(pair * TT, TT), :], ALU.add)\
                           .then_inc(s.resid, 1)
                        dve.wait_ge(s.resid, pair * 2 + rel + 1 + HEAD)
                        d.done(dve.tensor_tensor(r[:, 0, :, :], r[:, 0, :, :], part(rel % 2, "ob").unsqueeze(1)
                                                 .to_broadcast([P, TT, D]), ALU.add))
                        moments(0)
                    if (rel := a.ends(i, a.NORM1)) is not None:
                        dve.wait_ge(rstd_ready, pair * 4 + rel * 2 + 1 + HEAD)
                        for t in range(TT):
                            ins = dve.tensor_scalar(x1[:, t, :], r[:, 0, t, :], mv[:, 0, t, 0:1],
                                                    rstd[:, 0, t:t + 1], ALU.subtract, ALU.mult)
                        ins.then_inc(x1_norm, 1)
                    if (rel := a.ends(i, a.LN2)) is not None:
                        dve.wait_ge(tl_mm, pair * (2 * NT_) + (rel + 1) * NT_ + HEAD)
                        ins = dve.tensor_tensor(r[:, 1, :, :], TL.rearrange("p (t n) -> p t n", t=TT), x1b[:],
                                                ALU.add)
                        d.done(ins)
                        dve.sem_inc(tl_cp, 1)
                        moments(1)
                    if (rel := a.ends(i, a.NORM2)) is not None:
                        dve.wait_ge(rstd_ready, pair * 4 + rel * 2 + 2 + HEAD)
                        for t in range(TT):
                            d.mark(dve.tensor_scalar(r[:, 1, t, :], r[:, 1, t, :], mv[:, 1, t, 0:1],
                                                     rstd[:, 1, t:t + 1], ALU.subtract, ALU.mult))
                        d.wait()
                        gate = b.gates[:, bass.ds(pair * 2 + rel, 1)]
                        xb = g.x[:, bass.ds(pair * TT, TT), :]
                        both = lambda key: part(rel % 2, key).unsqueeze(1).to_broadcast([P, TT, D])
                        d.done(dve.tensor_tensor(r[:, 1, :, :], r[:, 1, :, :], both("n2w"), ALU.mult))
                        d.done(dve.tensor_tensor(r[:, 1, :, :], r[:, 1, :, :], both("n2b"), ALU.add))
                        d.done(dve.scalar_tensor_tensor(out=xb, in0=r[:, 1, :, :], scalar=gate, in1=xb,
                                                        op0=ALU.mult, op1=ALU.add))
                        dve.sem_inc(unit_done, 1)
                    if i == NH - 1:
                        d.restart()

                a.steps(dve, step)


def channel_mix_stage(nc, g, name):
    C = 512
    with Stage(nc, name) as st:
        d = st.sb("d", [P, 2, C])
        mum1 = st.sb("mum1", [P, 2])
        xk = st.sb("xk", [P, 4, C])
        xr = st.sb("xr", [P, 4, C])
        ka = st.sb("ka", [P, 4, C])
        sg = st.sb("sg", [P, 2, C])
        prod = st.sb("prod", [P, 2, C])
        KP, RP, VP = (st.ps(n, [P, 2, C]) for n in ("KP", "RP", "VP"))
        (mu_ready, diff, mixed_k, mixed_r, k_mm, relu, squared, r_mm, v_mm, sig, multiplied, added) = [
            st.sem(n) for n in ("mu_ready", "diff", "mixed_k", "mixed_r", "k_mm", "relu", "squared", "r_mm",
                                "v_mm", "sig", "multiplied", "added")]

        with nc.Block() as block:
            @block.vector
            def _(dve):
                dve.tensor_scalar(mum1[:], g.w("L1f_mu"), 1.0, None, ALU.subtract).then_inc(mu_ready, 1)
                dve.wait_ge(mu_ready, 1)
                for c in range(4):
                    h = g.hT[:, c * C:(c + 1) * C].rearrange("p (b t) -> p b t", b=2)
                    dd = d[:, c % 2, :].rearrange("p (b t) -> p b t", b=2)
                    dve.tensor_copy(dd[:, :, 0:1], h[:, :, 0:1]).then_inc(diff, 1)
                    dve.tensor_tensor(dd[:, :, 1:], h[:, :, 1:], h[:, :, 0:T - 1], ALU.subtract).then_inc(diff, 1)
                    dve.wait_ge(diff, 2 * c + 2)
                    for n, to, sem in ((1, xk, mixed_k), (0, xr, mixed_r)):
                        dve.scalar_tensor_tensor(out=to[:, c, :], in0=d[:, c % 2, :], scalar=mum1[:, n:n + 1],
                                                 in1=g.hT[:, c * C:(c + 1) * C], op0=ALU.mult, op1=ALU.add)\
                           .then_inc(sem, 1)
                for c in range(4):
                    dve.wait_ge(sig, c + 1)
                    dve.wait_ge(v_mm, c + 1)
                    if c >= 2:
                        dve.wait_ge(added, c - 1)
                    dve.tensor_tensor(prod[:, c % 2, :], VP[:, c % 2, :], sg[:, c % 2, :], ALU.mult)\
                       .then_inc(multiplied, 1)
                    dve.wait_ge(multiplied, c + 1)
                    xc = g.x[:, 4 * c:4 * c + 4, :]
                    dve.tensor_tensor(xc, xc, prod[:, c % 2, :].rearrange("p (t n) -> p t n", t=4), ALU.add)\
                       .then_inc(added, 1)

            @block.tensor
            def _(pe):
                def rows(c, to, src, w, sem):
                    for t in range(4):
                        last = pe.matmul(to[:, c % 2, t * P:(t + 1) * P], src[:, c, t * P:(t + 1) * P], g.w(w),
                                         start=True, stop=True)
                    last.then_inc(sem, 1)

                for c in range(5):
                    if c < 4:
                        pe.wait_ge(mixed_k, c + 1)
                        if c >= 2:
                            pe.wait_ge(relu, c - 1)
                        pe.matmul(KP[:, c % 2, :], g.w("L1f_wk"), xk[:, c, :], start=True, stop=True)\
                          .then_inc(k_mm, 1)
                        pe.wait_ge(mixed_r, c + 1)
                        if c >= 2:
                            pe.wait_ge(sig, c - 1)
                        rows(c, RP, xr, "L1f_wr", r_mm)
                    if c >= 1:
                        pe.wait_ge(squared, c)
                        if c >= 3:
                            pe.wait_ge(multiplied, c - 2)
                        rows(c - 1, VP, ka, "L1f_wv", v_mm)

            @block.scalar
            def _(act):
                for c in range(4):
                    act.wait_ge(k_mm, c + 1)
                    act.activation(ka[:, c, :], KP[:, c % 2, :], ACT.Relu).then_inc(relu, 1)
                    act.wait_ge(r_mm, c + 1)
                    if c >= 2:
                        act.wait_ge(multiplied, c - 1)
                    act.activation(sg[:, c % 2, :], RP[:, c % 2, :], ACT.Sigmoid).then_inc(sig, 1)

            @block.gpsimd
            def _(pool):
                for c in range(4):
                    pool.wait_ge(relu, c + 1)
                    pool.tensor_tensor(ka[:, c, :], ka[:, c, :], ka[:, c, :], ALU.mult).then_inc(squared, 1)


def kernel_attention_stage(nc, g, name):
    C = 512
    H, HD = 16, 8
    inv = HD ** -0.5
    with Stage(nc, name) as st:
        qk = st.sb("qk", [P, 2, NTOK])
        sq = st.sb("sq", [P, 2, NTOK])
        v = st.sb("v", [P, NT, D])
        qf = st.sb("qf", [P, NTOK])
        kf = st.sb("kf", [P, NT, D])
        kv = st.sb("kv", [P, B, D + H])
        bqk = st.sb("bqk", [P, 2])
        den = st.sb("den", [P, NT, H])
        rden = st.sb("rden", [P, NT, H])
        o = st.sb("o", [P, NT, D])
        oT = st.sb("oT", [P, 2, C])
        A = st.ps("A", [P, 2, C])
        Fp = st.ps("Fp", [P, 2, C])
        KV = st.ps("KV", [P, C])
        O = st.ps("O", [P, 2, C])
        Y = st.ps("Y", [P, C])
        (b_ready, a_mm, a_cp, a_sq, f_mm, f_exp, kv_mm, kv_masked, o_mm, den_ready, o_norm, t_mm, t_cp,
         y_mm, y_add, steps_done) = [st.sem(n) for n in (
             "b_ready", "a_mm", "a_cp", "a_sq", "f_mm", "f_exp", "kv_mm", "kv_masked", "o_mm", "den_ready",
             "o_norm", "t_mm", "t_cp", "y_mm", "y_add", "steps")]
        wqk, wv, wo, rblk, nhalf = (g.w("L2a_" + n) for n in ("wqk", "wv", "wo", "rblk", "nhalf"))

        with nc.Block() as block:
            @block.tensor
            def _(pe):
                def project(n):
                    if n >= 2:
                        pe.wait_ge(a_cp, n - 1)
                    c = n % 4
                    if n < 8:
                        last = pe.matmul(A[:, n % 2, :], wqk[:, (n // 4) * P:(n // 4 + 1) * P],
                                         g.hT[:, c * C:(c + 1) * C], start=True, stop=True)
                    else:
                        for t in range(4):
                            tile = slice((4 * c + t) * P, (4 * c + t + 1) * P)
                            pe.matmul(A[:, n % 2, t * P:(t + 1) * P], g.hT[:, tile], wv, start=True, stop=False)
                            last = pe.matmul(A[:, n % 2, t * P:(t + 1) * P], g.ones[0:1, :], g.w("L2a_bv"),
                                             start=False, stop=True)
                    last.then_inc(a_mm, 1)

                def features(n):
                    pe.wait_ge(a_sq, n + 1)
                    if n >= 2:
                        pe.wait_ge(f_exp, n - 1)
                    c = n % 4
                    if n < 4:
                        cols = slice(c * C, (c + 1) * C)
                        pe.matmul(Fp[:, n % 2, :], rblk, qk[:, 0, cols], start=True, stop=False)
                        last = pe.matmul(Fp[:, n % 2, :], nhalf, sq[:, 0, cols], start=False, stop=True)
                    else:
                        for t in range(4):
                            cols = slice((4 * c + t) * P, (4 * c + t + 1) * P)
                            pe.matmul(Fp[:, n % 2, t * P:(t + 1) * P], qk[:, 1, cols], rblk, start=True, stop=False)
                            last = pe.matmul(Fp[:, n % 2, t * P:(t + 1) * P], sq[:, 1, cols], nhalf,
                                             start=False, stop=True)
                    last.then_inc(f_mm, 1)

                for n in range(12):
                    project(n)
                    if n >= 2 and n - 2 < 8:
                        features(n - 2)
                pe.wait_ge(a_cp, 12)
                for c in range(4):
                    pe.wait_ge(f_exp, 4 + c + 1)
                    if c > 0:
                        pe.wait_ge(kv_masked, c)
                    for b in (2 * c, 2 * c + 1):
                        for t in range(TT):
                            last = pe.matmul(KV[:, (b % 2) * P:(b % 2 + 1) * P], kf[:, TT * b + t, :],
                                             v[:, TT * b + t, :], start=(t == 0), stop=(t == TT - 1))
                    last.then_inc(kv_mm, 1)
                for c in range(8 + 2):
                    if c < 8:
                        if c % 2 == 0:
                            pe.wait_ge(kv_masked, c // 2 + 1)
                        if c >= 2:
                            pe.wait_ge(o_norm, c - 1)
                        for t in range(TT):
                            tile = slice((TT * c + t) * P, (TT * c + t + 1) * P)
                            last = pe.matmul(O[:, c % 2, t * (D + H):(t + 1) * (D + H)], qf[:, tile], kv[:, c, :],
                                             start=True, stop=True)
                        last.then_inc(o_mm, 1)
                    j = c - 1
                    if 0 <= j < 8:
                        pe.wait_ge(o_norm, j + 1)
                        if j >= 2:
                            pe.wait_ge(t_cp, j - 1)
                        for t in range(TT):
                            last = pe.transpose(A[:, j % 2, t * P:(t + 1) * P], o[:, TT * j + t, :], g.ident[:])
                        last.then_inc(t_mm, 1)
                    j = c - 2
                    if 0 <= j < 8:
                        pe.wait_ge(t_cp, j + 1)
                        if j >= 1:
                            pe.wait_ge(y_add, j)
                        for t in range(TT):
                            last = pe.matmul(Y[:, t * P:(t + 1) * P], oT[:, j % 2, t * P:(t + 1) * P], wo,
                                             start=True, stop=True)
                        last.then_inc(y_mm, 1)

            @block.scalar
            def _(act):
                act.activation(bqk[:], g.w("L2a_bqk"), ACT.Copy, scale=inv).then_inc(b_ready, 1)
                act.wait_ge(b_ready, 1)

                def exps(n):
                    act.wait_ge(f_mm, n + 1)
                    c = n % 4
                    out = qf[:, c * C:(c + 1) * C] if n < 4 else kf[:, 4 * c:4 * c + 4, :]
                    src = Fp[:, n % 2, :] if n < 4 else Fp[:, n % 2, :].rearrange("p (t n) -> p t n", t=4)
                    act.activation(out, src, ACT.Exp).then_inc(f_exp, 1)

                for n in range(12):
                    act.wait_ge(a_mm, n + 1)
                    c = n % 4
                    if n < 8:
                        act.activation(qk[:, n // 4, c * C:(c + 1) * C], A[:, n % 2, :], ACT.Identity,
                                       bias=bqk[:, n // 4:n // 4 + 1], scale=inv).then_inc(a_cp, 1)
                    else:
                        act.activation(v[:, 4 * c:4 * c + 4, :], A[:, n % 2, :].rearrange("p (t n) -> p t n", t=4),
                                       ACT.Copy).then_inc(a_cp, 1)
                    if n >= 2 and n - 2 < 8:
                        exps(n - 2)
                for j in range(8):
                    act.wait_ge(t_mm, j + 1)
                    if j >= 2:
                        act.wait_ge(y_mm, j - 1)
                    act.activation(oT[:, j % 2, 0:T], A[:, j % 2, 0:T], ACT.Copy).then_inc(t_cp, 1)

            @block.vector
            def _(dve):
                d = Steps(dve, steps_done)
                d.done(dve.tensor_copy(kv[:, :, D:], g.w("L2a_headof").unsqueeze(1).to_broadcast([P, B, H])))
                for n in range(8):
                    dve.wait_ge(a_cp, n + 1)
                    cols = slice((n % 4) * C, (n % 4 + 1) * C)
                    dve.tensor_tensor(sq[:, n // 4, cols], qk[:, n // 4, cols], qk[:, n // 4, cols], ALU.mult)\
                       .then_inc(a_sq, 1)
                for c in range(4):
                    dve.wait_ge(kv_mm, c + 1)
                    dve.tensor_tensor(kv[:, 2 * c:2 * c + 2, 0:D],
                                      KV[:, 0:T].rearrange("p (b n) -> p b n", b=2),
                                      g.w("L2a_blocks").unsqueeze(1).to_broadcast([P, 2, D]), ALU.mult)\
                       .then_inc(kv_masked, 1)

                def outputs(j):
                    dve.wait_ge(o_mm, j + 1)
                    po = O[:, j % 2, 0:TT * (D + H)].rearrange("p (t n) -> p t n", t=TT)
                    tiles = slice(TT * j, TT * j + TT)
                    d.done(dve.tensor_scalar(den[:, tiles, :], po[:, :, D:], 1e-8, None, ALU.add))
                    d.done(dve.reciprocal(rden[:, tiles, :], den[:, tiles, :]))
                    dve.tensor_tensor(o[:, tiles, :].rearrange("p t (h e) -> p t h e", h=H),
                                      po[:, :, 0:D].rearrange("p t (h e) -> p t h e", h=H),
                                      rden[:, tiles, :].unsqueeze(3).to_broadcast([P, TT, H, HD]), ALU.mult)\
                       .then_inc(o_norm, 1)

                for j in range(8 + 2):
                    if j < 8:
                        outputs(j)
                    n = j - 2
                    if n >= 0:
                        dve.wait_ge(y_mm, n + 1)
                        xb = g.x[:, TT * n:TT * n + TT, :]
                        dve.tensor_tensor(xb, xb, Y[:, 0:T].rearrange("p (t n) -> p t n", t=TT), ALU.add)\
                           .then_inc(y_add, 1)
                        dve.wait_ge(y_add, n + 1)
                        dve.tensor_tensor(xb, xb, g.w("L2a_bo").unsqueeze(1).to_broadcast([P, TT, D]), ALU.add)


MOE_E, MOE_CAP, MOE_H = 8, 160, 512


def moe_stage(nc, g, name):
    E, CAP, C = MOE_E, MOE_CAP, 512
    NS = E * CAP
    NCH = E + E * (CAP - P) // P
    KH = MOE_H // P
    w1, w2, b1, b2 = (g.big("moe_" + n) for n in ("w1", "w2", "b1", "b2"))
    ow1, ow2, ob1, ob2 = (g.big("moe_" + n) for n in ("ow1", "ow2", "ob1", "ob2"))
    with Stage(nc, name) as st:
        lg = st.sb("lg", [P, NT, E])
        mx = st.sb("mx", [P, NT])
        cand = st.sb("cand", [P, NT, E])
        eid = st.sb("eid", [P, NT])
        onehot = st.sb("onehot", [P, NT, E])
        tot = st.sb("tot", [P, E, NT])
        run = st.sb("run", [P, E, NT])
        rank = st.sb("rank", [P, NT])
        inv = st.sb("inv", [P, NT])
        tmp = st.sb("tmp", [P, 2, NT])
        slot = st.sb("slot", [P, NT])
        row = st.sb("row", [P, NT])
        pick = st.sb("pick", [P, 2, NS])
        bufT = st.sb("bufT", [P, NS])
        rows = st.sb("rows", [P, NTOK])
        hid = st.sb("hid", [P, 2, KH, C])
        y = st.sb("y", [P, NCH, D])
        dg = st.sb("dg", [P, 2, P])
        place = st.sb("place", [P, 2, NCH, P])
        sem = st.sem
        steps_done, logits, onehot_ready, counted, cum_ready, slots_ready = (
            sem("steps"), sem("logits"), sem("onehot"), sem("counted"), sem("cum"), sem("slots"))

        with Stage(nc, name + "r") as sr:
            L = sr.ps("L", [P, C])
            CU = sr.ps("CU", [P, C])
            TO = sr.ps("TO", [P, C])
            with nc.Block() as block:
                @block.tensor
                def _(pe):
                    for t in range(NT):
                        last = pe.matmul(L[:, t * E:(t + 1) * E], g.hT[:, t * P:(t + 1) * P], g.w("moe_rw"),
                                         start=True, stop=True)
                    last.then_inc(logits, 1)
                    pe.wait_ge(onehot_ready, 1)
                    oh = onehot[:].rearrange("p t e -> p (t e)")
                    pe.matmul(CU[:, 0:NT * E], g.causal01[:, 0:P], oh, start=True, stop=True)
                    pe.matmul(TO[:, 0:NT * E], g.ones[:], oh, start=True, stop=True).then_inc(counted, 1)

                @block.vector
                def _(dve):
                    d = Steps(dve, steps_done)
                    iota = g.w("moe_iota").unsqueeze(1).to_broadcast([P, NT, E])
                    dve.wait_ge(logits, 1)
                    d.done(dve.tensor_tensor(lg[:], L[:, 0:NT * E].rearrange("p (t e) -> p t e", t=NT),
                                             g.w("moe_rb").unsqueeze(1).to_broadcast([P, NT, E]), ALU.add))
                    d.done(dve.tensor_reduce(mx[:], lg[:], AX_X, ALU.max))
                    d.done(dve.tensor_tensor(cand[:], lg[:], mx[:].unsqueeze(2).to_broadcast([P, NT, E]),
                                             ALU.is_lt))
                    d.done(dve.scalar_tensor_tensor(out=cand[:], in0=cand[:], scalar=float(E), in1=iota,
                                                    op0=ALU.mult, op1=ALU.add))
                    d.done(dve.tensor_reduce(eid[:], cand[:], AX_X, ALU.min))
                    dve.tensor_tensor(onehot[:], iota, eid[:].unsqueeze(2).to_broadcast([P, NT, E]),
                                      ALU.is_equal).then_inc(onehot_ready, 1)
                    dve.wait_ge(counted, 1)
                    d.done(dve.tensor_copy(tot[:], TO[:, 0:NT * E].rearrange("p (t e) -> p e t", t=NT)))
                    d.done(dve.tensor_tensor_scan(out=run[:].rearrange("p e t -> p (e t)"), data0=g.w("moe_keep"),
                                                  data1=tot[:].rearrange("p e t -> p (e t)"), initial=0.0,
                                                  op0=ALU.mult, op1=ALU.add))
                    d.done(dve.tensor_tensor(run[:], run[:], tot[:], ALU.subtract))
                    d.done(dve.tensor_tensor(cand[:], CU[:, 0:NT * E].rearrange("p (t e) -> p t e", t=NT),
                                             run[:].rearrange("p e t -> p t e"), ALU.add))
                    d.done(dve.tensor_tensor(cand[:], cand[:], onehot[:], ALU.mult))
                    d.done(dve.tensor_reduce(rank[:], cand[:], AX_X, ALU.add))
                    d.done(dve.tensor_scalar(inv[:], rank[:], float(CAP), None, ALU.is_gt))
                    d.done(dve.tensor_scalar(tmp[:, 0, :], inv[:], 10000.0, -1.0, ALU.mult, ALU.add))
                    d.done(dve.tensor_tensor(tmp[:, 0, :], tmp[:, 0, :], rank[:], ALU.add))
                    d.done(dve.scalar_tensor_tensor(out=slot[:], in0=eid[:], scalar=float(CAP), in1=tmp[:, 0, :],
                                                    op0=ALU.mult, op1=ALU.add))
                    d.done(dve.scalar_tensor_tensor(out=row[:], in0=eid[:], scalar=float(P), in1=tmp[:, 0, :],
                                                    op0=ALU.mult, op1=ALU.add))
                    d.done(dve.tensor_scalar(tmp[:, 1, :], eid[:], float(CAP - P - P), float(E * P - P),
                                             ALU.mult, ALU.add))
                    d.done(dve.tensor_scalar(tmp[:, 0, :], rank[:], float(P), None, ALU.is_gt))
                    d.done(dve.tensor_tensor(tmp[:, 1, :], tmp[:, 1, :], tmp[:, 0, :], ALU.mult))
                    dve.tensor_tensor(row[:], row[:], tmp[:, 1, :], ALU.add)

        with Stage(nc, name + "e") as se:
            BU = se.ps("BU", [P, 3, C])
            HP_ = se.ps("HP", [P, 2, C])
            YP = se.ps("YP", [P, 2, C])
            RP = se.ps("RP", [P, C])
            picked, gathered, buf_ready, h_mm, h_act, y_mm, y_cp, dg_ready, r_mm, r_cp = [
                se.sem(n) for n in ("picked", "gathered", "buf_ready", "h_mm", "h_act", "y_mm", "y_cp", "dg_ready",
                                    "r_mm", "r_cp")]
            cuts = [(0, 512), (512, 1024), (1024, NS)]
            with nc.Block() as block:
                @block.vector
                def _(dve):
                    for t in range(NT):
                        if t >= 2:
                            dve.wait_ge(gathered, t - 1)
                        dve.tensor_scalar(pick[:, t % 2, :], g.iota_free[:, 0:NS], slot[:, t:t + 1], None,
                                          ALU.is_equal).then_inc(picked, 1)
                    dve.wait_ge(gathered, NT)
                    for n, (lo, hi) in enumerate(cuts):
                        dve.tensor_copy(bufT[:, lo:hi], BU[:, n, 0:hi - lo]).then_inc(buf_ready, 1)
                    for t in range(NT):
                        if t >= 2:
                            dve.wait_ge(r_mm, t - 1)
                        dve.tensor_scalar(dg[:, t % 2, :], g.ident[:], row[:, t:t + 1], None, ALU.mult)\
                           .then_inc(dg_ready, 1)
                        if t % 4 == 3:
                            dve.wait_ge(r_mm, t + 1)
                            dve.tensor_copy(rows[:, (t - 3) * P:(t + 1) * P], RP[:, :]).then_inc(r_cp, 1)

                @block.tensor
                def _(pe):
                    for t in range(NT):
                        pe.wait_ge(picked, t + 1)
                        for n, (lo, hi) in enumerate(cuts):
                            last = pe.matmul(BU[:, n, 0:hi - lo], g.h[:, t, :], pick[:, t % 2, lo:hi],
                                             start=(t == 0), stop=(t == NT - 1))
                        last.then_inc(gathered, 1)

                    def spread(t):
                        pe.wait_ge(dg_ready, t + 1)
                        if t % 4 == 0 and t:
                            pe.wait_ge(r_cp, t // 4)
                        pe.matmul(RP[:, (t % 4) * P:(t % 4 + 1) * P], g.ones[:], dg[:, t % 2, :],
                                  start=True, stop=True).then_inc(r_mm, 1)

                    def hidden(e):
                        for c in range(KH):
                            n = KH * e + c
                            if n >= 2:
                                pe.wait_ge(h_act, n - 1)
                            pe.matmul(HP_[:, n % 2, 0:CAP], w1[:, n * P:(n + 1) * P], bufT[:, e * CAP:(e + 1) * CAP],
                                      start=True, stop=True).then_inc(h_mm, 1)

                    def second(e):
                        pe.wait_ge(h_act, KH * (e + 1))
                        if e >= 2:
                            pe.wait_ge(y_cp, e - 1)
                        q = (e % 4) * (CAP - P)
                        for c in range(KH):
                            pe.matmul(YP[:, e % 2, 0:D], hid[:, e % 2, c, 0:P],
                                      w2[:, (KH * e + c) * D:(KH * e + c + 1) * D], start=(c == 0), stop=False)
                        pe.matmul(YP[:, e % 2, 0:D], g.ones[0:1, :], b2[0:1, e * D:(e + 1) * D], start=False, stop=True)
                        for c in range(KH):
                            pe.matmul(YP[q:q + CAP - P, e % 2, D:2 * D], hid[:, e % 2, c, P:CAP],
                                      w2[:, (KH * e + c) * D:(KH * e + c + 1) * D], start=(c == 0), stop=False,
                                      tile_position=(0, q))
                        last = pe.matmul(YP[q:q + CAP - P, e % 2, D:2 * D], g.ones[0:1, 0:CAP - P],
                                         b2[0:1, e * D:(e + 1) * D], start=False, stop=True, tile_position=(0, q))
                        last.then_inc(y_mm, 1)

                    pe.wait_ge(buf_ready, 3)
                    for e in range(E + 1):
                        if e < E:
                            hidden(e)
                            spread(2 * e)
                            spread(2 * e + 1)
                        if e >= 1:
                            second(e - 1)

                @block.scalar
                def _(act):
                    def copies(e):
                        act.wait_ge(y_mm, e + 1)
                        q = (e % 4) * (CAP - P)
                        act.activation(y[:, e, :], YP[:, e % 2, 0:D], ACT.Copy)
                        act.activation(y[q:q + CAP - P, E + e // 4, :], YP[q:q + CAP - P, e % 2, D:2 * D],
                                       ACT.Copy).then_inc(y_cp, 1)

                    for e in range(E):
                        if e >= 2:
                            act.wait_ge(y_mm, e - 1)
                        for c in range(KH):
                            n = KH * e + c
                            act.wait_ge(h_mm, n + 1)
                            act.activation(hid[:, e % 2, c, 0:CAP], HP_[:, n % 2, 0:CAP], ACT.Relu,
                                           bias=b1[:, n:n + 1]).then_inc(h_act, 1)
                        if e >= 1:
                            copies(e - 1)
                    copies(E - 1)

        with Stage(nc, name + "o") as so:
            HO = so.ps("HO", [P, 2, C])
            YO = so.ps("YO", [P, 2, C])
            YE = so.ps("YE", [P, 2, C])
            placed, h_mm, h_act, o_mm, e_mm, added, own = [
                so.sem(n) for n in ("placed", "h_mm", "h_act", "o_mm", "e_mm", "added", "own")]
            with nc.Block() as block:
                @block.tensor
                def _(pe):
                    def hidden(c):
                        for k in range(KH):
                            n = KH * c + k
                            if n >= 2:
                                pe.wait_ge(h_act, n - 1)
                            pe.matmul(HO[:, n % 2, :], ow1[:, k * P:(k + 1) * P], g.hT[:, c * C:(c + 1) * C],
                                      start=True, stop=True).then_inc(h_mm, 1)

                    def outputs(t):
                        if t >= 2:
                            pe.wait_ge(added, 2 * (t - 1))
                        c = t // 4
                        cols = slice((t % 4) * P, (t % 4 + 1) * P)
                        pe.wait_ge(h_act, KH * (c + 1))
                        for k in range(KH):
                            pe.matmul(YO[:, t % 2, 0:D], hid[:, c % 2, k, cols], ow2[:, k * D:(k + 1) * D],
                                      start=(k == 0), stop=False)
                        pe.matmul(YO[:, t % 2, 0:D], g.ones[0:1, :], ob2[0:1, :], start=False, stop=True)\
                          .then_inc(o_mm, 1)
                        pe.wait_ge(placed, t + 1)
                        for k in range(NCH):
                            last = pe.matmul(YE[:, t % 2, 0:D], place[:, t % 2, k, :], y[:, k, :],
                                             start=(k == 0), stop=(k == NCH - 1))
                        last.then_inc(e_mm, 1)

                    hidden(0)
                    for c in range(4):
                        if c < 3:
                            hidden(c + 1)
                        for t in range(4 * c, 4 * c + 4):
                            outputs(t)

                @block.scalar
                def _(act):
                    for c in range(4):
                        if c >= 2:
                            act.wait_ge(o_mm, 4 * (c - 1))
                        for k in range(KH):
                            n = KH * c + k
                            act.wait_ge(h_mm, n + 1)
                            act.activation(hid[:, c % 2, k, :], HO[:, n % 2, :], ACT.Relu, bias=ob1[:, k:k + 1])\
                               .then_inc(h_act, 1)

                @block.vector
                def _(dve):
                    def one_hot(t):
                        if t >= 2:
                            dve.wait_ge(e_mm, t - 1)
                        dve.tensor_tensor(place[:, t % 2, :, :],
                                          rows[:, t * P:(t + 1) * P].unsqueeze(1).to_broadcast([P, NCH, P]),
                                          g.w("moe_rowid").unsqueeze(2).to_broadcast([P, NCH, P]),
                                          ALU.is_equal).then_inc(placed, 1)

                    one_hot(0)
                    for t in range(NT):
                        if t + 1 < NT:
                            one_hot(t + 1)
                        xt = g.x[:, t, :]
                        dve.wait_ge(o_mm, t + 1)
                        dve.scalar_tensor_tensor(out=xt, in0=YO[:, t % 2, 0:D], scalar=inv[:, t:t + 1], in1=xt,
                                                 op0=ALU.mult, op1=ALU.add).then_inc(added, 1)
                        dve.wait_ge(added, 2 * t + 1)
                        dve.wait_ge(e_mm, t + 1)
                        dve.tensor_tensor(xt, xt, YE[:, t % 2, 0:D], ALU.add).then_inc(added, 1)


def alibi_attention_stage(nc, g, name):
    scale = D ** -0.5
    with Stage(nc, name) as st:
        qT = st.sb("qT", [P, NTOK])
        v = st.sb("v", [P, NT, D])
        dist = st.sb("dist", [P, TT, T])
        sc = st.sb("sc", [P, 2, TT, T])
        pr = st.sb("pr", [P, 2, TT, T])
        prT = st.sb("prT", [P, 2, 512])
        negmax = st.sb("negmax", [P, B, TT])
        sums = st.sb("sums", [P, B, TT])
        rinv = st.sb("rinv", [P, B, TT])
        FR = st.ps("FR", [P, 2, 512])
        S = st.ps("S", [P, 2, 512])
        PT = st.ps("PT", [P, 2, 512])
        O = st.ps("O", [P, 2, 4, P])
        (iota_done, bias_ready, front_mm, front_cp, scored, biased, maxed, expd, turned, prT_cp, pv, added,
         recip) = [
            st.sem(n) for n in ("iota", "bias_ready", "front_mm", "front_cp", "scored", "biased", "maxed",
                                "expd", "turned", "prT_cp", "pv", "added", "recip")]

        with nc.Block() as block:
            @block.gpsimd
            def _(pool):
                pool.iota(dist[:], pattern=[[-P, TT], [1, T]], base=0, channel_multiplier=-1,
                          allow_small_or_imprecise_dtypes=True).then_inc(iota_done, 1)
                pool.wait_ge(iota_done, 1)
                pool.tensor_scalar(dist[:], dist[:], g.w("L1a_slope"), None, ALU.mult).then_inc(iota_done, 1)
                pool.wait_ge(iota_done, 2)
                pool.affine_select(out=dist[:], in_=dist[:], compare_op=ALU.is_ge, fill=NEG, base=0,
                                   pattern=[[P, TT], [-1, T]], channel_multiplier=1).then_inc(bias_ready, 1)

            @block.tensor
            def _(pe):
                for c in range(4):
                    if c >= 2:
                        pe.wait_ge(front_cp, c - 1)
                    pe.matmul(FR[:, c % 2, :], g.w("L1a_wqk"), g.hT[:, c * 512:(c + 1) * 512],
                              start=True, stop=True).then_inc(front_mm, 1)
                for c in range(4, 8):
                    pe.wait_ge(front_cp, c - 1)
                    for t in range(4):
                        tile = 4 * (c - 4) + t
                        last = pe.matmul(FR[:, c % 2, t * P:(t + 1) * P], g.hT[:, tile * P:(tile + 1) * P],
                                         g.w("L1a_wv"), start=True, stop=True)
                    last.then_inc(front_mm, 1)
                for i in range(B + 3):
                    if i < B:
                        if i == 0:
                            pe.wait_ge(front_cp, 4)
                        if i >= 2:
                            pe.wait_ge(biased, i - 1)
                        for t in range(TT):
                            tile = TT * i + t
                            last = pe.matmul(S[:, i % 2, t * T:(t + 1) * T], qT[:, tile * P:(tile + 1) * P],
                                             g.hT[:, i * T:(i + 1) * T], start=True, stop=True)
                        last.then_inc(scored, 1)
                    j = i - 2
                    if 0 <= j < B:
                        pe.wait_ge(expd, j + 1)
                        if j >= 2:
                            pe.wait_ge(prT_cp, j - 1)
                        for t in range(TT):
                            for k in range(TT):
                                last = pe.transpose(PT[:, j % 2, (2 * k + t) * P:(2 * k + t + 1) * P],
                                                    pr[:, j % 2, t, k * P:(k + 1) * P], g.ident[:])
                        last.then_inc(turned, 1)
                    j = i - 3
                    if 0 <= j < B:
                        pe.wait_ge(prT_cp, j + 1)
                        if j == 0:
                            pe.wait_ge(front_cp, 8)
                        if j >= 2:
                            pe.wait_ge(added, 2 * (j - 1))
                        for t in range(TT):
                            for k in range(TT):
                                last = pe.matmul(O[:, j % 2, t, :],
                                                 prT[:, j % 2, (2 * k + t) * P:(2 * k + t + 1) * P],
                                                 v[:, TT * j + k, :], start=(k == 0), stop=(k == TT - 1))
                        last.then_inc(pv, 1)

            @block.scalar
            def _(act):
                for c in range(4):
                    act.wait_ge(front_mm, c + 1)
                    act.activation(qT[:, c * 512:(c + 1) * 512], FR[:, c % 2, :], ACT.Copy,
                                   scale=scale).then_inc(front_cp, 1)
                for c in range(4, 8):
                    act.wait_ge(front_mm, c + 1)
                    act.activation(v[:, 4 * (c - 4):4 * (c - 3), :],
                                   FR[:, c % 2, :].rearrange("p (t n) -> p t n", t=4), ACT.Copy)\
                       .then_inc(front_cp, 1)
                for i in range(B):
                    act.wait_ge(maxed, i + 1)
                    if i >= 2:
                        act.wait_ge(turned, i - 1)
                    for t in range(TT):
                        ins = act.activation(pr[:, i % 2, t, :], sc[:, i % 2, t, :], ACT.Exp,
                                             bias=negmax[:, i, t:t + 1], accum_out=sums[:, i, t:t + 1])
                    ins.then_inc(expd, 1)

            @block.vector
            def _(dve):
                dve.wait_ge(bias_ready, 1)
                for i in range(B + 3):
                    if i < B:
                        dve.wait_ge(scored, i + 1)
                        if i >= 2:
                            dve.wait_ge(expd, i - 1)
                        dve.tensor_tensor(sc[:, i % 2, :, :], S[:, i % 2, :].rearrange("p (t k) -> p t k", t=TT),
                                          dist[:], ALU.add).then_inc(biased, 1)
                        dve.wait_ge(biased, i + 1)
                        dve.tensor_reduce(negmax[:, i, :], sc[:, i % 2, :, :], AX_X, ALU.max,
                                          negate=True).then_inc(maxed, 1)
                    j = i - 2
                    if 0 <= j < B:
                        dve.wait_ge(turned, j + 1)
                        if j >= 2:
                            dve.wait_ge(pv, j - 1)
                        dve.tensor_copy(prT[:, j % 2, :], PT[:, j % 2, :]).then_inc(prT_cp, 1)
                    j = i - 3
                    if 0 <= j < B:
                        dve.wait_ge(expd, j + 1)
                        dve.reciprocal(rinv[:, j, :], sums[:, j, :]).then_inc(recip, 1)
                        dve.wait_ge(recip, j + 1)
                        dve.wait_ge(pv, j + 1)
                        for t in range(TT):
                            xt = g.x[:, TT * j + t, :]
                            dve.scalar_tensor_tensor(out=xt, in0=O[:, j % 2, t, :], scalar=rinv[:, j, t:t + 1],
                                                     in1=xt, op0=ALU.mult, op1=ALU.add).then_inc(added, 1)


def mamba_stage(nc, g, name):
    C = 512
    NC_ = NTOK // C
    M = 2
    N = STATE
    ROWS = 80
    ax, az = g.w("m_in_w"), g.w("m_in_b")
    with Stage(nc, name) as st:
        u = st.sb("u", [P, M, NTOK])
        gate = st.sb("gate", [P, M, NTOK])
        delta = st.sb("delta", [P, M, NTOK])
        du = st.sb("du", [P, M, NTOK])
        aneg = st.sb("aneg", [P, M * N])
        xd = g.h[:].rearrange("p t d -> p (t d)")

        with Stage(nc, name + "f") as sf:
            xpad = sf.sb("xpad", [P, M, B, T + 4])
            e = sf.sb("e", [P, M, NTOK])
            XZ = sf.ps("XZ", [P, 4, C])
            XD = sf.ps("XD", [P, 2, C])
            DP = sf.ps("DP", [P, 2, C])
            (pads, xz_mm, xz_cp, conv, u_ready, xd_mm, xd_cp, dp_mm, v_ready, abs_ready, exp_ready, one_ready,
             ln_ready, steps, a_exp) = [
                sf.sem(n) for n in ("pads", "xz_mm", "xz_cp", "conv", "u_ready", "xd_mm", "xd_cp", "dp_mm",
                                    "v_ready", "abs_ready", "exp_ready", "one_ready", "ln_ready", "steps", "a_exp")]
            w4 = [xpad[:, m, :, :].rearrange("p b t -> p (b t)")[:, 0:NTOK] for m in range(M)]
            with nc.Block() as block:
                @block.gpsimd
                def _(pool):
                    pool.memset(xpad[:, :, :, 0:4], 0.0).then_inc(pads, 1)

                @block.tensor
                def _(pe):
                    def deltas(c):
                        pe.wait_ge(xd_cp, c + 1)
                        for m in range(M):
                            n = M * c + m
                            if n >= 2:
                                pe.wait_ge(v_ready, n - 1)
                            pe.matmul(DP[:, n % 2, :], g.w("m_dt_w")[:, m * P:(m + 1) * P], xd[0:DT_RANK, c * C:(c + 1) * C],
                                      start=True, stop=True).then_inc(dp_mm, 1)

                    for c in range(NC_):
                        for m in range(4):
                            n = 4 * c + m
                            if n >= 4:
                                pe.wait_ge(xz_cp, n - 3)
                            pe.matmul(XZ[:, n % 4, :], ax[:, m * P:(m + 1) * P], g.hT[:, c * C:(c + 1) * C],
                                      start=True, stop=True).then_inc(xz_mm, 1)
                    for c in range(NC_):
                        pe.wait_ge(u_ready, M * (c + 1))
                        if c >= 2:
                            pe.wait_ge(xd_cp, c - 1)
                        for m in range(M):
                            last = pe.matmul(XD[0:ROWS, c % 2, :], g.w("m_x_w")[:, m * ROWS:(m + 1) * ROWS],
                                             u[:, m, c * C:(c + 1) * C], start=(m == 0), stop=(m == M - 1))
                        last.then_inc(xd_mm, 1)
                        deltas(c)

                @block.scalar
                def _(act):
                    act.activation(aneg[:], g.w("m_a_log"), ACT.Exp).then_inc(a_exp, 1)
                    for c in range(NC_):
                        for m in range(4):
                            n = 4 * c + m
                            act.wait_ge(xz_mm, n + 1)
                            if m < M:
                                act.activation(xpad[:, m, 2 * c:2 * c + 2, 4:],
                                               XZ[:, n % 4, :].rearrange("p (b t) -> p b t", b=2), ACT.Identity,
                                               bias=az[:, m:m + 1]).then_inc(xz_cp, 1)
                            else:
                                act.activation(gate[:, m - M, c * C:(c + 1) * C], XZ[:, n % 4, :], ACT.Silu,
                                               bias=az[:, m:m + 1]).then_inc(xz_cp, 1)
                    for c in range(NC_):
                        for m in range(M):
                            act.wait_ge(conv, 4 * (M * c + m) + 4)
                            cols = u[:, m, c * C:(c + 1) * C]
                            act.activation(cols, cols, ACT.Silu).then_inc(u_ready, 1)
                        act.wait_ge(xd_mm, c + 1)
                        act.activation(xd[0:ROWS, c * C:(c + 1) * C], XD[0:ROWS, c % 2, :], ACT.Copy).then_inc(xd_cp, 1)
                        for m in range(M):
                            n = M * c + m
                            act.wait_ge(dp_mm, n + 1)
                            act.activation(delta[:, m, c * C:(c + 1) * C], DP[:, n % 2, :], ACT.Identity,
                                           bias=g.w("m_dt_b")[:, m:m + 1]).then_inc(v_ready, 1)
                    for m in range(M):
                        act.wait_ge(abs_ready, m + 1)
                        act.activation(e[:, m, :], e[:, m, :], ACT.Exp, scale=-1.0).then_inc(exp_ready, 1)
                    for m in range(M):
                        act.wait_ge(one_ready, m + 1)
                        act.activation(du[:, m, :], w4[m], ACT.Ln).then_inc(ln_ready, 1)

                @block.vector
                def _(dve):
                    d = Steps(dve, steps)
                    dve.wait_ge(a_exp, 1)
                    dve.tensor_scalar(aneg[:], aneg[:], -1.0, None, ALU.mult)
                    dve.wait_ge(pads, 1)
                    n = 0
                    for c in range(NC_):
                        for m in range(M):
                            dve.wait_ge(xz_cp, 4 * c + m + 1)
                            out = u[:, m, c * C:(c + 1) * C].rearrange("p (b t) -> p b t", b=2)
                            for k in range(4):
                                src = xpad[:, m, 2 * c:2 * c + 2, 1 + k:1 + k + T]
                                wk = g.w("m_conv_w")[:, 4 * m + k:4 * m + k + 1]
                                if k == 0:
                                    ins = dve.tensor_scalar(out, src, wk, g.w("m_conv_b")[:, m:m + 1],
                                                            ALU.mult, ALU.add)
                                else:
                                    dve.wait_ge(conv, n)
                                    ins = dve.scalar_tensor_tensor(out=out, in0=src, scalar=wk, in1=out,
                                                                   op0=ALU.mult, op1=ALU.add)
                                ins.then_inc(conv, 1)
                                n += 1
                    dve.wait_ge(v_ready, M * NC_)
                    for m in range(M):
                        v = delta[:, m, :]
                        dve.scalar_tensor_tensor(out=e[:, m, :], in0=v, scalar=-1.0, in1=v, op0=ALU.mult,
                                                 op1=ALU.max).then_inc(abs_ready, 1)
                    dve.wait_ge(abs_ready, M)
                    for m in range(M):
                        dve.wait_ge(exp_ready, m + 1)
                        dve.tensor_scalar(w4[m], e[:, m, :], 1.0, None, ALU.add).then_inc(one_ready, 1)
                        d.mark(dve.tensor_scalar(delta[:, m, :], delta[:, m, :], 0.0, None, ALU.max))
                    for m in range(M):
                        dve.wait_ge(one_ready, m + 1)
                        d.mark(dve.scalar_tensor_tensor(out=e[:, m, :], in0=w4[m], scalar=-1.0, in1=e[:, m, :],
                                                        op0=ALU.add, op1=ALU.subtract))
                    d.wait()
                    for m in range(M):
                        dve.wait_ge(ln_ready, m + 1)
                        d.mark(dve.reciprocal(w4[m], w4[m]))
                        d.mark(dve.tensor_tensor(delta[:, m, :], delta[:, m, :], du[:, m, :], ALU.add))
                    d.wait()
                    for m in range(M):
                        d.mark(dve.tensor_tensor(e[:, m, :], e[:, m, :], w4[m], ALU.mult))
                    d.wait()
                    for m in range(M):
                        d.mark(dve.tensor_tensor(delta[:, m, :], delta[:, m, :], e[:, m, :], ALU.subtract))
                    d.wait()
                    dve.wait_ge(u_ready, M * NC_)
                    for m in range(M):
                        dve.tensor_tensor(du[:, m, :], delta[:, m, :], u[:, m, :], ALU.mult)

        with Stage(nc, name + "s") as ss:
            dA = ss.sb("dA", [P, 2, M, C])
            dBu = ss.sb("dBu", [P, 2, M, C])
            hs = ss.sb("hs", [P, 2, M, C])
            bc = ss.sb("bc", [P, 2, 2, C])
            hc = g.hT[:, 0:2 * M * C].rearrange("p (i m c) -> p i m c", i=2, m=M)
            yv = ss.sb("yv", [P, M, C])
            BC = ss.ps("BC", [P, 2, 2, C])
            Y = ss.ps("Y", [P, M, C])
            OUT = ss.ps("OUT", [P, 2, C])
            bc_mm, bc_cp, exps, dbu, scans, hcs, summed, gated, out_mm, added = [
                ss.sem(n) for n in ("bc_mm", "bc_cp", "exps", "dbu", "scans", "hcs", "summed", "gated", "out_mm",
                                    "added")]
            Q = NC_ * N
            with nc.Block() as block:
                @block.tensor
                def _(pe):
                    def broadcasts(q):
                        if q >= 2:
                            pe.wait_ge(bc_cp, q - 1)
                        c, n = divmod(q, N)
                        for j in range(2):
                            row = 32 * (j + 1) + n
                            last = pe.matmul(BC[:, q % 2, j, :], g.ident[0:ROWS, row:row + 1].to_broadcast([ROWS, P]),
                                             xd[0:ROWS, c * C:(c + 1) * C], start=True, stop=True)
                        last.then_inc(bc_mm, 1)

                    def outputs(c):
                        pe.wait_ge(gated, 2 * (c + 1))
                        if c >= 2:
                            pe.wait_ge(added, c - 1)
                        for t in range(4):
                            o = OUT[:, c % 2, t * P:(t + 1) * P]
                            for m in range(M):
                                pe.matmul(o, yv[:, m, t * P:(t + 1) * P], g.w("m_out_w")[:, m * D:(m + 1) * D],
                                          start=(t == 0 and m == 0), stop=False, skip_group_check=True)
                            last = pe.matmul(o, g.ones[0:1, :], g.w("m_out_b"), start=False, stop=(t == 3),
                                             skip_group_check=True)
                        last.then_inc(out_mm, 1)

                    broadcasts(0)
                    for q in range(Q):
                        if q + 1 < Q:
                            broadcasts(q + 1)
                        if q % N == 2 and q > N:
                            outputs(q // N - 1)
                        if q % N == 0 and q:
                            pe.wait_ge(gated, 2 * (q // N) - 1)
                        pe.wait_ge(hcs, q + 1)
                        for m in range(M):
                            last = pe.matmul(Y[:, m, :], g.ident[:], hc[:, q % 2, m, :], start=(q % N == 0),
                                             stop=(q % N == N - 1))
                        last.then_inc(summed, 1)
                    outputs(NC_ - 1)

                @block.scalar
                def _(act):
                    for q in range(Q):
                        c, n = divmod(q, N)
                        act.wait_ge(bc_mm, q + 1)
                        if q >= 2:
                            act.wait_ge(hcs, q - 1)
                            act.wait_ge(dbu, q - 1)
                        act.activation(bc[:, q % 2, :, :], BC[:, q % 2, :, :], ACT.Copy).then_inc(bc_cp, 1)
                        if q >= 2:
                            act.wait_ge(scans, q - 1)
                        for m in range(M):
                            ins = act.activation(dA[:, q % 2, m, :], delta[:, m, c * C:(c + 1) * C], ACT.Exp,
                                                 scale=aneg[:, m * N + n:m * N + n + 1])
                        ins.then_inc(exps, 1)

                @block.gpsimd
                def _(pool):
                    for q in range(Q):
                        c = q // N
                        pool.wait_ge(bc_cp, q + 1)
                        if q >= 2:
                            pool.wait_ge(scans, q - 1)
                        pool.tensor_tensor(dBu[:, q % 2, :, :], du[:, :, c * C:(c + 1) * C],
                                           bc[:, q % 2, 0:1, :].to_broadcast([P, M, C]), ALU.mult).then_inc(dbu, 1)

                @block.vector
                def _(dve):
                    def times_c(q):
                        dve.wait_ge(scans, q + 1)
                        if q >= 2:
                            dve.wait_ge(summed, q - 1)
                        dve.tensor_tensor(hc[:, q % 2, :, :], hs[:, q % 2, :, :],
                                          bc[:, q % 2, 1:2, :].to_broadcast([P, M, C]), ALU.mult).then_inc(hcs, 1)

                    def finish(c):
                        dve.wait_ge(summed, N * (c + 1))
                        if c >= 1:
                            dve.wait_ge(out_mm, c)
                        for m in range(M):
                            ins = dve.scalar_tensor_tensor(out=yv[:, m, :], in0=u[:, m, c * C:(c + 1) * C],
                                                           scalar=g.w("m_d")[:, m:m + 1], in1=Y[:, m, :],
                                                           op0=ALU.mult, op1=ALU.add)
                        ins.then_inc(gated, 1)
                        dve.wait_ge(gated, 2 * c + 1)
                        dve.tensor_tensor(yv[:], yv[:], gate[:, :, c * C:(c + 1) * C], ALU.mult).then_inc(gated, 1)

                    def add_x(c):
                        dve.wait_ge(out_mm, c + 1)
                        xt = g.x[:, 4 * c:4 * c + 4, :]
                        dve.tensor_tensor(xt, xt, OUT[:, c % 2, :].rearrange("p (t d) -> p t d", t=4), ALU.add)\
                           .then_inc(added, 1)

                    for q in range(Q):
                        dve.wait_ge(exps, q + 1)
                        dve.wait_ge(dbu, q + 1)
                        if q >= 2:
                            dve.wait_ge(hcs, q - 1)
                        for m in range(M):
                            for b in range(2):
                                cols = slice(b * T, (b + 1) * T)
                                ins = dve.tensor_tensor_scan(out=hs[:, q % 2, m, cols], data0=dA[:, q % 2, m, cols],
                                                             data1=dBu[:, q % 2, m, cols], initial=0.0,
                                                             op0=ALU.mult, op1=ALU.add)
                        ins.then_inc(scans, 1)
                        if q >= 1:
                            times_c(q - 1)
                        if q % N == 0 and q:
                            finish(q // N - 1)
                        if q % N == 6 and q > N:
                            add_x(q // N - 1)
                    times_c(Q - 1)
                    finish(NC_ - 1)
                    add_x(NC_ - 1)


class RoutedPlan:
    G, NB = 4, 4
    UNITS = 4 * B
    GROUPS = UNITS // NB
    TAIL = 5

    def __init__(self):
        self.steps = []
        for i in range(self.UNITS + self.TAIL):
            items = []
            if i == 0:
                items += self.front(0, "gather") + self.front(0, "q") + self.front(0, "k")
            if i < self.UNITS:
                items.append(("v", i))
                nxt = i // self.NB + 1
                if nxt < self.GROUPS and i % self.NB:
                    items += self.front(nxt, ("gather", "q", "k")[i % self.NB - 1])
            if 0 <= i - 1 < self.UNITS:
                items.append(("turn", i - 1))
            self.steps.append(items)
        self.number = {item: n for n, item in enumerate(item for s in self.steps for item in s)}

    @staticmethod
    def front(group, what):
        return [(what, group, k) for k in range({"gather": 2, "q": 4, "k": 2}[what])]

    def unit(self, i):
        group, k = divmod(i, self.NB)
        g_, half = divmod(group, 2)
        return g_, half * self.NB + k


def routed_attention_stage(nc, g, name):
    plan = RoutedPlan()
    U, NB, G, H, DH, NQ, NK = plan.UNITS, plan.NB, plan.G, 8, 64, 128, 64
    ROWS = B * 2 * G
    wq, wk, wv, wo = g.big("r_wq"), g.big("r_wk"), g.big("r_wv"), g.big("r_wo")
    with Stage(nc, name) as st:
        sig = st.sb("sig", [P, TT, B, 2 * G])
        slot = st.sb("slot", [P, TT, B, 2 * G])
        rcount = st.sb("rcount", [P, TT, B])

        with Stage(nc, name + "r") as sr:
            lg = sr.sb("lg", [P, TT, B, 2 * G])
            row = sr.sb("row", [ROWS, T])
            work = sr.sb("work", [ROWS, T])
            best = sr.sb("best", [ROWS, 8])
            mask_kv = sr.sb("mask_kv", [ROWS, T])
            mask = sr.sb("mask", [ROWS, T])
            csum = sr.sb("csum", [ROWS, T])
            ones_row = sr.sb("ones_row", [ROWS, T])
            chosen = sr.sb("chosen", [P, TT, B, G])
            count = sr.sb("count", [P, TT, B])
            missed = sr.sb("missed", [P, TT, B])
            L = sr.ps("L", [P, 512])
            LT = sr.ps("LT", [P, 512])
            ST = sr.ps("ST", [P, 512])
            logits, lg_ready, rows_ready, slots_ready, back, steps = [
                sr.sem(n) for n in ("logits", "lg_ready", "rows_ready", "slots_ready", "back", "steps")]
            with nc.Block() as block:
                @block.tensor
                def _(pe):
                    for t in range(NT):
                        last = pe.matmul(L[:, t * 2 * G:(t + 1) * 2 * G], g.hT[:, t * P:(t + 1) * P],
                                         g.w("r_router"), start=True, stop=True)
                    last.then_inc(logits, 1)
                    pe.wait_ge(lg_ready, 1)
                    for h in range(TT):
                        last = pe.transpose(LT[0:ROWS, h * P:(h + 1) * P],
                                            lg[:, h, :, :].rearrange("p b j -> p (b j)"), g.ident[:])
                    last.then_inc(rows_ready, 1)
                    pe.wait_ge(slots_ready, 1)
                    for h in range(TT):
                        last = pe.transpose(ST[:, h * ROWS:(h + 1) * ROWS], csum[:, h * P:(h + 1) * P],
                                            g.ident[0:ROWS, 0:ROWS])
                    last.then_inc(back, 1)

                @block.scalar
                def _(act):
                    act.wait_ge(lg_ready, 1)
                    act.activation(sig[:], lg[:], ACT.Sigmoid)

                @block.vector
                def _(dve):
                    d = Steps(dve, steps)
                    dve.wait_ge(logits, 1)
                    dve.tensor_copy(lg[:], L[:, 0:NT * 2 * G].rearrange("p (b h j) -> p h b j", b=B, h=TT))\
                       .then_inc(lg_ready, 1)
                    dve.memset(ones_row[:], 1.0)
                    dve.wait_ge(rows_ready, 1)
                    d.mark(dve.tensor_copy(row[:], LT[0:ROWS, 0:T]))
                    d.done(dve.tensor_copy(work[:], LT[0:ROWS, 0:T]))
                    for k in range(NQ // 8):
                        d.done(dve.max(best[:], work[:]))
                        d.done(dve.match_replace(out=work[:], in_to_replace=best[:], in_values=work[:],
                                                 imm_value=NEG))
                        if 8 * (k + 1) == NK:
                            d.done(dve.tensor_tensor(mask_kv[:], work[:], row[:], ALU.not_equal))
                    d.done(dve.tensor_tensor(mask[:], work[:], row[:], ALU.not_equal))
                    d.done(dve.tensor_tensor(mask_kv[:], mask_kv[:], mask[:], ALU.subtract))
                    d.done(dve.scalar_tensor_tensor(out=mask[:], in0=mask_kv[:], scalar=g.w("r_iskv"), in1=mask[:],
                                                    op0=ALU.mult, op1=ALU.add))
                    d.done(dve.tensor_tensor_scan(out=csum[:], data0=ones_row[:], data1=mask[:], initial=0.0,
                                                  op0=ALU.mult, op1=ALU.add))
                    d.done(dve.tensor_tensor(csum[:], csum[:], mask[:], ALU.mult))
                    dve.tensor_scalar(csum[:], csum[:], -1.0, None, ALU.add).then_inc(slots_ready, 1)
                    dve.wait_ge(back, 1)
                    d.done(dve.tensor_copy(slot[:].rearrange("p h b j -> p (h b j)"), ST[:, 0:TT * ROWS]))
                    d.done(dve.tensor_scalar(chosen[:], slot[:, :, :, 0:G], 0.0, None, ALU.is_ge))
                    d.done(dve.tensor_reduce(count[:], chosen[:], AX_X, ALU.add))
                    d.mark(dve.tensor_scalar(missed[:], count[:], 0.0, None, ALU.is_le))
                    d.done(dve.tensor_scalar(rcount[:], count[:], 1e-5, None, ALU.max))
                    d.done(dve.reciprocal(rcount[:], rcount[:]))
                    for t in range(NT):
                        b, h = divmod(t, TT)
                        dve.scalar_tensor_tensor(out=g.x[:, t, :], in0=g.w("r_null"), scalar=missed[:, h, b:b + 1],
                                                 in1=g.x[:, t, :], op0=ALU.mult, op1=ALU.add)

        with Stage(nc, name + "a") as sa:
            oh = sa.sb("oh", [P, NB, TT, 2 * P])
            sq = g.hT[:, 0:NTOK].rearrange("p (u h s) -> p u h s", u=2 * NB, h=TT)
            sel = sa.sb("sel", [P, 2, NB, 2 * P])
            qT = sa.sb("qT", [P, 2, 4, NB, NQ])
            kT = sa.sb("kT", [P, 2, 4, NB, NK + 1])
            v = sa.sb("v", [P, 3, 4 * DH])
            ev = sa.sb("ev", [P, 2, 2, 4, NK + 1])
            mx = sa.sb("mx", [P, 2, 2, 4])
            rsum = sa.sb("rsum", [P, 2, 2, 4])
            pr = sa.sb("pr", [P, 2, H, NK])
            pn = sa.sb("pn", [P, 2, H])
            prT = sa.sb("prT", [P, 2, 512])
            pnT = sa.sb("pnT", [H, 2, NQ])
            sqT = sa.sb("sqT", [P, 4, T])
            oT = sa.sb("oT", [P, 2, 512])
            o = sa.sb("o", [P, 2, D])
            F = sa.ps("F", [P, 2, 512])
            S = sa.ps("S", [P, 2, 512])
            PT = sa.ps("PT", [P, 512])
            OT = sa.ps("OT", [P, 512])
            OUT = sa.ps("OUT", [P, 512])
            X = sa.ps("X", [P, 512])
            (onehots, scaled, nullk, f_mm, f_cp, scored, maxed, shifted, expd, summed, recip, normed, turned,
             prT_cp, pv, oT_cp, projected, o_cp, scattered, added) = [
                sa.sem(n) for n in ("onehots", "scaled", "nullk", "f_mm", "f_cp", "scored", "maxed", "shifted",
                                    "expd", "summed", "recip", "normed", "turned", "prT_cp", "pv", "oT_cp",
                                    "projected", "o_cp", "scattered", "added")]

            def copied(*item):
                return plan.number[item] + 1

            with nc.Block() as block:
                @block.tensor
                def _(pe):
                    def item(it):
                        n = plan.number[it]
                        f = F[:, n % 2, :]
                        if n >= 2:
                            pe.wait_ge(f_cp, n - 1)
                        if it[0] == "gather":
                            _, group, k = it
                            for bb in (2 * k, 2 * k + 1):
                                b = plan.unit(group * NB + bb)[1]
                                pe.wait_ge(scaled, group * NB + bb + 1)
                                for h in range(TT):
                                    last = pe.matmul(f[:, (bb % 2) * 256:(bb % 2 + 1) * 256], g.h[:, TT * b + h, :],
                                                     oh[:, bb, h, :], start=(h == 0), stop=(h == TT - 1))
                        elif it[0] == "q":
                            _, group, c = it
                            s = plan.unit(group * NB)[0]
                            pe.wait_ge(f_cp, copied("gather", group, 1))
                            last = pe.matmul(f, wq[:, (4 * s + c) * P:(4 * s + c + 1) * P], sel[:, group % 2, :, 0:NQ],
                                             start=True, stop=True)
                        elif it[0] == "k":
                            _, group, k = it
                            s = plan.unit(group * NB)[0]
                            for c in (2 * k, 2 * k + 1):
                                last = pe.matmul(f[:, (c % 2) * 256:(c % 2 + 1) * 256],
                                                 wk[:, (4 * s + c) * P:(4 * s + c + 1) * P],
                                                 sel[:, group % 2, :, NQ:NQ + NK], start=True, stop=True)
                        elif it[0] == "v":
                            i = it[1]
                            s = plan.unit(i)[0]
                            for par in range(2):
                                last = pe.matmul(f[par * DH:(par + 1) * DH, 0:256],
                                                 sel[:, (i // NB) % 2, i % NB, NQ + NK:],
                                                 wv[:, (2 * s + par) * 256:(2 * s + par + 1) * 256],
                                                 start=True, stop=True, tile_position=(0, par * DH))
                        else:
                            j = it[1]
                            pe.wait_ge(normed, 2 * (j + 1))
                            for h in range(TT):
                                pe.transpose(f[:, h * P:(h + 1) * P], sq[:, j % (2 * NB), h, :], g.ident[:])
                            last = pe.transpose(f[0:H, 2 * P:3 * P], pn[:, j % 2, :], g.ident[:])
                        last.then_inc(f_mm, 1)

                    for i in range(U + plan.TAIL):
                        items = plan.steps[i]
                        if i == 0:
                            for it in items[:-1]:
                                item(it)
                            items = items[-1:]
                        if i < U:
                            group = i // NB
                            pe.wait_ge(f_cp, copied("k", group, 1))
                            pe.wait_ge(nullk, group + 1)
                            if i >= 1:
                                pe.wait_ge(shifted, i)
                            for h in range(H):
                                rows = slice((h % 2) * DH, (h % 2 + 1) * DH)
                                last = pe.matmul(S[:, h % 2, (h // 2) * (NK + 1):(h // 2 + 1) * (NK + 1)],
                                                 qT[rows, group % 2, h // 2, i % NB, :],
                                                 kT[rows, group % 2, h // 2, i % NB, :], start=True, stop=True)
                            last.then_inc(scored, 1)
                        for it in items:
                            item(it)
                        j = i - 1
                        if 0 <= j < U:
                            if j >= 1:
                                pe.wait_ge(prT_cp, j)
                            for c in range(4):
                                last = pe.transpose(PT[:, c * P:(c + 1) * P],
                                                    pr[:, j % 2, 2 * c:2 * c + 2, :].rearrange("p h k -> p (h k)"),
                                                    g.ident[:])
                            last.then_inc(turned, 1)
                        j = i - 2
                        if 0 <= j < U:
                            s = plan.unit(j)[0]
                            pe.wait_ge(prT_cp, j + 1)
                            if j >= 1:
                                pe.wait_ge(oT_cp, j)
                            for c in range(4):
                                pe.matmul(OT[:, c * P:(c + 1) * P], g.big("r_nv")[:, (4 * s + c) * P:(4 * s + c + 1) * P],
                                          pnT[:, j % 2, :], start=(c == 0), stop=False, skip_group_check=True)
                            for h in range(H):
                                rows = slice((h % 2) * DH, (h % 2 + 1) * DH)
                                c = h // 2
                                last = pe.matmul(OT[rows, c * P:(c + 1) * P], v[rows, j % 3, c * DH:(c + 1) * DH],
                                                 prT[rows, j % 2, c * P:(c + 1) * P], start=False, stop=(h == H - 1),
                                                 skip_group_check=True)
                            last.then_inc(pv, 1)
                        j = i - 3
                        if 0 <= j < U:
                            s = plan.unit(j)[0]
                            pe.wait_ge(oT_cp, j + 1)
                            if j >= 1:
                                pe.wait_ge(o_cp, j)
                            for c in range(4):
                                last = pe.matmul(OUT[:, 0:D], oT[:, j % 2, c * P:(c + 1) * P],
                                                 wo[:, (4 * s + c) * P:(4 * s + c + 1) * P],
                                                 start=(c == 0), stop=(c == 3))
                            last.then_inc(projected, 1)
                        j = i - 4
                        if 0 <= j < U:
                            pe.wait_ge(o_cp, j + 1)
                            if j >= 1:
                                pe.wait_ge(added, TT * j)
                            for h in range(TT):
                                last = pe.matmul(X[:, h * D:(h + 1) * D], sqT[:, j % 4, h * P:(h + 1) * P],
                                                 o[:, j % 2, :], start=True, stop=True)
                            last.then_inc(scattered, 1)

                @block.scalar
                def _(act):
                    for i in range(U + plan.TAIL):
                        for it in plan.steps[i]:
                            n = plan.number[it]
                            f = F[:, n % 2, :]
                            if it[0] == "turn":
                                continue
                            act.wait_ge(f_mm, n + 1)
                            if it[0] == "gather":
                                _, group, k = it
                                act.activation(sel[:, group % 2, 2 * k:2 * k + 2, :],
                                               f.rearrange("p (b s) -> p b s", b=2), ACT.Copy).then_inc(f_cp, 1)
                            elif it[0] == "q":
                                _, group, c = it
                                act.activation(qT[:, group % 2, c, :, :], f.rearrange("p (b s) -> p b s", b=NB),
                                               ACT.Copy).then_inc(f_cp, 1)
                            elif it[0] == "k":
                                _, group, k = it
                                act.activation(kT[:, group % 2, 2 * k:2 * k + 2, :, 0:NK],
                                               f.rearrange("p (c b s) -> p c b s", c=2, b=NB),
                                               ACT.Copy).then_inc(f_cp, 1)
                            else:
                                act.activation(v[:, it[1] % 3, :], f[:, 0:256], ACT.Copy).then_inc(f_cp, 1)
                        if i < U:
                            act.wait_ge(shifted, i + 1)
                            act.activation(ev[:, i % 2, :, :, :], ev[:, i % 2, :, :, :], ACT.Exp,
                                           scale=DH ** -0.5).then_inc(expd, 1)
                        j = i - 1
                        if 0 <= j < U:
                            n = plan.number[("turn", j)]
                            f = F[:, n % 2, :]
                            act.wait_ge(f_mm, n + 1)
                            act.activation(sqT[:, j % 4, :], f[:, 0:2 * P], ACT.Copy)
                            act.activation(pnT[:, j % 2, :], f[0:H, 2 * P:3 * P], ACT.Copy).then_inc(f_cp, 1)
                            act.wait_ge(turned, j + 1)
                            act.activation(prT[:, j % 2, :], PT[:], ACT.Copy).then_inc(prT_cp, 1)
                        j = i - 2
                        if 0 <= j < U:
                            act.wait_ge(pv, j + 1)
                            act.activation(oT[:, j % 2, :], OT[:], ACT.Copy).then_inc(oT_cp, 1)

                @block.gpsimd
                def _(pool):
                    def scale_onehots(group):
                        s = plan.unit(group * NB)[0]
                        if group >= 2:
                            pool.wait_ge(scored, (group - 1) * NB)
                        pool.tensor_copy(kT[:, group % 2, :, :, NK],
                                         g.big("r_nk")[:, 4 * s:4 * s + 4].unsqueeze(2).to_broadcast([P, 4, NB]))\
                            .then_inc(nullk, 1)
                        for k in range(NB):
                            u = group * NB + k
                            b = plan.unit(u)[1]
                            pool.wait_ge(onehots, 2 * (u + 1))
                            if u >= 2 * NB:
                                pool.wait_ge(f_mm, plan.number[("turn", u - 2 * NB)] + 1)
                            pool.tensor_tensor(sq[:, u % (2 * NB), :, :], oh[:, k, :, 0:NQ],
                                               sig[:, :, b, s:s + 1].to_broadcast([P, TT, NQ]), ALU.mult)
                            pool.tensor_tensor(oh[:, k, :, NQ + NK:], oh[:, k, :, NQ:NQ + NK],
                                               sig[:, :, b, G + s:G + s + 1].to_broadcast([P, TT, NK]),
                                               ALU.mult).then_inc(scaled, 1)

                    scale_onehots(0)
                    for i in range(U):
                        if i % NB == 0 and i // NB + 1 < plan.GROUPS:
                            scale_onehots(i // NB + 1)
                        pool.wait_ge(recip, i + 1)
                        if i >= 2:
                            pool.wait_ge(turned, i - 1)
                        pool.tensor_tensor(pr[:, i % 2, :, :].rearrange("p (c q) k -> p q c k", q=2),
                                           ev[:, i % 2, :, :, 0:NK],
                                           rsum[:, i % 2, :, :].unsqueeze(3).to_broadcast([P, 2, 4, NK]),
                                           ALU.mult).then_inc(normed, 1)
                        pool.tensor_tensor(pn[:, i % 2, :].rearrange("p (c q) -> p q c", q=2),
                                           ev[:, i % 2, :, :, NK], rsum[:, i % 2, :, :], ALU.mult)\
                            .then_inc(normed, 1)

                @block.vector
                def _(dve):
                    def make_onehots(group):
                        s = plan.unit(group * NB)[0]
                        if group >= 1:
                            dve.wait_ge(f_mm, plan.number[("gather", group - 1, 1)] + 1)
                        for k in range(NB):
                            b = plan.unit(group * NB + k)[1]
                            for lo, n, j in ((0, NQ, s), (NQ, NK, G + s)):
                                dve.tensor_tensor(oh[:, k, :, lo:lo + n],
                                                  g.iota_free[:, 0:n].unsqueeze(1).to_broadcast([P, TT, n]),
                                                  slot[:, :, b, j:j + 1].to_broadcast([P, TT, n]),
                                                  ALU.is_equal).then_inc(onehots, 1)

                    make_onehots(0)
                    for i in range(U + plan.TAIL):
                        if i < U:
                            s4 = S[:, :, 0:4 * (NK + 1)].rearrange("p i (h k) -> p i h k", h=4)
                            dve.wait_ge(scored, i + 1)
                            dve.tensor_reduce(mx[:, i % 2, :, :], s4, AX_X, ALU.max).then_inc(maxed, 1)
                            dve.wait_ge(maxed, i + 1)
                            if i >= 2:
                                dve.wait_ge(normed, 2 * (i - 1))
                            dve.tensor_tensor(ev[:, i % 2, :, :, :], s4,
                                              mx[:, i % 2, :, :].unsqueeze(3).to_broadcast([P, 2, 4, NK + 1]),
                                              ALU.subtract).then_inc(shifted, 1)
                            if i % NB == 0 and i // NB + 1 < plan.GROUPS:
                                make_onehots(i // NB + 1)
                            dve.wait_ge(expd, i + 1)
                            dve.tensor_reduce(rsum[:, i % 2, :, :], ev[:, i % 2, :, :, :], AX_X, ALU.add)\
                               .then_inc(summed, 1)
                            dve.wait_ge(summed, i + 1)
                            dve.reciprocal(rsum[:, i % 2, :, :], rsum[:, i % 2, :, :]).then_inc(recip, 1)
                        j = i - 3
                        if 0 <= j < U:
                            dve.wait_ge(projected, j + 1)
                            if j >= 2:
                                dve.wait_ge(scattered, j - 1)
                            dve.tensor_copy(o[:, j % 2, :], OUT[:, 0:D]).then_inc(o_cp, 1)
                        j = i - 4
                        if 0 <= j < U:
                            b = plan.unit(j)[1]
                            dve.wait_ge(scattered, j + 1)
                            for h in range(TT):
                                xt = g.x[:, TT * b + h, :]
                                dve.scalar_tensor_tensor(out=xt, in0=X[:, h * D:(h + 1) * D],
                                                         scalar=rcount[:, h, b:b + 1], in1=xt,
                                                         op0=ALU.mult, op1=ALU.add).then_inc(added, 1)


class Globals:

    def __init__(self, nc, stack, weights, a):
        def sb(name, shape, dt=F32):
            return stack.enter_context(nc.sbuf_tensor("all_" + name, shape, dt))

        self.a = a
        self.at = weights.at
        self.x = sb("x", [P, NT, D])
        self.h = sb("h", [P, NT, D])
        self.hT = sb("hT", [P, NTOK + 2 * T])
        self.W = sb("W", [P, weights.n])
        self.enc_layout = weights.enc_layout
        self.big_at = {**weights.routed.at, **weights.moe.at}
        self.big_n = {"routed": weights.routed.n, "moe": weights.moe.n}
        self.ident = sb("ident", [P, P])
        self.ident_bf = sb("ident_bf", [P, P], BF16)
        self.ones = sb("ones", [P, P])
        self.neg_half = sb("neg_half", [P, NT])
        self.eps = sb("eps", [P, TT])
        self.causal01 = sb("causal01", [P, T])
        self.masks = {m: sb(f"mask_{m}", [P, TT, T], BF16) for m in ("causal", "window")}

    def w(self, name):
        c, n, rows = self.at[name]
        return self.W[0:rows, c:c + n]

    def big(self, name):
        c, n, rows = self.big_at[name]
        return self.BIG[0:rows, c:c + n]

    def has(self, name):
        return name in self.at


def load_stage(nc, g):
    with Stage(nc, "load") as st:
        x_in, zero, made, w_in = st.sem("x_in"), st.sem("zero"), st.sem("made"), st.sem("w_in")
        with nc.Block() as block:
            @block.sync
            def _(sp):
                sp.dma_start(g.x[:], g.a["x"].rearrange("b (t p) d -> p (b t) d", p=P)).then_inc(x_in, 16)
                n = g.W.shape[1]
                cut = list(range(0, n, 4096)) + [n]
                for lo, hi in zip(cut, cut[1:]):
                    sp.dma_start(g.W[:, lo:hi], g.a["weights"][:, lo:hi]).then_inc(w_in, 16)
                sp.wait_ge(x_in, 16)
                sp.wait_ge(w_in, 16 * (len(cut) - 1))

            @block.gpsimd
            def _(pool):
                pool.memset(g.ident[:], 0.0).then_inc(zero, 1)
                pool.memset(g.ident_bf[:], 0.0).then_inc(zero, 1)
                pool.memset(g.masks["causal"][:], 0.0).then_inc(zero, 1)
                pool.memset(g.masks["window"][:], 0.0).then_inc(zero, 1)
                pool.memset(g.ones[:], 1.0)
                pool.memset(g.neg_half[:], -0.5)
                pool.memset(g.eps[:], LN_EPS)
                pool.memset(g.hT[:, NTOK:], 0.0)
                pool.memset(g.causal01[:], 1.0).then_inc(zero, 1)
                pool.wait_ge(zero, 5)
                pool.affine_select(out=g.causal01[:], in_=g.causal01[:], compare_op=ALU.is_ge, fill=0.0,
                                   base=0, pattern=[[1, T]], channel_multiplier=-1)
                for m in (g.ident, g.ident_bf):
                    pool.affine_select(out=m[:], in_=m[:], compare_op=ALU.not_equal, fill=1.0, base=0,
                                       pattern=[[-1, P]], channel_multiplier=1)
                for m in ("causal", "window"):
                    pool.affine_select(out=g.masks[m][:], in_=g.masks[m][:], compare_op=ALU.is_ge, fill=NEG,
                                       base=0, pattern=[[P, TT], [-1, T]], channel_multiplier=1).then_inc(made, 1)
                pool.wait_ge(made, 2)
                m = g.masks["window"]
                pool.affine_select(out=m[:], in_=m[:], compare_op=ALU.is_ge, fill=NEG,
                                   base=63, pattern=[[-P, TT], [1, T]], channel_multiplier=-1)


def load_big_stage(nc, g, which, iota, n, stack):
    g.BIG = stack.enter_context(nc.sbuf_tensor(f"big{n}", [P, g.big_n[which]], F32))
    g.iota_free = stack.enter_context(nc.sbuf_tensor(f"iota{n}", [P, iota], F32))
    with Stage(nc, f"load_big{n}") as st:
        loaded = st.sem("loaded")
        with nc.Block() as block:
            @block.sync
            def _(sp):
                width = g.big_n[which]
                half = width // 2
                sp.dma_start(g.BIG[:, 0:half], g.a[which][:, 0:half]).then_inc(loaded, 16)
                sp.dma_start(g.BIG[:, half:width], g.a[which][:, half:width]).then_inc(loaded, 16)
                sp.wait_ge(loaded, 32)

            @block.gpsimd
            def _(pool):
                pool.iota(g.iota_free[:], pattern=[[1, iota]], base=0, channel_multiplier=0,
                          allow_small_or_imprecise_dtypes=True)


def store_stage(nc, g):
    with Stage(nc, "store") as st:
        out_done = st.sem("out_done")
        with nc.Block() as block:
            @block.sync
            def _(sp):
                sp.dma_start(g.a["out"].rearrange("b (t p) d -> p (b t) d", p=P), g.x[:]).then_inc(out_done, 16)
                sp.wait_ge(out_done, 16)


LAYERS = ["L0_attn_a", "L0_ffn", "L0_attn_b", "L0_ffn", "L1_attn_a", "L1_ffn", "L1_attn_b", "L1_ffn",
          "L2_attn_a", "L2_ffn", "L2_attn_b", "L2_ffn", "L3_attn_a", "L3_ffn", "L3_attn_b", "L3_ffn"]


def build_program(nc, weights, a, layers=range(16)):
    with ExitStack() as stack:
        g = Globals(nc, stack, weights, a)
        load_stage(nc, g)
        big = ExitStack()
        for n in layers:
            if LAYERS[n] == "L0_ffn":
                load_big_stage(nc, g, "routed", P, n, big)
            if LAYERS[n] == "L2_ffn":
                load_big_stage(nc, g, "moe", MOE_E * MOE_CAP, n, big)
            layer_norm_stage(nc, g, f"ln{n}")
            name = LAYERS[n]
            if name == "L0_attn_a":
                mamba_stage(nc, g, f"s{n}")
            elif name == "L0_ffn":
                routed_attention_stage(nc, g, f"s{n}")
            elif name == "L0_attn_b":
                attention_stage(nc, g, f"s{n}", "L0b_", 8, 8 ** -0.5, mask="causal")
            elif name == "L2_attn_b":
                attention_stage(nc, g, f"s{n}", "L2b_", 8, 128 ** -0.5)
            elif name == "L1_attn_b":
                linear_attention_stage(nc, g, f"s{n}", "L1b_", 8, 1.0, wo=True, linear=True)
            elif name == "L1_attn_a":
                alibi_attention_stage(nc, g, f"s{n}")
            elif name == "L3_attn_a":
                attention_stage(nc, g, f"s{n}", "L3a_", 64, 64 ** -0.5)
            elif name == "L1_ffn":
                channel_mix_stage(nc, g, f"s{n}")
            elif name == "L2_attn_a":
                kernel_attention_stage(nc, g, f"s{n}")
            elif name == "L2_ffn":
                moe_stage(nc, g, f"s{n}")
            elif name == "L3_ffn":
                encoder_stage(nc, g, f"s{n}")
            elif name == "L3_attn_b":
                attention_stage(nc, g, f"s{n}", "L3b_", 8, 8 ** -0.5, mask="window")
            big.close()
            big = ExitStack()
        store_stage(nc, g)



def head_chunks(w, hd):
    hs = 32 if hd <= 32 else 64
    out = np.zeros((w.shape[1], w.shape[0] // hd, hs), w.dtype)
    out[:, :, :hd] = w.T.reshape(w.shape[1], -1, hd)
    return out.reshape(w.shape[1], -1)


def head_rows(w, hd):
    hs = 32 if hd <= 32 else 64
    out = np.zeros((w.shape[0] // hd, hs, w.shape[1]), w.dtype)
    out[:, :hd] = w.reshape(-1, hd, w.shape[1])
    return out.reshape(-1, P, w.shape[1]).transpose(1, 0, 2).reshape(P, -1)


def head_columns(b, hd):
    hs = 32 if hd <= 32 else 64
    out = np.zeros((b.shape[0] // hd, hs), b.dtype)
    out[:, :hd] = b.reshape(-1, hd)
    return out.reshape(-1, P).T


def pack(i):
    W = Weights()
    w, b = i["L0_attn_b_W"], i["L0_attn_b_b"]
    W.add("L0b_wq", head_chunks(w[:D], 8))
    W.add("L0b_wk", head_chunks(w[D:2 * D], 8))
    W.add("L0b_wv", w[2 * D:].T)
    W.add("L0b_wo", head_rows(np.eye(D, dtype=w.dtype), 8))
    W.add("L0b_bq", head_columns(b[:D], 8))
    W.add("L0b_bk", head_columns(b[D:2 * D], 8))
    W.add("L0b_bv", b[None, 2 * D:])
    W.add("L2b_wq", head_chunks(i["L2_attn_b_Wq"].T, 8))
    W.add("L2b_wk", head_chunks(i["L2_attn_b_Wk"].T, 8))
    W.add("L2b_wv", i["L2_attn_b_Wk"])
    W.add("L2b_wo", head_rows(np.eye(D, dtype=w.dtype), 8))
    W.add("L2b_bq", head_columns(i["L2_attn_b_bq"], 8))
    W.add("L2b_bk", head_columns(i["L2_attn_b_bk"], 8))
    W.add("L2b_bv", i["L2_attn_b_bk"][None])
    W.add("L3b_wq", head_chunks(i["L3_attn_b_Wq"], 8))
    W.add("L3b_wk", head_chunks(i["L3_attn_b_Wk"], 8))
    W.add("L3b_wv", i["L3_attn_b_Wv"].T)
    W.add("L3b_wo", head_rows(i["L3_attn_b_Wo"].T, 8))
    W.add("L3a_wq", head_chunks(i["L3_attn_a_Wq"], 64))
    W.add("L3a_wk", head_chunks(i["L3_attn_a_Wk"], 64))
    W.add("L3a_wv", i["L3_attn_a_Wv"].T)
    W.add("L3a_wo", head_rows(i["L3_attn_a_Wo"].T, 64))
    W.add("L3a_bq", head_columns(i["L3_attn_a_bq"], 64))
    W.add("L3a_bk", head_columns(i["L3_attn_a_bk"], 64))
    W.add("L3a_bv", i["L3_attn_a_bv"][None])
    w = i["L1_attn_b_w_attn"]
    W.add("L1b_wq", head_chunks(w[:D], 8))
    W.add("L1b_wk", head_chunks(w[D:2 * D], 8))
    W.add("L1b_wv", w[2 * D:].T)
    W.add("L1b_wo", i["L1_attn_b_w_proj"].T)
    W.add("L1a_wqk", i["L1_attn_a_W_qk"])
    W.add("L1a_wv", i["L1_attn_a_W_v"].T)
    W.add("L1a_slope", np.broadcast_to(i["L1_attn_a_alibi_slope"][None], (P, 1)))
    W.add("L3a_bo", np.broadcast_to(i["L3_attn_a_bo"][None], (P, D)))
    for n in "rkv":
        W.add(f"L1f_w{n}", i[f"L1_ffn_W_{n}"].T)
    W.add("L1f_mu", np.stack([i["L1_ffn_mu_r"], i["L1_ffn_mu_k"]], 1))
    W.add("L2a_wqk", np.concatenate([i["L2_attn_a_Wq"].T, i["L2_attn_a_Wk"].T], 1))
    W.add("L2a_bqk", np.stack([i["L2_attn_a_bq"], i["L2_attn_a_bk"]], 1))
    W.add("L2a_wv", i["L2_attn_a_Wv"].T)
    W.add("L2a_bv", i["L2_attn_a_bv"][None])
    W.add("L2a_wo", i["L2_attn_a_Wo"].T)
    W.add("L2a_bo", np.broadcast_to(i["L2_attn_a_bo"][None], (P, D)))
    r = np.zeros((16, 8, 16, 8), np.float32)
    blocks = np.zeros((16, 8, 16, 8), np.float32)
    for h in range(16):
        r[h, :, h] = i["L2_attn_a_R"]
        blocks[h, :, h] = 1.0
    W.add("L2a_rblk", r.reshape(P, P))
    W.add("L2a_blocks", blocks.reshape(P, P))
    nhalf = np.zeros((16, 8, 16, 8), np.float32)
    for h in range(16):
        nhalf[h, :, h] = -0.5
    W.add("L2a_nhalf", nhalf.reshape(P, P))
    W.add("L2a_headof", np.ascontiguousarray(blocks.reshape(P, 16, 8)[:, :, 0]))
    W.add("moe_rw", i["L2_ffn_router_w"])
    W.add("moe_rb", np.broadcast_to(i["L2_ffn_router_b"][None], (P, MOE_E)))
    W.add("moe_iota", np.broadcast_to(np.arange(MOE_E, dtype=np.float32)[None], (P, MOE_E)))
    keep = np.ones((P, MOE_E, NT), np.float32)
    keep[:, :, 0] = 0.0
    W.add("moe_keep", keep.reshape(P, -1))
    W.add("moe_rowid", (np.arange(P)[:, None] + P * np.arange(MOE_E + 2)[None]).astype(np.float32))
    W.add("m_in_w", i["L0_attn_a_in_proj_w"].T)
    W.add("m_in_b", i["L0_attn_a_in_proj_b"].reshape(4, P).T)
    W.add("m_conv_w", i["L0_attn_a_conv_w"].reshape(2, P, 4).transpose(1, 0, 2).reshape(P, 8))
    W.add("m_conv_b", i["L0_attn_a_conv_b"].reshape(2, P).T)
    xw = np.zeros((P, 2, 80), np.float32)
    xp = i["L0_attn_a_x_proj_w"].reshape(-1, 2, P).transpose(2, 1, 0)
    xw[:, :, 0:DT_RANK] = xp[:, :, 0:DT_RANK]
    xw[:, :, 32:32 + STATE] = xp[:, :, DT_RANK:DT_RANK + STATE]
    xw[:, :, 64:64 + STATE] = xp[:, :, DT_RANK + STATE:]
    W.add("m_x_w", xw.reshape(P, -1))
    W.add("m_dt_w", i["L0_attn_a_dt_proj_w"].T)
    W.add("m_dt_b", i["L0_attn_a_dt_proj_b"].reshape(2, P).T)
    W.add("m_a_log", i["L0_attn_a_A_log"].reshape(2, P, STATE).transpose(1, 0, 2).reshape(P, -1))
    W.add("m_d", i["L0_attn_a_D_param"].reshape(2, P).T)
    W.add("m_out_w", i["L0_attn_a_out_proj_w"].T.reshape(2, P, D).transpose(1, 0, 2).reshape(P, -1))
    W.add("m_out_b", i["L0_attn_a_out_proj_b"][None])
    M = W.moe = Weights()
    M.add("moe_w1", i["L2_ffn_w1"].transpose(1, 0, 2).reshape(D, -1))
    M.add("moe_w2", i["L2_ffn_w2"].reshape(MOE_E * 4, P, D).transpose(1, 0, 2).reshape(P, -1))
    M.add("moe_b1", i["L2_ffn_b1"].reshape(MOE_E * 4, P).T)
    M.add("moe_b2", i["L2_ffn_b2"].reshape(1, -1))
    M.add("moe_ow1", i["L2_ffn_ow1"])
    M.add("moe_ow2", i["L2_ffn_ow2"].reshape(4, P, D).transpose(1, 0, 2).reshape(P, -1))
    M.add("moe_ob1", i["L2_ffn_ob1"].reshape(4, P).T)
    M.add("moe_ob2", i["L2_ffn_ob2"][None])
    R = W.routed = Weights()
    R.add("r_wq", i["L0_ffn_w_q"].transpose(2, 0, 1).reshape(D, -1))
    wkv = i["L0_ffn_w_kv"].reshape(4, 2, 4, 2, 64, D)
    R.add("r_wk", wkv[:, 0].transpose(4, 0, 1, 2, 3).reshape(D, -1))
    R.add("r_wv", wkv[:, 1].transpose(4, 0, 2, 1, 3).reshape(D, -1))
    R.add("r_wo", i["L0_ffn_w_out"].transpose(2, 0, 1).reshape(4, P, 4, D).transpose(1, 2, 0, 3).reshape(P, -1))
    R.add("r_nk", i["L0_ffn_null_kv"][0].reshape(4, 4, P).transpose(2, 0, 1).reshape(P, -1))
    nv = np.zeros((4, 2, 4, 4, 2, 64), np.float32)
    for h in range(8):
        nv[h // 2, h % 2, :, h // 2, h % 2] = i["L0_ffn_null_kv"][1, :, h, 0]
    R.add("r_nv", nv.reshape(8, -1))
    W.add("r_router", np.concatenate([i["L0_ffn_w_qr"], i["L0_ffn_w_kvr"]], 0).T)
    W.add("r_null", np.broadcast_to(i["L0_ffn_null_token"][0], (P, D)))
    W.add("r_iskv", np.tile([0.0] * 4 + [1.0] * 4, B).astype(np.float32)[:, None])
    W.add("enc_gate_w", i["L3_ffn_gate_w"].T)
    W.add("enc_gate_b", np.broadcast_to(i["L3_ffn_gate_b"][None], (B, 4)))
    W.add("enc_iota", np.broadcast_to(np.arange(4, dtype=np.float32)[None], (B, 4)))
    experts = [encoder_weights(i, e) for e in range(4)]
    W.enc_layout = (experts[0][0].at, experts[0][0].n, experts[0][1].at, experts[0][1].n)
    W.enc_a = np.stack([e[0].packed() for e in experts])
    W.enc_b = np.stack([e[1].packed() for e in experts])
    return W


def encoder_weights(i, e):
    A, Bw = Weights(), Weights()
    p = {n: i["L3_ffn_" + n][e] for n in ("in_proj_w", "in_proj_b", "out_proj_w", "out_proj_b", "lin1_w",
                                          "lin1_b", "lin2_w", "lin2_b", "ln1_w", "ln1_b", "ln2_w", "ln2_b")}
    w, b = p["in_proj_w"], p["in_proj_b"]
    A.add("wq", head_chunks(w[:D], 8))
    A.add("wk", head_chunks(w[D:2 * D], 8))
    A.add("wv", w[2 * D:].T)
    A.add("bq", head_columns(b[:D], 8))
    A.add("bk", head_columns(b[D:2 * D], 8))
    A.add("bv", b[None, 2 * D:])
    Bw.add("wo", head_rows(p["out_proj_w"].T, 8))
    Bw.add("w1", p["lin1_w"].T)
    Bw.add("w2", p["lin2_w"].T.reshape(4, P, D).transpose(1, 0, 2).reshape(P, -1))
    Bw.add("b1", p["lin1_b"].reshape(4, P).T)
    for to, of in (("ob", "out_proj_b"), ("b2", "lin2_b"), ("n1w", "ln1_w"), ("n1b", "ln1_b"),
                   ("n2w", "ln2_w"), ("n2b", "ln2_b")):
        Bw.add(to, np.broadcast_to(p[of][None], (P, D)))
    return A, Bw


def kernel(**inputs):
    import concourse.bacc as _bacc
    from concourse.bass_utils import run_bass_kernel_spmd as _run

    nc = _bacc.Bacc("TRN2", target_bir_lowering=False, num_devices=1)
    weights = pack({k: np.asarray(v) for k, v in inputs.items()})
    arrays = {"x": np.ascontiguousarray(inputs["L0_attn_a_x"]), "weights": weights.packed(),
              "enc_a": weights.enc_a, "enc_b": weights.enc_b,
              "routed": weights.routed.packed(), "moe": weights.moe.packed()}
    a = {n: nc.dram_tensor(n, v.shape, mybir.dt.from_np(v.dtype), kind="ExternalInput").ap()
         for n, v in arrays.items()}
    a["out"] = nc.dram_tensor("out", (B, T, D), F32, kind="ExternalOutput").ap()
    build_program(nc, weights, a)
    r = _run(nc, [arrays], core_ids=[0])
    return r.results[0]["out"]
```

```python
from contextlib import ExitStack

import concourse.bass as bass
import numpy as np
from concourse import mybir

F32 = mybir.dt.float32
BF16 = mybir.dt.bfloat16
ALU = mybir.AluOpType
ACT = mybir.ActivationFunctionType
AX_X = mybir.AxisListType.X

P = 128
B, T, D = 8, 256, 128
TT = T // P
NT = B * TT
NTOK = B * T
LN_EPS = 1e-5
NEG = -1.0e30
DT_RANK, STATE = 8, 16
HEAD = 8


class Stage:

    def __init__(self, nc, name):
        self.nc, self.name, self.stack, self.sems = nc, name, ExitStack(), []

    def sb(self, name, shape, dt=F32):
        return self.stack.enter_context(self.nc.sbuf_tensor(f"{self.name}_{name}", shape, dt))

    def ps(self, name, shape, dt=F32):
        return self.stack.enter_context(self.nc.psum_tensor(f"{self.name}_{name}", shape, dt))

    def sem(self, name):
        s = self.nc.alloc_semaphore(f"{self.name}_{name}")
        self.sems.append(s)
        return s

    def __enter__(self):
        return self

    def __exit__(self, *a):
        if a[0] is None:
            self.nc.clear_and_free_semaphores(self.sems)
            self.nc.all_engine_barrier()
        self.stack.close()


class Steps:

    def __init__(self, eng, sem):
        self.eng, self.sem, self.n = eng, sem, 0

    def mark(self, ins):
        self.n += 1
        ins.then_inc(self.sem, 1)

    def wait(self):
        self.eng.wait_ge(self.sem, self.n)

    def done(self, ins):
        self.mark(ins)
        self.wait()

    def restart(self):
        self.wait()
        self.eng.sem_clear(self.sem)
        self.n = 0


def layer_norm_stage(nc, g, name):
    with Stage(nc, name) as st:
        stats = st.sb("stats", [P, NT, 6])
        mv = st.sb("mean_var", [P, NT, 2])
        veps = st.sb("veps", [P, NT])
        rstd = st.sb("rstd", [P, NT])
        hTp = st.ps("hTp", [P, 4, 512])
        stats_done, aggr_done, veps_done = st.sem("stats"), st.sem("aggr"), st.sem("veps")
        rstd_done, h_done, turned = st.sem("rstd"), st.sem("h"), st.sem("turned")

        with nc.Block() as block:
            @block.vector
            def _(dve):
                for c in range(5):
                    if c < 4:
                        for t in range(4 * c, 4 * c + 4):
                            dve.bn_stats(stats[:, t, :], g.x[:, t, :]).then_inc(stats_done, 1)
                        for t in range(4 * c, 4 * c + 4):
                            dve.wait_ge(stats_done, t + 1)
                            dve.bn_aggr(mv[:, t, :], stats[:, t, :]).then_inc(aggr_done, 1)
                    if c >= 1:
                        dve.wait_ge(rstd_done, c)
                        for t in range(4 * c - 4, 4 * c):
                            dve.tensor_scalar(g.h[:, t, :], g.x[:, t, :], mv[:, t, 0:1], rstd[:, t:t + 1],
                                              ALU.subtract, ALU.mult).then_inc(h_done, 1)

            @block.gpsimd
            def _(pool):
                for c in range(4):
                    tiles = slice(4 * c, 4 * c + 4)
                    pool.wait_ge(aggr_done, 4 * c + 4)
                    pool.tensor_scalar(veps[:, tiles], mv[:, tiles, 1], LN_EPS, None, ALU.add).then_inc(veps_done, 1)
                    pool.wait_ge(veps_done, c + 1)
                    pool.tensor_tensor(rstd[:, tiles], veps[:, tiles], g.neg_half[:, tiles], ALU.pow)\
                        .then_inc(rstd_done, 1)

            @block.tensor
            def _(pe):
                for t in range(NT):
                    pe.wait_ge(h_done, t + 1)
                    pe.transpose(hTp[:, t // 4, (t % 4) * P:(t % 4 + 1) * P], g.h[:, t, :],
                                 g.ident[:]).then_inc(turned, 1)

            @block.scalar
            def _(act):
                for c in range(4):
                    act.wait_ge(turned, 4 * c + 4)
                    act.activation(g.hT[:, c * 512:(c + 1) * 512], hTp[:, c, :], ACT.Copy)


class Weights:

    def __init__(self):
        self.at, self.n, self.parts = {}, 0, []

    def add(self, name, a):
        a = np.asarray(a)
        assert a.ndim == 2 and a.shape[0] <= P, (name, a.shape)
        self.at[name] = (self.n, a.shape[1], a.shape[0])
        self.n += a.shape[1]
        self.parts.append(a)

    def packed(self):
        out = np.zeros((P, self.n), self.parts[0].dtype)
        c = 0
        for a in self.parts:
            out[:a.shape[0], c:c + a.shape[1]] = a
            c += a.shape[1]
        return out


def linear_attention_stage(nc, g, name):
    H, HD, HP = 16, 8, 4
    NC = H // HP
    U = B * NC
    SC = T + P
    items = ([("q", 0), ("q", 1), ("k", 0), ("k", 1), ("v", 0)])
    NI = len(items)
    with Stage(nc, name) as st:
        qT = st.sb("qT", [P, 2, NC, T])
        kT = st.sb("kT", [P, 2, NC, T])
        ex = st.sb("ex", [P, 2, 512])
        v = st.sb("v", [P, 2, TT, H, 32])
        sT = st.sb("sT", [P, 2, HP, SC])
        oc = st.sb("oc", [P, 2, T])
        den = st.sb("den", [P, 2, TT, HP])
        o = st.sb("o", [P, 2, TT, D])
        oT = st.sb("oT", [P, 2, T])
        F = st.ps("F", [P, 512])
        S = st.ps("S", [P, HP, 512])
        O = st.ps("O", [P, 512])
        TK = st.ps("TK", [P, 512])
        Wb = st.ps("W", [P, 512])
        (v_ready, f_mm, f_cp, phi, scored, masked, pv, oc_cp, turned, steps, o_norm, t_mm, oT_cp, y_mm, y_add) = [
            st.sem(n) for n in ("v_ready", "f_mm", "f_cp", "phi", "scored", "masked", "pv", "oc_cp", "turned",
                                "steps", "o_norm", "t_mm", "oT_cp", "y_mm", "y_add")]
        weights = {n: g.w("L1b_w" + n) for n in "qkv"}

        def fronts(u):
            b, c = divmod(u, NC)
            if b + 1 >= B:
                return []
            return [(b + 1, k) for k in {0: [0], 1: [1], 2: [2], 3: [3, 4]}[c]]

        with nc.Block() as block:
            @block.gpsimd
            def _(pool):
                pool.memset(v[:], 0.0).then_inc(v_ready, 1)
                pool.wait_ge(v_ready, 1)
                pool.memset(v[:, :, :, :, HD:HD + 1], 1.0).then_inc(v_ready, 1)

            @block.tensor
            def _(pe):
                def front(b, k):
                    what, half = items[k]
                    n = b * NI + k
                    if n:
                        pe.wait_ge(f_cp, n)
                    if what == "v":
                        for t in range(TT):
                            tile = (TT * b + t) * P
                            last = pe.matmul(F[:, t * P:(t + 1) * P], g.hT[:, tile:tile + P], weights["v"],
                                             start=True, stop=True)
                    else:
                        for j in range(2):
                            c = 2 * half + j
                            last = pe.matmul(F[:, j * T:(j + 1) * T], weights[what][:, c * P:(c + 1) * P],
                                             g.hT[:, b * T:(b + 1) * T], start=True, stop=True)
                    last.then_inc(f_mm, 1)

                for k in range(NI):
                    front(0, k)
                for u in range(U + 4):
                    if u < U:
                        b, c = divmod(u, NC)
                        if c == 0:
                            pe.wait_ge(phi, 4 * (b + 1))
                        if u:
                            pe.wait_ge(masked, u)
                        for t in range(TT):
                            for h in range(HP):
                                rows = slice(32 * h, 32 * h + HD)
                                last = pe.matmul(S[:, h, t * T:t * T + T - t * P], kT[rows, b % 2, c, t * P:(t + 1) * P],
                                                 qT[rows, b % 2, c, t * P:T], start=True, stop=True,
                                                 tile_position=(32 * h, 0))
                        last.then_inc(scored, 1)
                        for fb, k in fronts(u):
                            front(fb, k)
                    j = u - 1
                    if 0 <= j < U:
                        b, c = divmod(j, NC)
                        pe.wait_ge(masked, j + 1)
                        if c == 0:
                            pe.wait_ge(f_cp, NI * (b + 1))
                        if j:
                            pe.wait_ge(oc_cp, j)
                        for t in range(TT):
                            for h in range(HP):
                                last = pe.matmul(O[32 * h:32 * (h + 1), t * P:T], v[:, b % 2, t, HP * c + h, :],
                                                 sT[:, j % 2, h, t * T:t * T + T - t * P], start=(t == 0),
                                                 stop=(t == TT - 1), skip_group_check=True,
                                                 tile_position=(0, 32 * h))
                        last.then_inc(pv, 1)
                    j = u - 2
                    if 0 <= j < U:
                        pe.wait_ge(oc_cp, j + 1)
                        if j:
                            pe.wait_ge(o_norm, j)
                        for t in range(TT):
                            last = pe.transpose(TK[:, t * P:(t + 1) * P], oc[:, j % 2, t * P:(t + 1) * P], g.ident[:])
                        last.then_inc(turned, 1)
                    j = u - 3
                    if 0 <= j < U and j % NC == NC - 1:
                        b = j // NC
                        pe.wait_ge(o_norm, j + 1)
                        if b:
                            pe.wait_ge(y_add, b)
                        for t in range(TT):
                            last = pe.transpose(Wb[:, t * P:(t + 1) * P], o[:, b % 2, t, :], g.ident[:])
                        last.then_inc(t_mm, 1)
                    j = u - 4
                    if 0 <= j < U and j % NC == NC - 1:
                        b = j // NC
                        pe.wait_ge(oT_cp, b + 1)
                        for t in range(TT):
                            last = pe.matmul(Wb[:, t * P:(t + 1) * P], oT[:, b % 2, t * P:(t + 1) * P],
                                             g.w("L1b_wo"), start=True, stop=True)
                        last.then_inc(y_mm, 1)

            @block.scalar
            def _(act):
                def front(b, k):
                    what, half = items[k]
                    n = b * NI + k
                    act.wait_ge(f_mm, n + 1)
                    if what == "v":
                        if b == 0:
                            act.wait_ge(v_ready, 2)
                        if b >= 2:
                            act.wait_ge(pv, NC * (b - 1))
                        act.activation(v[:, b % 2, :, :, 0:HD], F[:, 0:T].rearrange("p (t h e) -> p t h e", t=TT, h=H),
                                       ACT.Copy).then_inc(f_cp, 1)
                        return
                    r = 4 * b + k
                    if r >= 2:
                        act.wait_ge(phi, r - 1)
                    to = (qT if what == "q" else kT)[:, b % 2, 2 * half:2 * half + 2, :]
                    act.activation(ex[:, r % 2, :], F[:, :], ACT.Exp)
                    act.activation(to, F[:].rearrange("p (c t) -> p c t", c=2), ACT.Relu).then_inc(f_cp, 1)

                for k in range(NI):
                    front(0, k)
                for u in range(U + 3):
                    if u < U:
                        for fb, k in fronts(u):
                            front(fb, k)
                    j = u - 1
                    if 0 <= j < U:
                        act.wait_ge(pv, j + 1)
                        if j >= 2:
                            act.wait_ge(turned, j - 1)
                        act.activation(oc[:, j % 2, :], O[:, 0:T], ACT.Copy).then_inc(oc_cp, 1)
                    j = u - 3
                    if 0 <= j < U and j % NC == NC - 1:
                        b = j // NC
                        act.wait_ge(t_mm, b + 1)
                        if b >= 2:
                            act.wait_ge(y_mm, b - 1)
                        act.activation(oT[:, b % 2, :], Wb[:, 0:T], ACT.Copy).then_inc(oT_cp, 1)

            @block.vector
            def _(dve):
                d = Steps(dve, steps)

                def front(b, k):
                    what, half = items[k]
                    if what != "v":
                        dve.wait_ge(f_cp, b * NI + k + 1)
                        to = (qT if what == "q" else kT)[:, b % 2, 2 * half:2 * half + 2, :]
                        dve.scalar_tensor_tensor(out=to, in0=ex[:, (4 * b + k) % 2, :].rearrange("p (c t) -> p c t", c=2),
                                                 scalar=1.0, in1=to, op0=ALU.min, op1=ALU.add).then_inc(phi, 1)

                for k in range(NI):
                    front(0, k)
                for u in range(U + 4):
                    if u < U:
                        dve.wait_ge(scored, u + 1)
                        if u >= 2:
                            dve.wait_ge(pv, u - 1)
                        for t in range(TT):
                            n = T - t * P
                            ins = dve.tensor_tensor(sT[:, u % 2, :, t * T:t * T + n], S[:, :, t * T:t * T + n],
                                                    g.causal01[:, 0:n].unsqueeze(1).to_broadcast([P, HP, n]), ALU.mult)
                        ins.then_inc(masked, 1)
                        for fb, k in fronts(u):
                            front(fb, k)
                    j = u - 2
                    if 0 <= j < U:
                        b, c = divmod(j, NC)
                        dve.wait_ge(turned, j + 1)
                        if c == 0 and b >= 2:
                            dve.wait_ge(t_mm, b - 1)
                        tk = TK[:, 0:T].rearrange("p (t h e) -> p t h e", t=TT, h=HP)
                        d.done(dve.tensor_scalar(den[:, j % 2, :, :], tk[:, :, :, HD], 1e-6, None, ALU.add))
                        d.done(dve.reciprocal(den[:, j % 2, :, :], den[:, j % 2, :, :]))
                        dve.tensor_tensor(o[:, b % 2, :, 32 * c:32 * (c + 1)].rearrange("p t (h e) -> p t h e", h=HP),
                                          tk[:, :, :, 0:HD],
                                          den[:, j % 2, :, :].unsqueeze(3).to_broadcast([P, TT, HP, HD]), ALU.mult)\
                           .then_inc(o_norm, 1)
                    j = u - 4
                    if 0 <= j < U and j % NC == NC - 1:
                        b = j // NC
                        dve.wait_ge(y_mm, b + 1)
                        xb = g.x[:, TT * b:TT * b + TT, :]
                        dve.tensor_tensor(xb, xb, Wb[:, 0:T].rearrange("p (t d) -> p t d", t=TT), ALU.add)\
                           .then_inc(y_add, 1)


class AttentionPlan:
    H = 16
    SCORES, NORM, TURN, PV, PROJ, RESID = 7, 6, 4, 3, 2, 1
    NH = 2 * H

    def __init__(self, hd, masked):
        self.hd = hd
        self.HS = 32 if hd <= 32 else 64
        self.HP = P // self.HS
        self.NC = self.H // self.HP
        self.NV = self.H * hd // P
        self.NF = 2 * self.NC + self.NV
        self.per = -(-self.NF // 10)
        self.width = [P, T] if masked else [T, T]

    def head(self, i, offset):
        return i + offset if i + offset >= 0 else None

    def fronts(self, i):
        for rel in (1, 2, 3):
            first = self.H * (rel - 1) - self.PV + 1
            if first <= i < first + 10:
                s0 = (i - first) * self.per
                return [(rel, s) for s in range(s0, min(s0 + self.per, self.NF))]
        return []

    def copies(self, i):
        return {self.H * (rel - 1) - self.PV - 1: rel for rel in (2, 3)}.get(i)

    def steps(self, eng, step):
        for i in range(-self.SCORES, 0):
            step(0, i)
        with eng.Fori(0, B // 2) as pair:
            for i in range(self.NH):
                step(pair, i)


def attention_stage(nc, g, name, W, hd, scale, mask=None):
    a = AttentionPlan(hd, mask is not None)
    H, NH, HS, HP, NC, NF = a.H, a.NH, a.HS, a.HP, a.NC, a.NF
    with Stage(nc, name) as st:
        b = AttentionBuffers(st, a)
        s = b.sems
        with nc.Block() as block:
            @block.gpsimd
            def _(pool):
                attention_pool_setup(pool, b)
                a.steps(pool, lambda pair, i: attention_pool_step(pool, a, b, pair, i))

            @block.tensor
            def _(pe):
                for x in (s.front_mm, s.scored, s.turned, s.pv, s.y_ps):
                    pe.sem_inc(x, HEAD)
                wq, wk, wv, wo = (g.w(W + n) for n in ("wq", "wk", "wv", "wo"))
                bv = g.w(W + "bv") if g.has(W + "bv") else None

                def front(pair, rel, t):
                    if t == 0:
                        pe.wait_ge(s.h_copied, pair * 2 + rel + 1 + HEAD)
                    attention_front_pe(pe, g, a, b, pair, rel, t, wq, wk, wv, bv)

                for t in range(NF):
                    front(0, 0, t)

                def step(pair, i):
                    attention_scores_pe(pe, g, a, b, pair, i, mask)
                    attention_output_pe(pe, g, a, b, pair, i)
                    j = a.head(i, a.PROJ)
                    if j is not None and j % HP == HP - 1:
                        chunk = j // HP
                        pe.wait_ge(s.oT_cp, pair * (2 * NC) + chunk + 1 + HEAD)
                        if chunk % NC == 0:
                            pe.wait_ge(s.resid, pair * 2 + chunk // NC + HEAD)
                        for t in range(TT):
                            last = pe.matmul(b.Y[:, t, :], b.oT[:, chunk % 2, t * P:(t + 1) * P],
                                             wo[:, (chunk % NC) * P:(chunk % NC + 1) * P],
                                             start=(chunk % NC == 0 and t == 0), stop=(chunk % NC == NC - 1),
                                             skip_group_check=True)
                        last.then_inc(s.y_ps, 1)
                    for rel, t in a.fronts(i):
                        front(pair, rel, t)

                a.steps(pe, step)

            @block.scalar
            def _(act):
                for x in (s.front_cp, s.expd, s.oT_cp):
                    act.sem_inc(x, HEAD)
                bq, bk = (g.w(W + n) if g.has(W + n) else None for n in ("bq", "bk"))
                if bq is not None:
                    act.activation(b.bqs[:], bq, ACT.Copy, scale=scale).then_inc(s.bias, 1)
                    act.wait_ge(s.bias, 1)
                    bq = b.bqs
                for t in range(NF):
                    attention_front_act(act, a, b, 0, 0, t, bq, bk, scale)

                def step(pair, i):
                    attention_exp_act(act, a, b, pair, i)
                    for rel, t in a.fronts(i):
                        attention_front_act(act, a, b, pair, rel, t, bq, bk, scale)

                a.steps(act, step)

            @block.vector
            def _(dve):
                for x in (s.maxed, s.recip, s.prT_cp, s.resid, s.h_copied):
                    dve.sem_inc(x, HEAD)

                for n in range(2):
                    attention_copy_h(dve, g, a, b, 0, n, n)

                def step(pair, i):
                    attention_dve_step(dve, a, b, pair, i)
                    if (rel := a.copies(i)) is not None:
                        attention_copy_h(dve, g, a, b, pair, rel, pair * 2 + rel)
                    j = a.head(i, a.RESID)
                    if j is not None and j % H == H - 1:
                        rel = j // H
                        dve.wait_ge(s.y_ps, pair * (2 * NC) + (rel + 1) * NC + HEAD)
                        xb = g.x[:, bass.ds(pair * (2 * TT) + TT * rel, TT), :]
                        ins = dve.tensor_tensor(xb, xb, b.Y[:], ALU.add)
                        if g.has(W + "bo"):
                            ins.then_inc(s.bias_add, 1)
                            dve.wait_ge(s.bias_add, pair * 2 + rel + 1)
                            ins = dve.tensor_tensor(
                                xb, xb, g.w(W + "bo").unsqueeze(1).to_broadcast([P, TT, P]), ALU.add)
                        ins.then_inc(s.resid, 1)

                a.steps(dve, step)


class AttentionSems:

    def __init__(self, st):
        self.h_copied = st.sem("h_copied")
        self.front_mm = st.sem("front_mm")
        self.front_cp = st.sem("front_cp")
        self.scored = st.sem("scored")
        self.maxed = st.sem("maxed")
        self.expd = st.sem("expd")
        self.recip = st.sem("recip")
        self.normed = st.sem("normed")
        self.turned = st.sem("turned")
        self.prT_cp = st.sem("prT_cp")
        self.pv = st.sem("pv")
        self.oT_cp = st.sem("oT_cp")
        self.y_ps = st.sem("y_ps")
        self.resid = st.sem("resid")
        self.bias = st.sem("bias")
        self.bias_add = st.sem("bias_add")
        self.zeroed = st.sem("zeroed")


class AttentionBuffers:
    def __init__(self, st, a):
        self.hTs = st.sb("hTs", [P, 2, T])
        self.qT = st.sb("qT", [P, 2, a.NC, T])
        self.kT = st.sb("kT", [P, 2, a.NC, T])
        self.v = st.sb("v", [P, 2, TT, a.H, a.HS])
        self.bqs = st.sb("bqs", [P, a.NC])
        self.negmax = st.sb("negmax", [P, a.NH, TT])
        self.sums = st.sb("sums", [P, a.NH, TT])
        self.rinv = st.sb("rinv", [P, a.NH, TT])
        self.pr = st.sb("pr", [P, 4, TT, T])
        self.prT = st.sb("prT", [P, 2 * a.HP, 512])
        self.oT = st.sb("oT", [P, 2, T])
        self.S = st.ps("S", [P, 2, 512])
        self.PT = st.ps("PT", [P, 2, 512])
        self.FR = st.ps("FR", [P, 2, 512])
        self.O = st.ps("O", [P, 512])[:, 0:T]
        self.Y = st.ps("Y", [P, 4, P])[:, 0:TT, :]
        self.sems = AttentionSems(st)


def attention_pool_setup(pool, b):
    pool.memset(b.v[:], 0.0).then_inc(b.sems.zeroed, 1)
    pool.memset(b.pr[:], 0.0).then_inc(b.sems.zeroed, 1)
    pool.sem_inc(b.sems.normed, HEAD)


def attention_pool_step(pool, a, b, pair, i):
    s = b.sems
    j = a.head(i, a.NORM)
    if j is None:
        return
    pool.wait_ge(s.recip, pair * a.NH + j + 1 + HEAD)
    p = b.pr[:, j % 4, :, :]
    pool.tensor_tensor(p, p, b.rinv[:, j % a.NH, :].unsqueeze(2).to_broadcast([P, TT, T]), ALU.mult)\
        .then_inc(s.normed, 1)


def attention_front_pe(pe, g, a, b, pair, rel, t, wq, wk, wv, bv, banks=2):
    s = b.sems
    f = a.NF * rel + t
    pe.wait_ge(s.front_cp, pair * (2 * a.NF) + f + 1 - banks + HEAD)
    out = b.FR[:, f % banks, 0:T]
    src = b.hTs[:, rel % 2, :]
    if t < 2 * a.NC:
        w = (wq if t < a.NC else wk)[:, (t % a.NC) * P:(t % a.NC + 1) * P]
        last = pe.matmul(out, w, src, start=True, stop=True)
    else:
        c = slice((t - 2 * a.NC) * P, (t - 2 * a.NC + 1) * P)
        for k in range(TT):
            tile = slice(k * P, (k + 1) * P)
            last = pe.matmul(out[:, tile], src[:, tile], wv[:, c], start=True, stop=bv is None)
            if bv is not None:
                last = pe.matmul(out[:, tile], g.ones[0:1, :], bv[0:1, c], start=False, stop=True)
    last.then_inc(s.front_mm, 1)


def attention_front_act(act, a, b, pair, rel, t, bq, bk, scale, banks=2):
    s = b.sems
    f = a.NF * rel + t
    if t == 0 and rel == 0:
        act.wait_ge(s.zeroed, 2)
    if t == 0 and rel >= 2:
        act.wait_ge(s.pv, pair * (2 * a.NC) + (rel - 1) * a.NC + HEAD)
    act.wait_ge(s.front_mm, pair * (2 * a.NF) + f + 1 + HEAD)
    src = b.FR[:, f % banks, 0:T]
    c = t % a.NC
    if t < a.NC:
        ins = act.activation(b.qT[:, rel % 2, c, :], src, ACT.Identity,
                             bias=bq[:, c:c + 1] if bq is not None else 0.0, scale=scale)
    elif t < 2 * a.NC:
        ins = act.activation(b.kT[:, rel % 2, c, :], src, ACT.Identity,
                             bias=bk[:, c:c + 1] if bk is not None else 0.0)
    else:
        n = P // a.hd
        c = t - 2 * a.NC
        ins = act.activation(b.v[:, rel % 2, :, c * n:(c + 1) * n, 0:a.hd],
                             src.rearrange("p (t h d) -> p t h d", t=TT, h=n), ACT.Copy)
    ins.then_inc(s.front_cp, 1)


def attention_scores_pe(pe, g, a, b, pair, i, mask):
    s = b.sems
    j = a.head(i, a.SCORES)
    if j is None:
        return
    rel, hh = j // a.H, j % a.H
    if hh == 0:
        pe.wait_ge(s.front_cp, pair * (2 * a.NF) + (rel + 1) * a.NF + HEAD)
    pe.wait_ge(s.expd, pair * a.NH + j - 1 + HEAD)
    rows = slice(a.HS * (hh % a.HP), a.HS * (hh % a.HP) + a.hd)
    for t in range(TT):
        n = a.width[t]
        out = b.S[:, j % 2, t * T:t * T + n]
        last = pe.matmul(out, b.qT[rows, rel % 2, hh // a.HP, t * P:(t + 1) * P],
                         b.kT[rows, rel % 2, hh // a.HP, 0:n], start=True, stop=mask is None)
        if mask is not None:
            last = pe.matmul(out, g.ident_bf[:], g.masks[mask][:, t, 0:n], start=False, stop=True)
    last.then_inc(s.scored, 1)


def attention_score_pairs_pe(pe, a, b, pair, i):
    s = b.sems
    j = a.head(i, a.SCORES)
    if j is None or j % 2:
        return
    rel = j // a.H
    if j % a.H == 0:
        pe.wait_ge(s.front_cp, pair * (2 * a.NF) + (rel + 1) * a.NF + HEAD)
    pe.wait_ge(s.expd, pair * a.NH + j + HEAD)
    for t in range(TT):
        for n in (j, j + 1):
            hh = n % a.H
            rows = slice(a.HS * (hh % a.HP), a.HS * (hh % a.HP) + a.hd)
            last = pe.matmul(b.S[:, n % 2, t * T:(t + 1) * T], b.qT[rows, rel % 2, hh // a.HP, t * P:(t + 1) * P],
                             b.kT[rows, rel % 2, hh // a.HP, :], start=True, stop=True)
            if t == TT - 1:
                last.then_inc(s.scored, 1)


def attention_output_pe(pe, g, a, b, pair, i):
    s = b.sems
    j = a.head(i, a.TURN)
    if j is not None:
        n = pair * a.NH + j + HEAD
        pe.wait_ge(s.normed, n + 1)
        pe.wait_ge(s.prT_cp, n - 1)
        for t in range(TT):
            for k in range(a.width[t] // P):
                last = pe.transpose(b.PT[:, j % 2, (2 * k + t) * P:(2 * k + t + 1) * P],
                                    b.pr[:, j % 4, t, k * P:(k + 1) * P], g.ident[:])
        last.then_inc(s.turned, 1)
    j = a.head(i, a.PV)
    if j is not None and j % a.HP == a.HP - 1:
        chunk = j // a.HP
        pe.wait_ge(s.prT_cp, pair * a.NH + j + 1 + HEAD)
        pe.wait_ge(s.oT_cp, pair * (2 * a.NC) + chunk + HEAD)
        for k in range(TT):
            lo = k * P if a.width[0] == P else 0
            for h in range(a.HP):
                jh = j - a.HP + 1 + h
                last = pe.matmul(b.O[a.HS * h:a.HS * (h + 1), lo:T],
                                 b.v[:, (jh // a.H) % 2, k, jh % a.H, :],
                                 b.prT[:, jh % (2 * a.HP), k * T + lo:(k + 1) * T],
                                 start=(k == 0), stop=(k == TT - 1), skip_group_check=True)
        last.then_inc(s.pv, 1)


def attention_exp_act(act, a, b, pair, i):
    s = b.sems
    j = a.head(i, a.SCORES)
    act.wait_ge(s.maxed, pair * a.NH + j + 1 + HEAD)
    act.wait_ge(s.turned, pair * a.NH + j - 3 + HEAD)
    for t in range(TT):
        n = a.width[t]
        ins = act.activation(b.pr[:, j % 4, t, 0:n], b.S[:, j % 2, t * T:t * T + n], ACT.Exp,
                             bias=b.negmax[:, j % a.NH, t:t + 1], accum_out=b.sums[:, j % a.NH, t:t + 1])
    ins.then_inc(s.expd, 1)
    j = a.head(i, a.PV)
    if j is not None and j % a.HP == a.HP - 1:
        chunk = j // a.HP
        act.wait_ge(s.pv, pair * (2 * a.NC) + chunk + 1 + HEAD)
        act.wait_ge(s.y_ps, pair * (2 * a.NC) + chunk - 1 + HEAD)
        act.activation(b.oT[:, chunk % 2, :], b.O, ACT.Copy).then_inc(s.oT_cp, 1)


def attention_copy_h(dve, g, a, b, pair, rel, batch):
    s = b.sems
    if rel >= 2:
        dve.wait_ge(s.front_mm, pair * (2 * a.NF) + (rel - 1) * a.NF + HEAD)
    src = g.hT[:, batch * T:(batch + 1) * T] if isinstance(batch, int) else g.hT[:, bass.ds(batch * T, T)]
    dve.tensor_scalar(b.hTs[:, rel % 2, :], src, 1.0, None, ALU.mult).then_inc(s.h_copied, 1)


def attention_dve_step(dve, a, b, pair, i):
    s = b.sems
    j = a.head(i, a.SCORES)
    dve.wait_ge(s.scored, pair * a.NH + j + 1 + HEAD)
    m = b.negmax[:, j % a.NH, :]
    if a.width[0] == T:
        ins = dve.tensor_reduce(m, b.S[:, j % 2, :].rearrange("p (t k) -> p t k", t=TT), AX_X, ALU.max,
                                negate=True)
    else:
        for t in range(TT):
            ins = dve.tensor_reduce(m[:, t:t + 1], b.S[:, j % 2, t * T:t * T + a.width[t]], AX_X, ALU.max,
                                    negate=True)
    ins.then_inc(s.maxed, 1)
    j = a.head(i, a.NORM)
    if j is not None:
        dve.wait_ge(s.expd, pair * a.NH + j + 1 + HEAD)
        dve.reciprocal(b.rinv[:, j % a.NH, :], b.sums[:, j % a.NH, :]).then_inc(s.recip, 1)
    j = a.head(i, a.TURN)
    if j is not None:
        dve.wait_ge(s.turned, pair * a.NH + j + 1 + HEAD)
        dve.wait_ge(s.pv, pair * (2 * a.NC) + j // a.HP - 1 + HEAD)
        to, of = b.prT[:, j % (2 * a.HP), :], b.PT[:, j % 2, :]
        if a.width[0] == T:
            dve.tensor_copy(to, of).then_inc(s.prT_cp, 1)
        else:
            dve.tensor_copy(to[:, 0:2 * P], of[:, 0:2 * P])
            dve.tensor_copy(to[:, 3 * P:4 * P], of[:, 3 * P:4 * P]).then_inc(s.prT_cp, 1)


class EncoderPlan(AttentionPlan):
    K = 9
    SCORES, NORM, TURN, PV, PROJ = (7 + K, 6 + K, 4 + K, 3 + K, 2 + K)
    LN1, POW1, NORM1, AFFINE1, X1T, FF1, FF2, LN2, POW2, NORM2 = (K + 1, K, K - 1, K - 2, K - 3, K - 4,
                                                                  K - 6, K - 7, K - 8, K - 9)
    E, DFF = 4, 512

    def ends(self, i, offset):
        j = self.head(i, offset)
        return j // self.H if j is not None and j % self.H == self.H - 1 else None

    def steps(self, eng, step):
        for i in range(-self.SCORES, 0):
            step(0, i)
        with eng.Fori(0, B) as pair:
            for i in range(self.NH):
                step(pair, i)


ENC_A = ["wq", "wk", "wv", "bq", "bk", "bv"]
ENC_B = ["wo", "w1", "w2", "b1", "ob", "b2", "n1w", "n1b", "n2w", "n2b"]


def expert_gates(nc, g, name, gates, experts):
    E = EncoderPlan.E
    with Stage(nc, name) as st:
        hsum = st.sb("hsum", [P, B])
        z = st.sb("z", [B, 4, E])
        onehot = st.sb("onehot", [B, 2, E])
        cand = st.sb("cand", [B, E])
        small = st.sb("small", [B, 8])
        picked = st.sb("picked", [B, 2])
        gk = st.sb("gk", [B, 2])
        spread = st.sb("spread", [B, B, 2])
        expert_i = st.sb("expert_i", [B, 2], mybir.dt.int32)
        psg = st.ps("psg", [P, 512])
        psb = st.ps("psb", [P, 512])
        steps_done, summed, logits, expd, spread_done, gates_ps, numbers, moved, zeroed = [
            st.sem(n) for n in ("steps", "summed", "logits", "expd", "spread", "gates_ps", "numbers", "moved",
                                "zeroed")]
        lg, ex, gate, masked = (z[:, n, :] for n in range(4))
        iota = g.w("enc_iota")

        with nc.Block() as block:
            @block.vector
            def _(dve):
                d = Steps(dve, steps_done)
                dve.tensor_reduce(hsum[:], g.hT[:, 0:NTOK].rearrange("p (b t) -> p b t", b=B), AX_X, ALU.add)\
                    .then_inc(summed, 1)
                dve.wait_ge(logits, 1)
                d.done(dve.tensor_scalar(lg, psg[0:B, 0:E], 1.0 / T, None, ALU.mult))
                d.done(dve.tensor_tensor(lg, lg, g.w("enc_gate_b"), ALU.add))
                d.done(dve.tensor_reduce(small[:, 0:1], lg, AX_X, ALU.max))
                dve.tensor_scalar(small[:, 1:2], small[:, 0:1], -1.0, None, ALU.mult).then_inc(summed, 1)
                dve.wait_ge(expd, 1)
                d.done(dve.reciprocal(small[:, 3:4], small[:, 2:3]))
                d.done(dve.tensor_scalar(gate, ex, small[:, 3:4], None, ALU.mult))
                d.done(dve.tensor_copy(masked, lg))
                for k in range(2):
                    d.done(dve.tensor_reduce(small[:, 4:5], masked, AX_X, ALU.max))
                    d.done(dve.tensor_scalar(cand[:], masked, small[:, 4:5], float(E), ALU.is_lt, ALU.mult))
                    d.done(dve.tensor_tensor(cand[:], cand[:], iota, ALU.add))
                    d.done(dve.tensor_reduce(picked[:, k:k + 1], cand[:], AX_X, ALU.min))
                    d.done(dve.tensor_scalar(onehot[:, k, :], iota, picked[:, k:k + 1], None, ALU.is_equal))
                    if k == 0:
                        d.done(dve.scalar_tensor_tensor(out=masked, in0=onehot[:, 0, :], scalar=NEG, in1=masked,
                                                        op0=ALU.mult, op1=ALU.add))
                d.done(dve.tensor_tensor(onehot[:], onehot[:], gate.unsqueeze(1).to_broadcast([B, 2, E]),
                                         ALU.mult))
                d.done(dve.tensor_reduce(gk[:], onehot[:], AX_X, ALU.add))
                dve.tensor_tensor(spread[:], g.ident[0:B, 0:B].unsqueeze(2).to_broadcast([B, B, 2]),
                                  gk[:].unsqueeze(1).to_broadcast([B, B, 2]), ALU.mult).then_inc(spread_done, 1)
                dve.tensor_copy(expert_i[:], picked[:]).then_inc(numbers, 1)
                dve.wait_ge(gates_ps, 1)
                dve.tensor_copy(gates[:, 0:2 * B], psb[:, 0:2 * B])

            @block.tensor
            def _(pe):
                pe.wait_ge(summed, 1)
                pe.matmul(psg[0:B, 0:E], hsum[:], g.w("enc_gate_w"), start=True, stop=True).then_inc(logits, 1)
                pe.wait_ge(spread_done, 1)
                pe.matmul(psb[:, 0:2 * B], g.ones[0:B, :], spread[:].rearrange("p b k -> p (b k)"),
                          start=True, stop=True).then_inc(gates_ps, 1)

            @block.scalar
            def _(act):
                act.wait_ge(summed, 2)
                act.activation(ex, lg, ACT.Exp, bias=small[:, 1:2], accum_out=small[:, 2:3]).then_inc(expd, 1)

            @block.gpsimd
            def _(pool):
                pool.memset(experts[:], 0).then_inc(zeroed, 1)

            @block.sync
            def _(sp):
                sp.wait_ge(numbers, 1)
                sp.wait_ge(zeroed, 1)
                sp.dma_start(experts[0:1, 0:2 * B], expert_i[:]).then_inc(moved, 16)
                sp.wait_ge(moved, 16)


def encoder_stage(nc, g, name):
    a = EncoderPlan(8, False)
    H, NH, HP, NC, NF = a.H, a.NH, a.HP, a.NC, a.NF
    scale = a.hd ** -0.5
    with Stage(nc, name) as st:
        gates = st.sb("gates", [P, 2 * B])
        experts = st.sb("experts", [1, 2 * B + 4], mybir.dt.int32)
        expert_gates(nc, g, name + "g", gates, experts)
        b = AttentionBuffers(st, a)
        s = b.sems
        b.gates, b.experts = gates, experts
        atA, nA, atB, nB = g.enc_layout
        wA = st.sb("wA", [P, 2, nA])
        wB = st.sb("wB", [P, 2, nB])
        r = st.sb("r", [P, 2, TT, D])
        stats = st.sb("stats", [P, 2, TT, 6])
        mv = st.sb("mv", [P, 2, TT, 2])
        veps = st.sb("veps", [P, 2, TT])
        rstd = st.sb("rstd", [P, 2, TT])
        x1 = st.sb("x1", [P, TT, D])
        x1b = st.sb("x1b", [P, TT, D])
        x1T = st.sb("x1T", [P, T])
        hid = st.sb("hid", [P, 4, T])
        TL = b.FR[:, 1, 0:T]
        (tl_mm, tl_cp, var_ready, rstd_ready, x1_norm, x1_ready, dve_steps, pool_steps, a_in, b_in, unit_done) = [
            st.sem(n) for n in ("tl_mm", "tl_cp", "var", "rstd", "x1_norm", "x1_ready", "dve_steps",
                                "pool_steps", "a_in0", "b_in0", "unit_done")]
        a_in, b_in = [a_in, st.sem("a_in1")], [b_in, st.sem("b_in1")]
        NT_ = 6

        def part(par, key):
            at, w = (atA, wA) if key in atA else (atB, wB)
            c, n, rows = at[key]
            return w[0:rows, par, c:c + n]

        with nc.Block() as block:
            @block.sync
            def _(sp):
                def expert(pair, rel):
                    return sp.value_load(b.experts[0:1, bass.ds(pair * 2 + rel, 1)], min_val=0, max_val=a.E - 1)

                def load(e, rel, group):
                    if group == "a":
                        sp.dma_start(wA[:, rel % 2, :], g.a["enc_a"][bass.ds(e, 1), :, :]
                                     .rearrange("e p n -> p (e n)")).then_inc(a_in[rel % 2], 16)
                    else:
                        sp.dma_start(wB[:, rel % 2, :], g.a["enc_b"][bass.ds(e, 1), :, :]
                                     .rearrange("e p n -> p (e n)")).then_inc(b_in[rel % 2], 16)

                for rel in range(2):
                    e = expert(0, rel)
                    load(e, rel, "a")
                    load(e, rel, "b")
                with sp.Fori(0, B) as pair:
                    for rel in (2, 3):
                        e = expert(pair, rel)
                        sp.wait_ge(s.front_cp, pair * (2 * NF) + (rel - 1) * NF + HEAD)
                        load(e, rel, "a")
                        sp.wait_ge(unit_done, pair * 2 + rel - 1)
                        load(e, rel, "b")
                for x in a_in + b_in:
                    sp.wait_ge(x, 16 * (B + 1))

            @block.gpsimd
            def _(pool):
                attention_pool_setup(pool, b)
                pool.sem_inc(rstd_ready, HEAD)
                ps = Steps(pool, pool_steps)

                def power(pair, rel, n):
                    pool.wait_ge(var_ready, pair * 4 + rel * 2 + n + 1)
                    ps.done(pool.tensor_tensor(veps[:, n, :], mv[:, n, :, 1], g.eps[:, 0:TT], ALU.add))
                    pool.tensor_tensor(rstd[:, n, :], veps[:, n, :], g.neg_half[:, 0:TT], ALU.pow)\
                        .then_inc(rstd_ready, 1)

                def step(pair, i):
                    attention_pool_step(pool, a, b, pair, i)
                    if (rel := a.ends(i, a.POW1)) is not None:
                        power(pair, rel, 0)
                    if (rel := a.ends(i, a.AFFINE1)) is not None:
                        pool.wait_ge(x1_norm, pair * 2 + rel + 1)
                        for key, op in (("n1w", ALU.mult), ("n1b", ALU.add)):
                            ps.mark(pool.tensor_tensor(x1[:], x1[:], part(rel % 2, key).unsqueeze(1)
                                                       .to_broadcast([P, TT, D]), op))
                            ps.wait()
                        pool.tensor_tensor(x1b[:], x1[:], part(rel % 2, "b2").unsqueeze(1)
                                           .to_broadcast([P, TT, D]), ALU.add).then_inc(x1_ready, 1)
                    if (rel := a.ends(i, a.POW2)) is not None:
                        power(pair, rel, 1)
                    if i == NH - 1:
                        ps.restart()

                a.steps(pool, step)

            @block.tensor
            def _(pe):
                for x in (s.front_mm, s.scored, s.turned, s.pv, s.y_ps, tl_mm):
                    pe.sem_inc(x, HEAD)

                def front(pair, rel, t):
                    if t == 0:
                        pe.wait_ge(s.h_copied, pair * 2 + rel + 1 + HEAD)
                        pe.wait_ge(a_in[rel % 2], pair * 16 + 16 * (rel // 2 + 1))
                    par = rel % 2
                    attention_front_pe(pe, g, a, b, pair, rel, t, part(par, "wq"), part(par, "wk"),
                                       part(par, "wv"), part(par, "bv"), banks=1)

                def tail(pair, rel, t):
                    n = pair * (2 * NT_) + rel * NT_ + t + HEAD
                    pe.wait_ge(tl_cp, n)
                    par = rel % 2
                    if t == 0:
                        pe.wait_ge(x1_ready, pair * 2 + rel + 1)
                        for k in range(TT):
                            last = pe.transpose(TL[:, k * P:(k + 1) * P], x1[:, k, :], g.ident[:])
                    elif t < 5:
                        last = pe.matmul(TL, part(par, "w1")[:, (t - 1) * P:t * P], x1T[:], start=True, stop=True)
                    else:
                        for k in range(TT):
                            for c in range(4):
                                last = pe.matmul(TL[:, k * P:(k + 1) * P], hid[:, c, k * P:(k + 1) * P],
                                                 part(par, "w2")[:, c * P:(c + 1) * P],
                                                 start=(c == 0), stop=(c == 3))
                    last.then_inc(tl_mm, 1)

                for t in range(NF):
                    front(0, 0, t)

                def step(pair, i):
                    attention_score_pairs_pe(pe, a, b, pair, i)
                    attention_output_pe(pe, g, a, b, pair, i)
                    j = a.head(i, a.PROJ)
                    if j is not None and j % HP == HP - 1:
                        chunk = j // HP
                        pe.wait_ge(s.oT_cp, pair * (2 * NC) + chunk + 1 + HEAD)
                        if chunk % NC == 0:
                            pe.wait_ge(s.resid, pair * 2 + chunk // NC + HEAD)
                            rel = chunk // NC
                            pe.wait_ge(b_in[rel % 2], pair * 16 + 16 * (rel // 2 + 1))
                        for t in range(TT):
                            last = pe.matmul(b.Y[:, t, :], b.oT[:, chunk % 2, t * P:(t + 1) * P],
                                             part((chunk // NC) % 2, "wo")[:, (chunk % NC) * P:(chunk % NC + 1) * P],
                                             start=(chunk % NC == 0 and t == 0), stop=(chunk % NC == NC - 1),
                                             skip_group_check=True)
                        last.then_inc(s.y_ps, 1)
                    for rel, t in a.fronts(i):
                        front(pair, rel, t)
                    for off, ts in ((a.X1T, [0]), (a.FF1, [1, 2]), (a.FF1 - 1, [3, 4]), (a.FF2, [5])):
                        if (rel := a.ends(i, off)) is not None:
                            for t in ts:
                                tail(pair, rel, t)

                a.steps(pe, step)

            @block.scalar
            def _(act):
                for x in (s.front_cp, s.expd, s.oT_cp, tl_cp):
                    act.sem_inc(x, HEAD)

                def front(pair, rel, t):
                    if t == 0:
                        act.wait_ge(a_in[rel % 2], pair * 16 + 16 * (rel // 2 + 1))
                        act.activation(b.bqs[:], part(rel % 2, "bq"), ACT.Copy, scale=scale).then_inc(s.bias, 1)
                        act.wait_ge(s.bias, pair * 2 + rel + 1)
                    attention_front_act(act, a, b, pair, rel, t, b.bqs, part(rel % 2, "bk"), scale, banks=1)

                def tail(pair, rel, t):
                    n = pair * (2 * NT_) + rel * NT_ + t + HEAD
                    act.wait_ge(tl_mm, n + 1)
                    if t == 0:
                        act.activation(x1T[:], TL, ACT.Copy).then_inc(tl_cp, 1)
                    else:
                        act.activation(hid[:, t - 1, :], TL, ACT.Relu,
                                       bias=part(rel % 2, "b1")[:, t - 1:t]).then_inc(tl_cp, 1)

                for t in range(NF):
                    front(0, 0, t)

                def step(pair, i):
                    attention_exp_act(act, a, b, pair, i)
                    for rel, t in a.fronts(i):
                        front(pair, rel, t)
                    for off, ts in ((a.X1T, [0]), (a.FF1, [1, 2]), (a.FF1 - 1, [3, 4])):
                        if (rel := a.ends(i, off)) is not None:
                            for t in ts:
                                tail(pair, rel, t)

                a.steps(act, step)

            @block.vector
            def _(dve):
                for x in (s.maxed, s.recip, s.prT_cp, s.resid, s.h_copied):
                    dve.sem_inc(x, HEAD)
                d = Steps(dve, dve_steps)
                attention_copy_h(dve, g, a, b, 0, 0, 0)
                attention_copy_h(dve, g, a, b, 0, 1, 0)

                def moments(n):
                    for t in range(TT):
                        d.mark(dve.bn_stats(stats[:, n, t, :], r[:, n, t, :]))
                    for t in range(TT):
                        d.wait()
                        ins = dve.bn_aggr(mv[:, n, t, :], stats[:, n, t, :])
                    ins.then_inc(var_ready, 1)

                def step(pair, i):
                    attention_dve_step(dve, a, b, pair, i)
                    if (rel := a.copies(i)) is not None:
                        attention_copy_h(dve, g, a, b, pair, rel, pair + rel // 2)
                    if (rel := a.ends(i, a.LN1)) is not None:
                        dve.wait_ge(s.y_ps, pair * (2 * NC) + (rel + 1) * NC + HEAD)
                        dve.tensor_tensor(r[:, 0, :, :], b.Y, g.h[:, bass.ds(pair * TT, TT), :], ALU.add)\
                           .then_inc(s.resid, 1)
                        dve.wait_ge(s.resid, pair * 2 + rel + 1 + HEAD)
                        d.done(dve.tensor_tensor(r[:, 0, :, :], r[:, 0, :, :], part(rel % 2, "ob").unsqueeze(1)
                                                 .to_broadcast([P, TT, D]), ALU.add))
                        moments(0)
                    if (rel := a.ends(i, a.NORM1)) is not None:
                        dve.wait_ge(rstd_ready, pair * 4 + rel * 2 + 1 + HEAD)
                        for t in range(TT):
                            ins = dve.tensor_scalar(x1[:, t, :], r[:, 0, t, :], mv[:, 0, t, 0:1],
                                                    rstd[:, 0, t:t + 1], ALU.subtract, ALU.mult)
                        ins.then_inc(x1_norm, 1)
                    if (rel := a.ends(i, a.LN2)) is not None:
                        dve.wait_ge(tl_mm, pair * (2 * NT_) + (rel + 1) * NT_ + HEAD)
                        ins = dve.tensor_tensor(r[:, 1, :, :], TL.rearrange("p (t n) -> p t n", t=TT), x1b[:],
                                                ALU.add)
                        d.done(ins)
                        dve.sem_inc(tl_cp, 1)
                        moments(1)
                    if (rel := a.ends(i, a.NORM2)) is not None:
                        dve.wait_ge(rstd_ready, pair * 4 + rel * 2 + 2 + HEAD)
                        for t in range(TT):
                            d.mark(dve.tensor_scalar(r[:, 1, t, :], r[:, 1, t, :], mv[:, 1, t, 0:1],
                                                     rstd[:, 1, t:t + 1], ALU.subtract, ALU.mult))
                        d.wait()
                        gate = b.gates[:, bass.ds(pair * 2 + rel, 1)]
                        xb = g.x[:, bass.ds(pair * TT, TT), :]
                        both = lambda key: part(rel % 2, key).unsqueeze(1).to_broadcast([P, TT, D])
                        d.done(dve.tensor_tensor(r[:, 1, :, :], r[:, 1, :, :], both("n2w"), ALU.mult))
                        d.done(dve.tensor_tensor(r[:, 1, :, :], r[:, 1, :, :], both("n2b"), ALU.add))
                        d.done(dve.scalar_tensor_tensor(out=xb, in0=r[:, 1, :, :], scalar=gate, in1=xb,
                                                        op0=ALU.mult, op1=ALU.add))
                        dve.sem_inc(unit_done, 1)
                    if i == NH - 1:
                        d.restart()

                a.steps(dve, step)


def channel_mix_stage(nc, g, name):
    C = 512
    with Stage(nc, name) as st:
        d = st.sb("d", [P, 2, C])
        mum1 = st.sb("mum1", [P, 2])
        xk = st.sb("xk", [P, 4, C])
        xr = st.sb("xr", [P, 4, C])
        ka = st.sb("ka", [P, 4, C])
        sg = st.sb("sg", [P, 2, C])
        prod = st.sb("prod", [P, 2, C])
        KP, RP, VP = (st.ps(n, [P, 2, C]) for n in ("KP", "RP", "VP"))
        (mu_ready, diff, mixed_k, mixed_r, k_mm, relu, squared, r_mm, v_mm, sig, multiplied, added) = [
            st.sem(n) for n in ("mu_ready", "diff", "mixed_k", "mixed_r", "k_mm", "relu", "squared", "r_mm",
                                "v_mm", "sig", "multiplied", "added")]

        with nc.Block() as block:
            @block.vector
            def _(dve):
                dve.tensor_scalar(mum1[:], g.w("L1f_mu"), 1.0, None, ALU.subtract).then_inc(mu_ready, 1)
                dve.wait_ge(mu_ready, 1)
                for c in range(4):
                    h = g.hT[:, c * C:(c + 1) * C].rearrange("p (b t) -> p b t", b=2)
                    dd = d[:, c % 2, :].rearrange("p (b t) -> p b t", b=2)
                    dve.tensor_copy(dd[:, :, 0:1], h[:, :, 0:1]).then_inc(diff, 1)
                    dve.tensor_tensor(dd[:, :, 1:], h[:, :, 1:], h[:, :, 0:T - 1], ALU.subtract).then_inc(diff, 1)
                    dve.wait_ge(diff, 2 * c + 2)
                    for n, to, sem in ((1, xk, mixed_k), (0, xr, mixed_r)):
                        dve.scalar_tensor_tensor(out=to[:, c, :], in0=d[:, c % 2, :], scalar=mum1[:, n:n + 1],
                                                 in1=g.hT[:, c * C:(c + 1) * C], op0=ALU.mult, op1=ALU.add)\
                           .then_inc(sem, 1)
                for c in range(4):
                    dve.wait_ge(sig, c + 1)
                    dve.wait_ge(v_mm, c + 1)
                    if c >= 2:
                        dve.wait_ge(added, c - 1)
                    dve.tensor_tensor(prod[:, c % 2, :], VP[:, c % 2, :], sg[:, c % 2, :], ALU.mult)\
                       .then_inc(multiplied, 1)
                    dve.wait_ge(multiplied, c + 1)
                    xc = g.x[:, 4 * c:4 * c + 4, :]
                    dve.tensor_tensor(xc, xc, prod[:, c % 2, :].rearrange("p (t n) -> p t n", t=4), ALU.add)\
                       .then_inc(added, 1)

            @block.tensor
            def _(pe):
                def rows(c, to, src, w, sem):
                    for t in range(4):
                        last = pe.matmul(to[:, c % 2, t * P:(t + 1) * P], src[:, c, t * P:(t + 1) * P], g.w(w),
                                         start=True, stop=True)
                    last.then_inc(sem, 1)

                for c in range(5):
                    if c < 4:
                        pe.wait_ge(mixed_k, c + 1)
                        if c >= 2:
                            pe.wait_ge(relu, c - 1)
                        pe.matmul(KP[:, c % 2, :], g.w("L1f_wk"), xk[:, c, :], start=True, stop=True)\
                          .then_inc(k_mm, 1)
                        pe.wait_ge(mixed_r, c + 1)
                        if c >= 2:
                            pe.wait_ge(sig, c - 1)
                        rows(c, RP, xr, "L1f_wr", r_mm)
                    if c >= 1:
                        pe.wait_ge(squared, c)
                        if c >= 3:
                            pe.wait_ge(multiplied, c - 2)
                        rows(c - 1, VP, ka, "L1f_wv", v_mm)

            @block.scalar
            def _(act):
                for c in range(4):
                    act.wait_ge(k_mm, c + 1)
                    act.activation(ka[:, c, :], KP[:, c % 2, :], ACT.Relu).then_inc(relu, 1)
                    act.wait_ge(r_mm, c + 1)
                    if c >= 2:
                        act.wait_ge(multiplied, c - 1)
                    act.activation(sg[:, c % 2, :], RP[:, c % 2, :], ACT.Sigmoid).then_inc(sig, 1)

            @block.gpsimd
            def _(pool):
                for c in range(4):
                    pool.wait_ge(relu, c + 1)
                    pool.tensor_tensor(ka[:, c, :], ka[:, c, :], ka[:, c, :], ALU.mult).then_inc(squared, 1)


def kernel_attention_stage(nc, g, name):
    C = 512
    H, HD = 16, 8
    inv = HD ** -0.5
    with Stage(nc, name) as st:
        qk = st.sb("qk", [P, 2, NTOK])
        sq = st.sb("sq", [P, 2, NTOK])
        v = st.sb("v", [P, NT, D])
        qf = st.sb("qf", [P, NTOK])
        kf = st.sb("kf", [P, NT, D])
        kv = st.sb("kv", [P, B, D + H])
        bqk = st.sb("bqk", [P, 2])
        den = st.sb("den", [P, NT, H])
        rden = st.sb("rden", [P, NT, H])
        o = st.sb("o", [P, NT, D])
        oT = st.sb("oT", [P, 2, C])
        A = st.ps("A", [P, 2, C])
        Fp = st.ps("Fp", [P, 2, C])
        KV = st.ps("KV", [P, C])
        O = st.ps("O", [P, 2, C])
        Y = st.ps("Y", [P, C])
        (b_ready, a_mm, a_cp, a_sq, f_mm, f_exp, kv_mm, kv_masked, o_mm, den_ready, o_norm, t_mm, t_cp,
         y_mm, y_add, steps_done) = [st.sem(n) for n in (
             "b_ready", "a_mm", "a_cp", "a_sq", "f_mm", "f_exp", "kv_mm", "kv_masked", "o_mm", "den_ready",
             "o_norm", "t_mm", "t_cp", "y_mm", "y_add", "steps")]
        wqk, wv, wo, rblk, nhalf = (g.w("L2a_" + n) for n in ("wqk", "wv", "wo", "rblk", "nhalf"))

        with nc.Block() as block:
            @block.tensor
            def _(pe):
                def project(n):
                    if n >= 2:
                        pe.wait_ge(a_cp, n - 1)
                    c = n % 4
                    if n < 8:
                        last = pe.matmul(A[:, n % 2, :], wqk[:, (n // 4) * P:(n // 4 + 1) * P],
                                         g.hT[:, c * C:(c + 1) * C], start=True, stop=True)
                    else:
                        for t in range(4):
                            tile = slice((4 * c + t) * P, (4 * c + t + 1) * P)
                            pe.matmul(A[:, n % 2, t * P:(t + 1) * P], g.hT[:, tile], wv, start=True, stop=False)
                            last = pe.matmul(A[:, n % 2, t * P:(t + 1) * P], g.ones[0:1, :], g.w("L2a_bv"),
                                             start=False, stop=True)
                    last.then_inc(a_mm, 1)

                def features(n):
                    pe.wait_ge(a_sq, n + 1)
                    if n >= 2:
                        pe.wait_ge(f_exp, n - 1)
                    c = n % 4
                    if n < 4:
                        cols = slice(c * C, (c + 1) * C)
                        pe.matmul(Fp[:, n % 2, :], rblk, qk[:, 0, cols], start=True, stop=False)
                        last = pe.matmul(Fp[:, n % 2, :], nhalf, sq[:, 0, cols], start=False, stop=True)
                    else:
                        for t in range(4):
                            cols = slice((4 * c + t) * P, (4 * c + t + 1) * P)
                            pe.matmul(Fp[:, n % 2, t * P:(t + 1) * P], qk[:, 1, cols], rblk, start=True, stop=False)
                            last = pe.matmul(Fp[:, n % 2, t * P:(t + 1) * P], sq[:, 1, cols], nhalf,
                                             start=False, stop=True)
                    last.then_inc(f_mm, 1)

                for n in range(12):
                    project(n)
                    if n >= 2 and n - 2 < 8:
                        features(n - 2)
                pe.wait_ge(a_cp, 12)
                for c in range(4):
                    pe.wait_ge(f_exp, 4 + c + 1)
                    if c > 0:
                        pe.wait_ge(kv_masked, c)
                    for b in (2 * c, 2 * c + 1):
                        for t in range(TT):
                            last = pe.matmul(KV[:, (b % 2) * P:(b % 2 + 1) * P], kf[:, TT * b + t, :],
                                             v[:, TT * b + t, :], start=(t == 0), stop=(t == TT - 1))
                    last.then_inc(kv_mm, 1)
                for c in range(8 + 2):
                    if c < 8:
                        if c % 2 == 0:
                            pe.wait_ge(kv_masked, c // 2 + 1)
                        if c >= 2:
                            pe.wait_ge(o_norm, c - 1)
                        for t in range(TT):
                            tile = slice((TT * c + t) * P, (TT * c + t + 1) * P)
                            last = pe.matmul(O[:, c % 2, t * (D + H):(t + 1) * (D + H)], qf[:, tile], kv[:, c, :],
                                             start=True, stop=True)
                        last.then_inc(o_mm, 1)
                    j = c - 1
                    if 0 <= j < 8:
                        pe.wait_ge(o_norm, j + 1)
                        if j >= 2:
                            pe.wait_ge(t_cp, j - 1)
                        for t in range(TT):
                            last = pe.transpose(A[:, j % 2, t * P:(t + 1) * P], o[:, TT * j + t, :], g.ident[:])
                        last.then_inc(t_mm, 1)
                    j = c - 2
                    if 0 <= j < 8:
                        pe.wait_ge(t_cp, j + 1)
                        if j >= 1:
                            pe.wait_ge(y_add, j)
                        for t in range(TT):
                            last = pe.matmul(Y[:, t * P:(t + 1) * P], oT[:, j % 2, t * P:(t + 1) * P], wo,
                                             start=True, stop=True)
                        last.then_inc(y_mm, 1)

            @block.scalar
            def _(act):
                act.activation(bqk[:], g.w("L2a_bqk"), ACT.Copy, scale=inv).then_inc(b_ready, 1)
                act.wait_ge(b_ready, 1)

                def exps(n):
                    act.wait_ge(f_mm, n + 1)
                    c = n % 4
                    out = qf[:, c * C:(c + 1) * C] if n < 4 else kf[:, 4 * c:4 * c + 4, :]
                    src = Fp[:, n % 2, :] if n < 4 else Fp[:, n % 2, :].rearrange("p (t n) -> p t n", t=4)
                    act.activation(out, src, ACT.Exp).then_inc(f_exp, 1)

                for n in range(12):
                    act.wait_ge(a_mm, n + 1)
                    c = n % 4
                    if n < 8:
                        act.activation(qk[:, n // 4, c * C:(c + 1) * C], A[:, n % 2, :], ACT.Identity,
                                       bias=bqk[:, n // 4:n // 4 + 1], scale=inv).then_inc(a_cp, 1)
                    else:
                        act.activation(v[:, 4 * c:4 * c + 4, :], A[:, n % 2, :].rearrange("p (t n) -> p t n", t=4),
                                       ACT.Copy).then_inc(a_cp, 1)
                    if n >= 2 and n - 2 < 8:
                        exps(n - 2)
                for j in range(8):
                    act.wait_ge(t_mm, j + 1)
                    if j >= 2:
                        act.wait_ge(y_mm, j - 1)
                    act.activation(oT[:, j % 2, 0:T], A[:, j % 2, 0:T], ACT.Copy).then_inc(t_cp, 1)

            @block.vector
            def _(dve):
                d = Steps(dve, steps_done)
                d.done(dve.tensor_copy(kv[:, :, D:], g.w("L2a_headof").unsqueeze(1).to_broadcast([P, B, H])))
                for n in range(8):
                    dve.wait_ge(a_cp, n + 1)
                    cols = slice((n % 4) * C, (n % 4 + 1) * C)
                    dve.tensor_tensor(sq[:, n // 4, cols], qk[:, n // 4, cols], qk[:, n // 4, cols], ALU.mult)\
                       .then_inc(a_sq, 1)
                for c in range(4):
                    dve.wait_ge(kv_mm, c + 1)
                    dve.tensor_tensor(kv[:, 2 * c:2 * c + 2, 0:D],
                                      KV[:, 0:T].rearrange("p (b n) -> p b n", b=2),
                                      g.w("L2a_blocks").unsqueeze(1).to_broadcast([P, 2, D]), ALU.mult)\
                       .then_inc(kv_masked, 1)

                def outputs(j):
                    dve.wait_ge(o_mm, j + 1)
                    po = O[:, j % 2, 0:TT * (D + H)].rearrange("p (t n) -> p t n", t=TT)
                    tiles = slice(TT * j, TT * j + TT)
                    d.done(dve.tensor_scalar(den[:, tiles, :], po[:, :, D:], 1e-8, None, ALU.add))
                    d.done(dve.reciprocal(rden[:, tiles, :], den[:, tiles, :]))
                    dve.tensor_tensor(o[:, tiles, :].rearrange("p t (h e) -> p t h e", h=H),
                                      po[:, :, 0:D].rearrange("p t (h e) -> p t h e", h=H),
                                      rden[:, tiles, :].unsqueeze(3).to_broadcast([P, TT, H, HD]), ALU.mult)\
                       .then_inc(o_norm, 1)

                for j in range(8 + 2):
                    if j < 8:
                        outputs(j)
                    n = j - 2
                    if n >= 0:
                        dve.wait_ge(y_mm, n + 1)
                        xb = g.x[:, TT * n:TT * n + TT, :]
                        dve.tensor_tensor(xb, xb, Y[:, 0:T].rearrange("p (t n) -> p t n", t=TT), ALU.add)\
                           .then_inc(y_add, 1)
                        dve.wait_ge(y_add, n + 1)
                        dve.tensor_tensor(xb, xb, g.w("L2a_bo").unsqueeze(1).to_broadcast([P, TT, D]), ALU.add)


MOE_E, MOE_CAP, MOE_H = 8, 160, 512


def moe_stage(nc, g, name):
    E, CAP, C = MOE_E, MOE_CAP, 512
    NS = E * CAP
    NCH = E + E * (CAP - P) // P
    KH = MOE_H // P
    w1, w2, b1, b2 = (g.big("moe_" + n) for n in ("w1", "w2", "b1", "b2"))
    ow1, ow2, ob1, ob2 = (g.big("moe_" + n) for n in ("ow1", "ow2", "ob1", "ob2"))
    with Stage(nc, name) as st:
        lg = st.sb("lg", [P, NT, E])
        mx = st.sb("mx", [P, NT])
        cand = st.sb("cand", [P, NT, E])
        eid = st.sb("eid", [P, NT])
        onehot = st.sb("onehot", [P, NT, E])
        tot = st.sb("tot", [P, E, NT])
        run = st.sb("run", [P, E, NT])
        rank = st.sb("rank", [P, NT])
        inv = st.sb("inv", [P, NT])
        tmp = st.sb("tmp", [P, 2, NT])
        slot = st.sb("slot", [P, NT])
        row = st.sb("row", [P, NT])
        pick = st.sb("pick", [P, 2, NS])
        bufT = st.sb("bufT", [P, NS])
        rows = st.sb("rows", [P, NTOK])
        hid = st.sb("hid", [P, 2, KH, C])
        y = st.sb("y", [P, NCH, D])
        dg = st.sb("dg", [P, 2, P])
        place = st.sb("place", [P, 2, NCH, P])
        sem = st.sem
        steps_done, logits, onehot_ready, counted, cum_ready, slots_ready = (
            sem("steps"), sem("logits"), sem("onehot"), sem("counted"), sem("cum"), sem("slots"))

        with Stage(nc, name + "r") as sr:
            L = sr.ps("L", [P, C])
            CU = sr.ps("CU", [P, C])
            TO = sr.ps("TO", [P, C])
            with nc.Block() as block:
                @block.tensor
                def _(pe):
                    for t in range(NT):
                        last = pe.matmul(L[:, t * E:(t + 1) * E], g.hT[:, t * P:(t + 1) * P], g.w("moe_rw"),
                                         start=True, stop=True)
                    last.then_inc(logits, 1)
                    pe.wait_ge(onehot_ready, 1)
                    oh = onehot[:].rearrange("p t e -> p (t e)")
                    pe.matmul(CU[:, 0:NT * E], g.causal01[:, 0:P], oh, start=True, stop=True)
                    pe.matmul(TO[:, 0:NT * E], g.ones[:], oh, start=True, stop=True).then_inc(counted, 1)

                @block.vector
                def _(dve):
                    d = Steps(dve, steps_done)
                    iota = g.w("moe_iota").unsqueeze(1).to_broadcast([P, NT, E])
                    dve.wait_ge(logits, 1)
                    d.done(dve.tensor_tensor(lg[:], L[:, 0:NT * E].rearrange("p (t e) -> p t e", t=NT),
                                             g.w("moe_rb").unsqueeze(1).to_broadcast([P, NT, E]), ALU.add))
                    d.done(dve.tensor_reduce(mx[:], lg[:], AX_X, ALU.max))
                    d.done(dve.tensor_tensor(cand[:], lg[:], mx[:].unsqueeze(2).to_broadcast([P, NT, E]),
                                             ALU.is_lt))
                    d.done(dve.scalar_tensor_tensor(out=cand[:], in0=cand[:], scalar=float(E), in1=iota,
                                                    op0=ALU.mult, op1=ALU.add))
                    d.done(dve.tensor_reduce(eid[:], cand[:], AX_X, ALU.min))
                    dve.tensor_tensor(onehot[:], iota, eid[:].unsqueeze(2).to_broadcast([P, NT, E]),
                                      ALU.is_equal).then_inc(onehot_ready, 1)
                    dve.wait_ge(counted, 1)
                    d.done(dve.tensor_copy(tot[:], TO[:, 0:NT * E].rearrange("p (t e) -> p e t", t=NT)))
                    d.done(dve.tensor_tensor_scan(out=run[:].rearrange("p e t -> p (e t)"), data0=g.w("moe_keep"),
                                                  data1=tot[:].rearrange("p e t -> p (e t)"), initial=0.0,
                                                  op0=ALU.mult, op1=ALU.add))
                    d.done(dve.tensor_tensor(run[:], run[:], tot[:], ALU.subtract))
                    d.done(dve.tensor_tensor(cand[:], CU[:, 0:NT * E].rearrange("p (t e) -> p t e", t=NT),
                                             run[:].rearrange("p e t -> p t e"), ALU.add))
                    d.done(dve.tensor_tensor(cand[:], cand[:], onehot[:], ALU.mult))
                    d.done(dve.tensor_reduce(rank[:], cand[:], AX_X, ALU.add))
                    d.done(dve.tensor_scalar(inv[:], rank[:], float(CAP), None, ALU.is_gt))
                    d.done(dve.tensor_scalar(tmp[:, 0, :], inv[:], 10000.0, -1.0, ALU.mult, ALU.add))
                    d.done(dve.tensor_tensor(tmp[:, 0, :], tmp[:, 0, :], rank[:], ALU.add))
                    d.done(dve.scalar_tensor_tensor(out=slot[:], in0=eid[:], scalar=float(CAP), in1=tmp[:, 0, :],
                                                    op0=ALU.mult, op1=ALU.add))
                    d.done(dve.scalar_tensor_tensor(out=row[:], in0=eid[:], scalar=float(P), in1=tmp[:, 0, :],
                                                    op0=ALU.mult, op1=ALU.add))
                    d.done(dve.tensor_scalar(tmp[:, 1, :], eid[:], float(CAP - P - P), float(E * P - P),
                                             ALU.mult, ALU.add))
                    d.done(dve.tensor_scalar(tmp[:, 0, :], rank[:], float(P), None, ALU.is_gt))
                    d.done(dve.tensor_tensor(tmp[:, 1, :], tmp[:, 1, :], tmp[:, 0, :], ALU.mult))
                    dve.tensor_tensor(row[:], row[:], tmp[:, 1, :], ALU.add)

        with Stage(nc, name + "e") as se:
            BU = se.ps("BU", [P, 3, C])
            HP_ = se.ps("HP", [P, 2, C])
            YP = se.ps("YP", [P, 2, C])
            RP = se.ps("RP", [P, C])
            picked, gathered, buf_ready, h_mm, h_act, y_mm, y_cp, dg_ready, r_mm, r_cp = [
                se.sem(n) for n in ("picked", "gathered", "buf_ready", "h_mm", "h_act", "y_mm", "y_cp", "dg_ready",
                                    "r_mm", "r_cp")]
            cuts = [(0, 512), (512, 1024), (1024, NS)]
            with nc.Block() as block:
                @block.vector
                def _(dve):
                    for t in range(NT):
                        if t >= 2:
                            dve.wait_ge(gathered, t - 1)
                        dve.tensor_scalar(pick[:, t % 2, :], g.iota_free[:, 0:NS], slot[:, t:t + 1], None,
                                          ALU.is_equal).then_inc(picked, 1)
                    dve.wait_ge(gathered, NT)
                    for n, (lo, hi) in enumerate(cuts):
                        dve.tensor_copy(bufT[:, lo:hi], BU[:, n, 0:hi - lo]).then_inc(buf_ready, 1)
                    for t in range(NT):
                        if t >= 2:
                            dve.wait_ge(r_mm, t - 1)
                        dve.tensor_scalar(dg[:, t % 2, :], g.ident[:], row[:, t:t + 1], None, ALU.mult)\
                           .then_inc(dg_ready, 1)
                        if t % 4 == 3:
                            dve.wait_ge(r_mm, t + 1)
                            dve.tensor_copy(rows[:, (t - 3) * P:(t + 1) * P], RP[:, :]).then_inc(r_cp, 1)

                @block.tensor
                def _(pe):
                    for t in range(NT):
                        pe.wait_ge(picked, t + 1)
                        for n, (lo, hi) in enumerate(cuts):
                            last = pe.matmul(BU[:, n, 0:hi - lo], g.h[:, t, :], pick[:, t % 2, lo:hi],
                                             start=(t == 0), stop=(t == NT - 1))
                        last.then_inc(gathered, 1)

                    def spread(t):
                        pe.wait_ge(dg_ready, t + 1)
                        if t % 4 == 0 and t:
                            pe.wait_ge(r_cp, t // 4)
                        pe.matmul(RP[:, (t % 4) * P:(t % 4 + 1) * P], g.ones[:], dg[:, t % 2, :],
                                  start=True, stop=True).then_inc(r_mm, 1)

                    def hidden(e):
                        for c in range(KH):
                            n = KH * e + c
                            if n >= 2:
                                pe.wait_ge(h_act, n - 1)
                            pe.matmul(HP_[:, n % 2, 0:CAP], w1[:, n * P:(n + 1) * P], bufT[:, e * CAP:(e + 1) * CAP],
                                      start=True, stop=True).then_inc(h_mm, 1)

                    def second(e):
                        pe.wait_ge(h_act, KH * (e + 1))
                        if e >= 2:
                            pe.wait_ge(y_cp, e - 1)
                        q = (e % 4) * (CAP - P)
                        for c in range(KH):
                            pe.matmul(YP[:, e % 2, 0:D], hid[:, e % 2, c, 0:P],
                                      w2[:, (KH * e + c) * D:(KH * e + c + 1) * D], start=(c == 0), stop=False)
                        pe.matmul(YP[:, e % 2, 0:D], g.ones[0:1, :], b2[0:1, e * D:(e + 1) * D], start=False, stop=True)
                        for c in range(KH):
                            pe.matmul(YP[q:q + CAP - P, e % 2, D:2 * D], hid[:, e % 2, c, P:CAP],
                                      w2[:, (KH * e + c) * D:(KH * e + c + 1) * D], start=(c == 0), stop=False,
                                      tile_position=(0, q))
                        last = pe.matmul(YP[q:q + CAP - P, e % 2, D:2 * D], g.ones[0:1, 0:CAP - P],
                                         b2[0:1, e * D:(e + 1) * D], start=False, stop=True, tile_position=(0, q))
                        last.then_inc(y_mm, 1)

                    pe.wait_ge(buf_ready, 3)
                    for e in range(E + 1):
                        if e < E:
                            hidden(e)
                            spread(2 * e)
                            spread(2 * e + 1)
                        if e >= 1:
                            second(e - 1)

                @block.scalar
                def _(act):
                    def copies(e):
                        act.wait_ge(y_mm, e + 1)
                        q = (e % 4) * (CAP - P)
                        act.activation(y[:, e, :], YP[:, e % 2, 0:D], ACT.Copy)
                        act.activation(y[q:q + CAP - P, E + e // 4, :], YP[q:q + CAP - P, e % 2, D:2 * D],
                                       ACT.Copy).then_inc(y_cp, 1)

                    for e in range(E):
                        if e >= 2:
                            act.wait_ge(y_mm, e - 1)
                        for c in range(KH):
                            n = KH * e + c
                            act.wait_ge(h_mm, n + 1)
                            act.activation(hid[:, e % 2, c, 0:CAP], HP_[:, n % 2, 0:CAP], ACT.Relu,
                                           bias=b1[:, n:n + 1]).then_inc(h_act, 1)
                        if e >= 1:
                            copies(e - 1)
                    copies(E - 1)

        with Stage(nc, name + "o") as so:
            HO = so.ps("HO", [P, 2, C])
            YO = so.ps("YO", [P, 2, C])
            YE = so.ps("YE", [P, 2, C])
            placed, h_mm, h_act, o_mm, e_mm, added, own = [
                so.sem(n) for n in ("placed", "h_mm", "h_act", "o_mm", "e_mm", "added", "own")]
            with nc.Block() as block:
                @block.tensor
                def _(pe):
                    def hidden(c):
                        for k in range(KH):
                            n = KH * c + k
                            if n >= 2:
                                pe.wait_ge(h_act, n - 1)
                            pe.matmul(HO[:, n % 2, :], ow1[:, k * P:(k + 1) * P], g.hT[:, c * C:(c + 1) * C],
                                      start=True, stop=True).then_inc(h_mm, 1)

                    def outputs(t):
                        if t >= 2:
                            pe.wait_ge(added, 2 * (t - 1))
                        c = t // 4
                        cols = slice((t % 4) * P, (t % 4 + 1) * P)
                        pe.wait_ge(h_act, KH * (c + 1))
                        for k in range(KH):
                            pe.matmul(YO[:, t % 2, 0:D], hid[:, c % 2, k, cols], ow2[:, k * D:(k + 1) * D],
                                      start=(k == 0), stop=False)
                        pe.matmul(YO[:, t % 2, 0:D], g.ones[0:1, :], ob2[0:1, :], start=False, stop=True)\
                          .then_inc(o_mm, 1)
                        pe.wait_ge(placed, t + 1)
                        for k in range(NCH):
                            last = pe.matmul(YE[:, t % 2, 0:D], place[:, t % 2, k, :], y[:, k, :],
                                             start=(k == 0), stop=(k == NCH - 1))
                        last.then_inc(e_mm, 1)

                    hidden(0)
                    for c in range(4):
                        if c < 3:
                            hidden(c + 1)
                        for t in range(4 * c, 4 * c + 4):
                            outputs(t)

                @block.scalar
                def _(act):
                    for c in range(4):
                        if c >= 2:
                            act.wait_ge(o_mm, 4 * (c - 1))
                        for k in range(KH):
                            n = KH * c + k
                            act.wait_ge(h_mm, n + 1)
                            act.activation(hid[:, c % 2, k, :], HO[:, n % 2, :], ACT.Relu, bias=ob1[:, k:k + 1])\
                               .then_inc(h_act, 1)

                @block.vector
                def _(dve):
                    def one_hot(t):
                        if t >= 2:
                            dve.wait_ge(e_mm, t - 1)
                        dve.tensor_tensor(place[:, t % 2, :, :],
                                          rows[:, t * P:(t + 1) * P].unsqueeze(1).to_broadcast([P, NCH, P]),
                                          g.w("moe_rowid").unsqueeze(2).to_broadcast([P, NCH, P]),
                                          ALU.is_equal).then_inc(placed, 1)

                    one_hot(0)
                    for t in range(NT):
                        if t + 1 < NT:
                            one_hot(t + 1)
                        xt = g.x[:, t, :]
                        dve.wait_ge(o_mm, t + 1)
                        dve.scalar_tensor_tensor(out=xt, in0=YO[:, t % 2, 0:D], scalar=inv[:, t:t + 1], in1=xt,
                                                 op0=ALU.mult, op1=ALU.add).then_inc(added, 1)
                        dve.wait_ge(added, 2 * t + 1)
                        dve.wait_ge(e_mm, t + 1)
                        dve.tensor_tensor(xt, xt, YE[:, t % 2, 0:D], ALU.add).then_inc(added, 1)


def alibi_attention_stage(nc, g, name):
    scale = D ** -0.5
    with Stage(nc, name) as st:
        qT = st.sb("qT", [P, NTOK])
        v = st.sb("v", [P, NT, D])
        dist = st.sb("dist", [P, TT, T])
        sc = st.sb("sc", [P, 2, TT, T])
        pr = st.sb("pr", [P, 2, TT, T])
        prT = st.sb("prT", [P, 2, 512])
        negmax = st.sb("negmax", [P, B, TT])
        sums = st.sb("sums", [P, B, TT])
        rinv = st.sb("rinv", [P, B, TT])
        FR = st.ps("FR", [P, 2, 512])
        S = st.ps("S", [P, 2, 512])
        PT = st.ps("PT", [P, 2, 512])
        O = st.ps("O", [P, 2, 4, P])
        (iota_done, bias_ready, front_mm, front_cp, scored, biased, maxed, expd, turned, prT_cp, pv, added,
         recip) = [
            st.sem(n) for n in ("iota", "bias_ready", "front_mm", "front_cp", "scored", "biased", "maxed",
                                "expd", "turned", "prT_cp", "pv", "added", "recip")]

        with nc.Block() as block:
            @block.gpsimd
            def _(pool):
                pool.iota(dist[:], pattern=[[-P, TT], [1, T]], base=0, channel_multiplier=-1,
                          allow_small_or_imprecise_dtypes=True).then_inc(iota_done, 1)
                pool.wait_ge(iota_done, 1)
                pool.tensor_scalar(dist[:], dist[:], g.w("L1a_slope"), None, ALU.mult).then_inc(iota_done, 1)
                pool.wait_ge(iota_done, 2)
                pool.affine_select(out=dist[:], in_=dist[:], compare_op=ALU.is_ge, fill=NEG, base=0,
                                   pattern=[[P, TT], [-1, T]], channel_multiplier=1).then_inc(bias_ready, 1)

            @block.tensor
            def _(pe):
                for c in range(4):
                    if c >= 2:
                        pe.wait_ge(front_cp, c - 1)
                    pe.matmul(FR[:, c % 2, :], g.w("L1a_wqk"), g.hT[:, c * 512:(c + 1) * 512],
                              start=True, stop=True).then_inc(front_mm, 1)
                for c in range(4, 8):
                    pe.wait_ge(front_cp, c - 1)
                    for t in range(4):
                        tile = 4 * (c - 4) + t
                        last = pe.matmul(FR[:, c % 2, t * P:(t + 1) * P], g.hT[:, tile * P:(tile + 1) * P],
                                         g.w("L1a_wv"), start=True, stop=True)
                    last.then_inc(front_mm, 1)
                for i in range(B + 3):
                    if i < B:
                        if i == 0:
                            pe.wait_ge(front_cp, 4)
                        if i >= 2:
                            pe.wait_ge(biased, i - 1)
                        for t in range(TT):
                            tile = TT * i + t
                            last = pe.matmul(S[:, i % 2, t * T:(t + 1) * T], qT[:, tile * P:(tile + 1) * P],
                                             g.hT[:, i * T:(i + 1) * T], start=True, stop=True)
                        last.then_inc(scored, 1)
                    j = i - 2
                    if 0 <= j < B:
                        pe.wait_ge(expd, j + 1)
                        if j >= 2:
                            pe.wait_ge(prT_cp, j - 1)
                        for t in range(TT):
                            for k in range(TT):
                                last = pe.transpose(PT[:, j % 2, (2 * k + t) * P:(2 * k + t + 1) * P],
                                                    pr[:, j % 2, t, k * P:(k + 1) * P], g.ident[:])
                        last.then_inc(turned, 1)
                    j = i - 3
                    if 0 <= j < B:
                        pe.wait_ge(prT_cp, j + 1)
                        if j == 0:
                            pe.wait_ge(front_cp, 8)
                        if j >= 2:
                            pe.wait_ge(added, 2 * (j - 1))
                        for t in range(TT):
                            for k in range(TT):
                                last = pe.matmul(O[:, j % 2, t, :],
                                                 prT[:, j % 2, (2 * k + t) * P:(2 * k + t + 1) * P],
                                                 v[:, TT * j + k, :], start=(k == 0), stop=(k == TT - 1))
                        last.then_inc(pv, 1)

            @block.scalar
            def _(act):
                for c in range(4):
                    act.wait_ge(front_mm, c + 1)
                    act.activation(qT[:, c * 512:(c + 1) * 512], FR[:, c % 2, :], ACT.Copy,
                                   scale=scale).then_inc(front_cp, 1)
                for c in range(4, 8):
                    act.wait_ge(front_mm, c + 1)
                    act.activation(v[:, 4 * (c - 4):4 * (c - 3), :],
                                   FR[:, c % 2, :].rearrange("p (t n) -> p t n", t=4), ACT.Copy)\
                       .then_inc(front_cp, 1)
                for i in range(B):
                    act.wait_ge(maxed, i + 1)
                    if i >= 2:
                        act.wait_ge(turned, i - 1)
                    for t in range(TT):
                        ins = act.activation(pr[:, i % 2, t, :], sc[:, i % 2, t, :], ACT.Exp,
                                             bias=negmax[:, i, t:t + 1], accum_out=sums[:, i, t:t + 1])
                    ins.then_inc(expd, 1)

            @block.vector
            def _(dve):
                dve.wait_ge(bias_ready, 1)
                for i in range(B + 3):
                    if i < B:
                        dve.wait_ge(scored, i + 1)
                        if i >= 2:
                            dve.wait_ge(expd, i - 1)
                        dve.tensor_tensor(sc[:, i % 2, :, :], S[:, i % 2, :].rearrange("p (t k) -> p t k", t=TT),
                                          dist[:], ALU.add).then_inc(biased, 1)
                        dve.wait_ge(biased, i + 1)
                        dve.tensor_reduce(negmax[:, i, :], sc[:, i % 2, :, :], AX_X, ALU.max,
                                          negate=True).then_inc(maxed, 1)
                    j = i - 2
                    if 0 <= j < B:
                        dve.wait_ge(turned, j + 1)
                        if j >= 2:
                            dve.wait_ge(pv, j - 1)
                        dve.tensor_copy(prT[:, j % 2, :], PT[:, j % 2, :]).then_inc(prT_cp, 1)
                    j = i - 3
                    if 0 <= j < B:
                        dve.wait_ge(expd, j + 1)
                        dve.reciprocal(rinv[:, j, :], sums[:, j, :]).then_inc(recip, 1)
                        dve.wait_ge(recip, j + 1)
                        dve.wait_ge(pv, j + 1)
                        for t in range(TT):
                            xt = g.x[:, TT * j + t, :]
                            dve.scalar_tensor_tensor(out=xt, in0=O[:, j % 2, t, :], scalar=rinv[:, j, t:t + 1],
                                                     in1=xt, op0=ALU.mult, op1=ALU.add).then_inc(added, 1)


def mamba_stage(nc, g, name):
    C = 512
    NC_ = NTOK // C
    M = 2
    N = STATE
    ROWS = 80
    ax, az = g.w("m_in_w"), g.w("m_in_b")
    with Stage(nc, name) as st:
        u = st.sb("u", [P, M, NTOK])
        gate = st.sb("gate", [P, M, NTOK])
        delta = st.sb("delta", [P, M, NTOK])
        du = st.sb("du", [P, M, NTOK])
        aneg = st.sb("aneg", [P, M * N])
        xd = g.h[:].rearrange("p t d -> p (t d)")

        with Stage(nc, name + "f") as sf:
            xpad = sf.sb("xpad", [P, M, B, T + 4])
            e = sf.sb("e", [P, M, NTOK])
            XZ = sf.ps("XZ", [P, 4, C])
            XD = sf.ps("XD", [P, 2, C])
            DP = sf.ps("DP", [P, 2, C])
            (pads, xz_mm, xz_cp, conv, u_ready, xd_mm, xd_cp, dp_mm, v_ready, abs_ready, exp_ready, one_ready,
             ln_ready, rest_ready, recip_ready, steps, a_exp) = [
                sf.sem(n) for n in ("pads", "xz_mm", "xz_cp", "conv", "u_ready", "xd_mm", "xd_cp", "dp_mm",
                                    "v_ready", "abs_ready", "exp_ready", "one_ready", "ln_ready", "rest_ready",
                                    "recip_ready", "steps", "a_exp")]
            w4 = [xpad[:, m, :, :].rearrange("p b t -> p (b t)")[:, 0:NTOK] for m in range(M)]
            with nc.Block() as block:
                @block.gpsimd
                def _(pool):
                    pool.memset(xpad[:, :, :, 0:4], 0.0).then_inc(pads, 1)

                @block.tensor
                def _(pe):
                    def deltas(c):
                        pe.wait_ge(xd_cp, c + 1)
                        for m in range(M):
                            n = M * c + m
                            if n >= 2:
                                pe.wait_ge(v_ready, n - 1)
                            pe.matmul(DP[:, n % 2, :], g.w("m_dt_w")[:, m * P:(m + 1) * P], xd[0:DT_RANK, c * C:(c + 1) * C],
                                      start=True, stop=True).then_inc(dp_mm, 1)

                    for c in range(NC_):
                        for m in range(4):
                            n = 4 * c + m
                            if n >= 4:
                                pe.wait_ge(xz_cp, n - 3)
                            pe.matmul(XZ[:, n % 4, :], ax[:, m * P:(m + 1) * P], g.hT[:, c * C:(c + 1) * C],
                                      start=True, stop=True).then_inc(xz_mm, 1)
                    for c in range(NC_):
                        pe.wait_ge(u_ready, M * (c + 1))
                        if c >= 2:
                            pe.wait_ge(xd_cp, c - 1)
                        for m in range(M):
                            last = pe.matmul(XD[0:ROWS, c % 2, :], g.w("m_x_w")[:, m * ROWS:(m + 1) * ROWS],
                                             u[:, m, c * C:(c + 1) * C], start=(m == 0), stop=(m == M - 1))
                        last.then_inc(xd_mm, 1)
                        deltas(c)

                @block.scalar
                def _(act):
                    act.activation(aneg[:], g.w("m_a_log"), ACT.Exp).then_inc(a_exp, 1)
                    for c in range(NC_):
                        for m in range(4):
                            n = 4 * c + m
                            act.wait_ge(xz_mm, n + 1)
                            if m < M:
                                act.activation(xpad[:, m, 2 * c:2 * c + 2, 4:],
                                               XZ[:, n % 4, :].rearrange("p (b t) -> p b t", b=2), ACT.Identity,
                                               bias=az[:, m:m + 1]).then_inc(xz_cp, 1)
                            else:
                                act.activation(gate[:, m - M, c * C:(c + 1) * C], XZ[:, n % 4, :], ACT.Silu,
                                               bias=az[:, m:m + 1]).then_inc(xz_cp, 1)
                    for c in range(NC_):
                        for m in range(M):
                            act.wait_ge(conv, 4 * (M * c + m) + 4)
                            cols = u[:, m, c * C:(c + 1) * C]
                            act.activation(cols, cols, ACT.Silu).then_inc(u_ready, 1)
                        act.wait_ge(xd_mm, c + 1)
                        act.activation(xd[0:ROWS, c * C:(c + 1) * C], XD[0:ROWS, c % 2, :], ACT.Copy).then_inc(xd_cp, 1)
                        for m in range(M):
                            n = M * c + m
                            act.wait_ge(dp_mm, n + 1)
                            act.activation(delta[:, m, c * C:(c + 1) * C], DP[:, n % 2, :], ACT.Identity,
                                           bias=g.w("m_dt_b")[:, m:m + 1]).then_inc(v_ready, 1)
                    for m in range(M):
                        act.wait_ge(abs_ready, m + 1)
                        act.activation(e[:, m, :], e[:, m, :], ACT.Exp, scale=-1.0).then_inc(exp_ready, 1)
                    for m in range(M):
                        act.wait_ge(one_ready, m + 1)
                        act.activation(du[:, m, :], w4[m], ACT.Ln).then_inc(ln_ready, 1)
                    for m in range(M):
                        act.wait_ge(ln_ready, m + 1)
                        act.wait_ge(rest_ready, m + 1)
                        act.activation(w4[m], du[:, m, :], ACT.Exp, scale=-1.0).then_inc(recip_ready, 1)

                @block.vector
                def _(dve):
                    d = Steps(dve, steps)
                    dve.wait_ge(a_exp, 1)
                    dve.tensor_scalar(aneg[:], aneg[:], -1.0, None, ALU.mult)
                    dve.wait_ge(pads, 1)
                    n = 0
                    for c in range(NC_):
                        for m in range(M):
                            dve.wait_ge(xz_cp, 4 * c + m + 1)
                            out = u[:, m, c * C:(c + 1) * C].rearrange("p (b t) -> p b t", b=2)
                            for k in range(4):
                                src = xpad[:, m, 2 * c:2 * c + 2, 1 + k:1 + k + T]
                                wk = g.w("m_conv_w")[:, 4 * m + k:4 * m + k + 1]
                                if k == 0:
                                    ins = dve.tensor_scalar(out, src, wk, g.w("m_conv_b")[:, m:m + 1],
                                                            ALU.mult, ALU.add)
                                else:
                                    dve.wait_ge(conv, n)
                                    ins = dve.scalar_tensor_tensor(out=out, in0=src, scalar=wk, in1=out,
                                                                   op0=ALU.mult, op1=ALU.add)
                                ins.then_inc(conv, 1)
                                n += 1
                    dve.wait_ge(v_ready, M * NC_)
                    for m in range(M):
                        v = delta[:, m, :]
                        dve.scalar_tensor_tensor(out=e[:, m, :], in0=v, scalar=-1.0, in1=v, op0=ALU.mult,
                                                 op1=ALU.max).then_inc(abs_ready, 1)
                    dve.wait_ge(abs_ready, M)
                    for m in range(M):
                        dve.wait_ge(exp_ready, m + 1)
                        dve.tensor_scalar(w4[m], e[:, m, :], 1.0, None, ALU.add).then_inc(one_ready, 1)
                        d.mark(dve.tensor_scalar(delta[:, m, :], delta[:, m, :], 0.0, None, ALU.max))
                    for m in range(M):
                        dve.wait_ge(one_ready, m + 1)
                        dve.scalar_tensor_tensor(out=e[:, m, :], in0=w4[m], scalar=-1.0, in1=e[:, m, :],
                                                 op0=ALU.add, op1=ALU.subtract).then_inc(rest_ready, 1)
                    d.wait()
                    for m in range(M):
                        dve.wait_ge(ln_ready, m + 1)
                        d.mark(dve.tensor_tensor(delta[:, m, :], delta[:, m, :], du[:, m, :], ALU.add))
                    dve.wait_ge(rest_ready, M)
                    for m in range(M):
                        dve.wait_ge(recip_ready, m + 1)
                        d.mark(dve.tensor_tensor(e[:, m, :], e[:, m, :], w4[m], ALU.mult))
                    d.wait()
                    for m in range(M):
                        d.mark(dve.tensor_tensor(delta[:, m, :], delta[:, m, :], e[:, m, :], ALU.subtract))
                    d.wait()
                    dve.wait_ge(u_ready, M * NC_)
                    for m in range(M):
                        dve.tensor_tensor(du[:, m, :], delta[:, m, :], u[:, m, :], ALU.mult)

        with Stage(nc, name + "s") as ss:
            dA = ss.sb("dA", [P, 2, M, C])
            dBu = ss.sb("dBu", [P, 2, M, C])
            hs = ss.sb("hs", [P, 2, M, C])
            bc = ss.sb("bc", [P, 3, 2, C])
            xparts = ss.sb("xparts", [ROWS, 3, NTOK], BF16)
            hc = g.hT[:, 0:2 * M * C].rearrange("p (i m c) -> p i m c", i=2, m=M)
            rest = g.hT[0:ROWS, 0:NTOK]
            yv = ss.sb("yv", [P, M, C])
            BC = ss.ps("BC", [P, 2, 2, C])
            Y = ss.ps("Y", [P, M, C])
            OUT = ss.ps("OUT", [P, 2, C])
            split, paired, bc_mm, bc_cp, exps, dbu, scans, hcs, summed, gated, out_mm, added = [
                ss.sem(n) for n in ("split", "paired", "bc_mm", "bc_cp", "exps", "dbu", "scans", "hcs", "summed", "gated", "out_mm",
                                    "added")]
            Q = NC_ * N
            with nc.Block() as block:
                @block.tensor
                def _(pe):
                    def broadcasts(q):
                        if q >= 2:
                            pe.wait_ge(bc_cp, q - 1)
                        c, n = divmod(q, N)
                        for j in range(2):
                            row = 32 * (j + 1) + n
                            for k in range(3):
                                last = pe.matmul(BC[:, q % 2, j, :],
                                                 g.ident_bf[0:ROWS, row:row + 1].to_broadcast([ROWS, P]),
                                                 xparts[:, k, c * C:(c + 1) * C], start=(k == 0), stop=(k == 2))
                        last.then_inc(bc_mm, 1)

                    def outputs(c):
                        pe.wait_ge(gated, 2 * (c + 1))
                        if c >= 2:
                            pe.wait_ge(added, c - 1)
                        for t in range(4):
                            o = OUT[:, c % 2, t * P:(t + 1) * P]
                            for m in range(M):
                                pe.matmul(o, yv[:, m, t * P:(t + 1) * P], g.w("m_out_w")[:, m * D:(m + 1) * D],
                                          start=(t == 0 and m == 0), stop=False, skip_group_check=True)
                            last = pe.matmul(o, g.ones[0:1, :], g.w("m_out_b"), start=False, stop=(t == 3),
                                             skip_group_check=True)
                        last.then_inc(out_mm, 1)

                    pe.wait_ge(split, 5)
                    broadcasts(0)
                    broadcasts(1)
                    for q in range(Q + 2):
                        if q + 2 < Q:
                            broadcasts(q + 2)
                        if q % N == 4 and q > N:
                            outputs(q // N - 1)
                        if q % 2 == 0 or q < 3:
                            continue
                        pair = q // 2 - 1
                        first, last_ = pair % (N // 2) == 0, pair % (N // 2) == N // 2 - 1
                        if first and pair:
                            pe.wait_ge(gated, 2 * (q // N) - 1)
                        pe.wait_ge(paired, pair + 1)
                        for m in range(M):
                            last = pe.matmul(Y[:, m, :], g.ident[:], hc[:, pair % 2, m, :], start=first, stop=last_)
                        last.then_inc(summed, 1)
                    outputs(NC_ - 1)

                @block.scalar
                def _(act):
                    def copy(q):
                        act.wait_ge(bc_mm, q + 1)
                        if q >= 3:
                            act.wait_ge(hcs, q - 2)
                            act.wait_ge(dbu, q - 2)
                        act.activation(bc[:, q % 3, :, :], BC[:, q % 2, :, :], ACT.Copy).then_inc(bc_cp, 1)

                    copy(0)
                    for q in range(Q):
                        c, n = divmod(q, N)
                        if q >= 2:
                            act.wait_ge(scans, q - 1)
                        for m in range(M):
                            ins = act.activation(dA[:, q % 2, m, :], delta[:, m, c * C:(c + 1) * C], ACT.Exp,
                                                 scale=aneg[:, m * N + n:m * N + n + 1])
                        ins.then_inc(exps, 1)
                        if q + 1 < Q:
                            copy(q + 1)

                @block.gpsimd
                def _(pool):
                    for q in range(Q):
                        c = q // N
                        pool.wait_ge(bc_cp, q + 1)
                        if q >= 2:
                            pool.wait_ge(scans, q - 1)
                        pool.tensor_tensor(dBu[:, q % 2, :, :], du[:, :, c * C:(c + 1) * C],
                                           bc[:, q % 3, 0:1, :].to_broadcast([P, M, C]), ALU.mult).then_inc(dbu, 1)

                @block.vector
                def _(dve):
                    x2 = xd[0:ROWS, :]
                    dve.tensor_copy(xparts[:, 0, :], x2).then_inc(split, 1)
                    dve.wait_ge(split, 1)
                    dve.tensor_tensor(rest, x2, xparts[:, 0, :], ALU.subtract).then_inc(split, 1)
                    dve.wait_ge(split, 2)
                    dve.tensor_copy(xparts[:, 1, :], rest).then_inc(split, 1)
                    dve.wait_ge(split, 3)
                    dve.tensor_tensor(rest, rest, xparts[:, 1, :], ALU.subtract).then_inc(split, 1)
                    dve.wait_ge(split, 4)
                    dve.tensor_copy(xparts[:, 2, :], rest).then_inc(split, 1)

                    def times_c(q):
                        dve.wait_ge(scans, q + 1)
                        if q >= 4 and q % 2 == 0:
                            dve.wait_ge(summed, q // 2 - 1)
                        to = hc[:, q // 2 % 2, :, :] if q % 2 == 0 else hs[:, 1, :, :]
                        dve.tensor_tensor(to, hs[:, q % 2, :, :],
                                          bc[:, q % 3, 1:2, :].to_broadcast([P, M, C]), ALU.mult).then_inc(hcs, 1)

                    def pair(q):
                        dve.wait_ge(hcs, q + 1)
                        to = hc[:, q // 2 % 2, :, :]
                        dve.tensor_tensor(to, to, hs[:, 1, :, :], ALU.add).then_inc(paired, 1)

                    def finish(c):
                        dve.wait_ge(summed, N // 2 * (c + 1))
                        if c >= 1:
                            dve.wait_ge(out_mm, c)
                        for m in range(M):
                            ins = dve.scalar_tensor_tensor(out=yv[:, m, :], in0=u[:, m, c * C:(c + 1) * C],
                                                           scalar=g.w("m_d")[:, m:m + 1], in1=Y[:, m, :],
                                                           op0=ALU.mult, op1=ALU.add)
                        ins.then_inc(gated, 1)
                        dve.wait_ge(gated, 2 * c + 1)
                        dve.tensor_tensor(yv[:], yv[:], gate[:, :, c * C:(c + 1) * C], ALU.mult).then_inc(gated, 1)

                    def add_x(c):
                        dve.wait_ge(out_mm, c + 1)
                        xt = g.x[:, 4 * c:4 * c + 4, :]
                        dve.tensor_tensor(xt, xt, OUT[:, c % 2, :].rearrange("p (t d) -> p t d", t=4), ALU.add)\
                           .then_inc(added, 1)

                    for q in range(Q):
                        dve.wait_ge(exps, q + 1)
                        dve.wait_ge(dbu, q + 1)
                        if q >= 2:
                            dve.wait_ge(hcs, q - 1)
                        if q >= 3 and q % 2:
                            dve.wait_ge(paired, q // 2)
                        for m in range(M):
                            for b in range(2):
                                cols = slice(b * T, (b + 1) * T)
                                ins = dve.tensor_tensor_scan(out=hs[:, q % 2, m, cols], data0=dA[:, q % 2, m, cols],
                                                             data1=dBu[:, q % 2, m, cols], initial=0.0,
                                                             op0=ALU.mult, op1=ALU.add)
                        ins.then_inc(scans, 1)
                        if q >= 1:
                            times_c(q - 1)
                        if q >= 2 and q % 2 == 0:
                            pair(q - 1)
                        if q % N == 2 and q > N:
                            finish(q // N - 1)
                        if q % N == 8 and q > N:
                            add_x(q // N - 1)
                    times_c(Q - 1)
                    pair(Q - 1)
                    finish(NC_ - 1)
                    add_x(NC_ - 1)


class RoutedPlan:
    G, NB = 4, 4
    UNITS = 4 * B
    GROUPS = UNITS // NB
    TAIL = 5

    def __init__(self):
        self.steps = []
        for i in range(self.UNITS + self.TAIL):
            items = []
            if i == 0:
                items += self.front(0, "gather") + self.front(0, "q") + self.front(0, "k")
            if i < self.UNITS:
                items.append(("v", i))
                nxt = i // self.NB + 1
                if nxt < self.GROUPS and i % self.NB:
                    items += self.front(nxt, ("gather", "q", "k")[i % self.NB - 1])
            if 0 <= i - 1 < self.UNITS:
                items.append(("turn", i - 1))
            self.steps.append(items)
        self.number = {item: n for n, item in enumerate(item for s in self.steps for item in s)}

    @staticmethod
    def front(group, what):
        return [(what, group, k) for k in range({"gather": 2, "q": 4, "k": 2}[what])]

    def unit(self, i):
        group, k = divmod(i, self.NB)
        g_, half = divmod(group, 2)
        return g_, half * self.NB + k


def routed_attention_stage(nc, g, name):
    plan = RoutedPlan()
    U, NB, G, H, DH, NQ, NK = plan.UNITS, plan.NB, plan.G, 8, 64, 128, 64
    ROWS = B * 2 * G
    wq, wk, wv, wo = g.big("r_wq"), g.big("r_wk"), g.big("r_wv"), g.big("r_wo")
    with Stage(nc, name) as st:
        sig = st.sb("sig", [P, TT, B, 2 * G])
        slot = st.sb("slot", [P, TT, B, 2 * G])
        rcount = st.sb("rcount", [P, TT, B])

        with Stage(nc, name + "r") as sr:
            lg = sr.sb("lg", [P, TT, B, 2 * G])
            row = sr.sb("row", [ROWS, T])
            work = sr.sb("work", [ROWS, T])
            best = sr.sb("best", [ROWS, 8])
            mask_kv = sr.sb("mask_kv", [ROWS, T])
            mask = sr.sb("mask", [ROWS, T])
            csum = sr.sb("csum", [ROWS, T])
            ones_row = sr.sb("ones_row", [ROWS, T])
            chosen = sr.sb("chosen", [P, TT, B, G])
            count = sr.sb("count", [P, TT, B])
            missed = sr.sb("missed", [P, TT, B])
            L = sr.ps("L", [P, 512])
            LT = sr.ps("LT", [P, 512])
            ST = sr.ps("ST", [P, 512])
            logits, lg_ready, rows_ready, slots_ready, back, steps = [
                sr.sem(n) for n in ("logits", "lg_ready", "rows_ready", "slots_ready", "back", "steps")]
            with nc.Block() as block:
                @block.tensor
                def _(pe):
                    for t in range(NT):
                        last = pe.matmul(L[:, t * 2 * G:(t + 1) * 2 * G], g.hT[:, t * P:(t + 1) * P],
                                         g.w("r_router"), start=True, stop=True)
                    last.then_inc(logits, 1)
                    pe.wait_ge(lg_ready, 1)
                    for h in range(TT):
                        last = pe.transpose(LT[0:ROWS, h * P:(h + 1) * P],
                                            lg[:, h, :, :].rearrange("p b j -> p (b j)"), g.ident[:])
                    last.then_inc(rows_ready, 1)
                    pe.wait_ge(slots_ready, 1)
                    for h in range(TT):
                        last = pe.transpose(ST[:, h * ROWS:(h + 1) * ROWS], csum[:, h * P:(h + 1) * P],
                                            g.ident[0:ROWS, 0:ROWS])
                    last.then_inc(back, 1)

                @block.scalar
                def _(act):
                    act.wait_ge(lg_ready, 1)
                    act.activation(sig[:], lg[:], ACT.Sigmoid)

                @block.vector
                def _(dve):
                    d = Steps(dve, steps)
                    dve.wait_ge(logits, 1)
                    dve.tensor_copy(lg[:], L[:, 0:NT * 2 * G].rearrange("p (b h j) -> p h b j", b=B, h=TT))\
                       .then_inc(lg_ready, 1)
                    dve.memset(ones_row[:], 1.0)
                    dve.wait_ge(rows_ready, 1)
                    d.mark(dve.tensor_copy(row[:], LT[0:ROWS, 0:T]))
                    d.done(dve.tensor_copy(work[:], LT[0:ROWS, 0:T]))
                    for k in range(NQ // 8):
                        d.done(dve.max(best[:], work[:]))
                        d.done(dve.match_replace(out=work[:], in_to_replace=best[:], in_values=work[:],
                                                 imm_value=NEG))
                        if 8 * (k + 1) == NK:
                            d.done(dve.tensor_tensor(mask_kv[:], work[:], row[:], ALU.not_equal))
                    d.done(dve.tensor_tensor(mask[:], work[:], row[:], ALU.not_equal))
                    d.done(dve.tensor_tensor(mask_kv[:], mask_kv[:], mask[:], ALU.subtract))
                    d.done(dve.scalar_tensor_tensor(out=mask[:], in0=mask_kv[:], scalar=g.w("r_iskv"), in1=mask[:],
                                                    op0=ALU.mult, op1=ALU.add))
                    d.done(dve.tensor_tensor_scan(out=csum[:], data0=ones_row[:], data1=mask[:], initial=0.0,
                                                  op0=ALU.mult, op1=ALU.add))
                    d.done(dve.tensor_tensor(csum[:], csum[:], mask[:], ALU.mult))
                    dve.tensor_scalar(csum[:], csum[:], -1.0, None, ALU.add).then_inc(slots_ready, 1)
                    dve.wait_ge(back, 1)
                    d.done(dve.tensor_copy(slot[:].rearrange("p h b j -> p (h b j)"), ST[:, 0:TT * ROWS]))
                    d.done(dve.tensor_scalar(chosen[:], slot[:, :, :, 0:G], 0.0, None, ALU.is_ge))
                    d.done(dve.tensor_reduce(count[:], chosen[:], AX_X, ALU.add))
                    d.mark(dve.tensor_scalar(missed[:], count[:], 0.0, None, ALU.is_le))
                    d.done(dve.tensor_scalar(rcount[:], count[:], 1e-5, None, ALU.max))
                    d.done(dve.reciprocal(rcount[:], rcount[:]))
                    for t in range(NT):
                        b, h = divmod(t, TT)
                        dve.scalar_tensor_tensor(out=g.x[:, t, :], in0=g.w("r_null"), scalar=missed[:, h, b:b + 1],
                                                 in1=g.x[:, t, :], op0=ALU.mult, op1=ALU.add)

        with Stage(nc, name + "a") as sa:
            oh = sa.sb("oh", [P, NB, TT, 2 * P])
            sq = g.hT[:, 0:NTOK].rearrange("p (u h s) -> p u h s", u=2 * NB, h=TT)
            sel = sa.sb("sel", [P, 2, NB, 2 * P])
            qT = sa.sb("qT", [P, 2, 4, NB, NQ])
            kT = sa.sb("kT", [P, 2, 4, NB, NK + 1])
            v = sa.sb("v", [P, 3, 4 * DH])
            ev = sa.sb("ev", [P, 2, 2, 4, NK + 1])
            mx = sa.sb("mx", [P, 2, 2, 4])
            rsum = sa.sb("rsum", [P, 2, 2, 4])
            pr = sa.sb("pr", [P, 2, H, NK])
            pn = sa.sb("pn", [P, 2, H])
            prT = sa.sb("prT", [P, 2, 512])
            pnT = sa.sb("pnT", [H, 2, NQ])
            sqT = sa.sb("sqT", [P, 4, T])
            oT = sa.sb("oT", [P, 2, 512])
            o = sa.sb("o", [P, 2, D])
            F = sa.ps("F", [P, 2, 512])
            S = sa.ps("S", [P, 2, 512])
            PT = sa.ps("PT", [P, 512])
            OT = sa.ps("OT", [P, 512])
            OUT = sa.ps("OUT", [P, 512])
            X = sa.ps("X", [P, 512])
            (onehots, scaled, nullk, f_mm, f_cp, scored, maxed, shifted, expd, summed, recip, normed, turned,
             prT_cp, pv, oT_cp, projected, o_cp, scattered, added) = [
                sa.sem(n) for n in ("onehots", "scaled", "nullk", "f_mm", "f_cp", "scored", "maxed", "shifted",
                                    "expd", "summed", "recip", "normed", "turned", "prT_cp", "pv", "oT_cp",
                                    "projected", "o_cp", "scattered", "added")]

            def copied(*item):
                return plan.number[item] + 1

            with nc.Block() as block:
                @block.tensor
                def _(pe):
                    def item(it):
                        n = plan.number[it]
                        f = F[:, n % 2, :]
                        if n >= 2:
                            pe.wait_ge(f_cp, n - 1)
                        if it[0] == "gather":
                            _, group, k = it
                            for bb in (2 * k, 2 * k + 1):
                                b = plan.unit(group * NB + bb)[1]
                                pe.wait_ge(scaled, group * NB + bb + 1)
                                for h in range(TT):
                                    last = pe.matmul(f[:, (bb % 2) * 256:(bb % 2 + 1) * 256], g.h[:, TT * b + h, :],
                                                     oh[:, bb, h, :], start=(h == 0), stop=(h == TT - 1))
                        elif it[0] == "q":
                            _, group, c = it
                            s = plan.unit(group * NB)[0]
                            pe.wait_ge(f_cp, copied("gather", group, 1))
                            last = pe.matmul(f, wq[:, (4 * s + c) * P:(4 * s + c + 1) * P], sel[:, group % 2, :, 0:NQ],
                                             start=True, stop=True)
                        elif it[0] == "k":
                            _, group, k = it
                            s = plan.unit(group * NB)[0]
                            for c in (2 * k, 2 * k + 1):
                                last = pe.matmul(f[:, (c % 2) * 256:(c % 2 + 1) * 256],
                                                 wk[:, (4 * s + c) * P:(4 * s + c + 1) * P],
                                                 sel[:, group % 2, :, NQ:NQ + NK], start=True, stop=True)
                        elif it[0] == "v":
                            i = it[1]
                            s = plan.unit(i)[0]
                            for par in range(2):
                                last = pe.matmul(f[par * DH:(par + 1) * DH, 0:256],
                                                 sel[:, (i // NB) % 2, i % NB, NQ + NK:],
                                                 wv[:, (2 * s + par) * 256:(2 * s + par + 1) * 256],
                                                 start=True, stop=True, tile_position=(0, par * DH))
                        else:
                            j = it[1]
                            pe.wait_ge(normed, 2 * (j + 1))
                            for h in range(TT):
                                pe.transpose(f[:, h * P:(h + 1) * P], sq[:, j % (2 * NB), h, :], g.ident[:])
                            last = pe.transpose(f[0:H, 2 * P:3 * P], pn[:, j % 2, :], g.ident[:])
                        last.then_inc(f_mm, 1)

                    for i in range(U + plan.TAIL):
                        items = plan.steps[i]
                        if i == 0:
                            for it in items[:-1]:
                                item(it)
                            items = items[-1:]
                        if i < U:
                            group = i // NB
                            pe.wait_ge(f_cp, copied("k", group, 1))
                            pe.wait_ge(nullk, group + 1)
                            if i >= 1:
                                pe.wait_ge(shifted, i)
                            for h in range(H):
                                rows = slice((h % 2) * DH, (h % 2 + 1) * DH)
                                last = pe.matmul(S[:, h % 2, (h // 2) * (NK + 1):(h // 2 + 1) * (NK + 1)],
                                                 qT[rows, group % 2, h // 2, i % NB, :],
                                                 kT[rows, group % 2, h // 2, i % NB, :], start=True, stop=True)
                            last.then_inc(scored, 1)
                        for it in items:
                            item(it)
                        j = i - 1
                        if 0 <= j < U:
                            if j >= 1:
                                pe.wait_ge(prT_cp, j)
                            for c in range(4):
                                last = pe.transpose(PT[:, c * P:(c + 1) * P],
                                                    pr[:, j % 2, 2 * c:2 * c + 2, :].rearrange("p h k -> p (h k)"),
                                                    g.ident[:])
                            last.then_inc(turned, 1)
                        j = i - 2
                        if 0 <= j < U:
                            s = plan.unit(j)[0]
                            pe.wait_ge(prT_cp, j + 1)
                            if j >= 1:
                                pe.wait_ge(oT_cp, j)
                            for c in range(4):
                                pe.matmul(OT[:, c * P:(c + 1) * P], g.big("r_nv")[:, (4 * s + c) * P:(4 * s + c + 1) * P],
                                          pnT[:, j % 2, :], start=(c == 0), stop=False, skip_group_check=True)
                            for h in range(H):
                                rows = slice((h % 2) * DH, (h % 2 + 1) * DH)
                                c = h // 2
                                last = pe.matmul(OT[rows, c * P:(c + 1) * P], v[rows, j % 3, c * DH:(c + 1) * DH],
                                                 prT[rows, j % 2, c * P:(c + 1) * P], start=False, stop=(h == H - 1),
                                                 skip_group_check=True)
                            last.then_inc(pv, 1)
                        j = i - 3
                        if 0 <= j < U:
                            s = plan.unit(j)[0]
                            pe.wait_ge(oT_cp, j + 1)
                            if j >= 1:
                                pe.wait_ge(o_cp, j)
                            for c in range(4):
                                last = pe.matmul(OUT[:, 0:D], oT[:, j % 2, c * P:(c + 1) * P],
                                                 wo[:, (4 * s + c) * P:(4 * s + c + 1) * P],
                                                 start=(c == 0), stop=(c == 3))
                            last.then_inc(projected, 1)
                        j = i - 4
                        if 0 <= j < U:
                            pe.wait_ge(o_cp, j + 1)
                            if j >= 1:
                                pe.wait_ge(added, TT * j)
                            for h in range(TT):
                                last = pe.matmul(X[:, h * D:(h + 1) * D], sqT[:, j % 4, h * P:(h + 1) * P],
                                                 o[:, j % 2, :], start=True, stop=True)
                            last.then_inc(scattered, 1)

                @block.scalar
                def _(act):
                    for i in range(U + plan.TAIL):
                        for it in plan.steps[i]:
                            n = plan.number[it]
                            f = F[:, n % 2, :]
                            if it[0] == "turn":
                                continue
                            act.wait_ge(f_mm, n + 1)
                            if it[0] == "gather":
                                _, group, k = it
                                act.activation(sel[:, group % 2, 2 * k:2 * k + 2, :],
                                               f.rearrange("p (b s) -> p b s", b=2), ACT.Copy).then_inc(f_cp, 1)
                            elif it[0] == "q":
                                _, group, c = it
                                act.activation(qT[:, group % 2, c, :, :], f.rearrange("p (b s) -> p b s", b=NB),
                                               ACT.Copy).then_inc(f_cp, 1)
                            elif it[0] == "k":
                                _, group, k = it
                                act.activation(kT[:, group % 2, 2 * k:2 * k + 2, :, 0:NK],
                                               f.rearrange("p (c b s) -> p c b s", c=2, b=NB),
                                               ACT.Copy).then_inc(f_cp, 1)
                            else:
                                act.activation(v[:, it[1] % 3, :], f[:, 0:256], ACT.Copy).then_inc(f_cp, 1)
                        if i < U:
                            act.wait_ge(shifted, i + 1)
                            act.activation(ev[:, i % 2, :, :, :], ev[:, i % 2, :, :, :], ACT.Exp,
                                           scale=DH ** -0.5).then_inc(expd, 1)
                        j = i - 1
                        if 0 <= j < U:
                            n = plan.number[("turn", j)]
                            f = F[:, n % 2, :]
                            act.wait_ge(f_mm, n + 1)
                            act.activation(sqT[:, j % 4, :], f[:, 0:2 * P], ACT.Copy)
                            act.activation(pnT[:, j % 2, :], f[0:H, 2 * P:3 * P], ACT.Copy).then_inc(f_cp, 1)
                            act.wait_ge(turned, j + 1)
                            act.activation(prT[:, j % 2, :], PT[:], ACT.Copy).then_inc(prT_cp, 1)
                        j = i - 2
                        if 0 <= j < U:
                            act.wait_ge(pv, j + 1)
                            act.activation(oT[:, j % 2, :], OT[:], ACT.Copy).then_inc(oT_cp, 1)

                @block.gpsimd
                def _(pool):
                    def scale_onehots(group):
                        s = plan.unit(group * NB)[0]
                        if group >= 2:
                            pool.wait_ge(scored, (group - 1) * NB)
                        pool.tensor_copy(kT[:, group % 2, :, :, NK],
                                         g.big("r_nk")[:, 4 * s:4 * s + 4].unsqueeze(2).to_broadcast([P, 4, NB]))\
                            .then_inc(nullk, 1)
                        for k in range(NB):
                            u = group * NB + k
                            b = plan.unit(u)[1]
                            pool.wait_ge(onehots, 2 * (u + 1))
                            if u >= 2 * NB:
                                pool.wait_ge(f_mm, plan.number[("turn", u - 2 * NB)] + 1)
                            pool.tensor_tensor(sq[:, u % (2 * NB), :, :], oh[:, k, :, 0:NQ],
                                               sig[:, :, b, s:s + 1].to_broadcast([P, TT, NQ]), ALU.mult)
                            pool.tensor_tensor(oh[:, k, :, NQ + NK:], oh[:, k, :, NQ:NQ + NK],
                                               sig[:, :, b, G + s:G + s + 1].to_broadcast([P, TT, NK]),
                                               ALU.mult).then_inc(scaled, 1)

                    scale_onehots(0)
                    for i in range(U):
                        if i % NB == 0 and i // NB + 1 < plan.GROUPS:
                            scale_onehots(i // NB + 1)
                        pool.wait_ge(recip, i + 1)
                        if i >= 2:
                            pool.wait_ge(turned, i - 1)
                        pool.tensor_tensor(pr[:, i % 2, :, :].rearrange("p (c q) k -> p q c k", q=2),
                                           ev[:, i % 2, :, :, 0:NK],
                                           rsum[:, i % 2, :, :].unsqueeze(3).to_broadcast([P, 2, 4, NK]),
                                           ALU.mult).then_inc(normed, 1)
                        pool.tensor_tensor(pn[:, i % 2, :].rearrange("p (c q) -> p q c", q=2),
                                           ev[:, i % 2, :, :, NK], rsum[:, i % 2, :, :], ALU.mult)\
                            .then_inc(normed, 1)

                @block.vector
                def _(dve):
                    def make_onehots(group):
                        s = plan.unit(group * NB)[0]
                        if group >= 1:
                            dve.wait_ge(f_mm, plan.number[("gather", group - 1, 1)] + 1)
                        for k in range(NB):
                            b = plan.unit(group * NB + k)[1]
                            for lo, n, j in ((0, NQ, s), (NQ, NK, G + s)):
                                dve.tensor_tensor(oh[:, k, :, lo:lo + n],
                                                  g.iota_free[:, 0:n].unsqueeze(1).to_broadcast([P, TT, n]),
                                                  slot[:, :, b, j:j + 1].to_broadcast([P, TT, n]),
                                                  ALU.is_equal).then_inc(onehots, 1)

                    make_onehots(0)
                    for i in range(U + plan.TAIL):
                        if i < U:
                            s4 = S[:, :, 0:4 * (NK + 1)].rearrange("p i (h k) -> p i h k", h=4)
                            dve.wait_ge(scored, i + 1)
                            dve.tensor_reduce(mx[:, i % 2, :, :], s4, AX_X, ALU.max).then_inc(maxed, 1)
                            dve.wait_ge(maxed, i + 1)
                            if i >= 2:
                                dve.wait_ge(normed, 2 * (i - 1))
                            dve.tensor_tensor(ev[:, i % 2, :, :, :], s4,
                                              mx[:, i % 2, :, :].unsqueeze(3).to_broadcast([P, 2, 4, NK + 1]),
                                              ALU.subtract).then_inc(shifted, 1)
                            if i % NB == 0 and i // NB + 1 < plan.GROUPS:
                                make_onehots(i // NB + 1)
                            dve.wait_ge(expd, i + 1)
                            dve.tensor_reduce(rsum[:, i % 2, :, :], ev[:, i % 2, :, :, :], AX_X, ALU.add)\
                               .then_inc(summed, 1)
                            dve.wait_ge(summed, i + 1)
                            dve.reciprocal(rsum[:, i % 2, :, :], rsum[:, i % 2, :, :]).then_inc(recip, 1)
                        j = i - 3
                        if 0 <= j < U:
                            dve.wait_ge(projected, j + 1)
                            if j >= 2:
                                dve.wait_ge(scattered, j - 1)
                            dve.tensor_copy(o[:, j % 2, :], OUT[:, 0:D]).then_inc(o_cp, 1)
                        j = i - 4
                        if 0 <= j < U:
                            b = plan.unit(j)[1]
                            dve.wait_ge(scattered, j + 1)
                            for h in range(TT):
                                xt = g.x[:, TT * b + h, :]
                                dve.scalar_tensor_tensor(out=xt, in0=X[:, h * D:(h + 1) * D],
                                                         scalar=rcount[:, h, b:b + 1], in1=xt,
                                                         op0=ALU.mult, op1=ALU.add).then_inc(added, 1)


class Globals:

    def __init__(self, nc, stack, weights, a):
        def sb(name, shape, dt=F32):
            return stack.enter_context(nc.sbuf_tensor("all_" + name, shape, dt))

        self.a = a
        self.at = weights.at
        self.x = sb("x", [P, NT, D])
        self.h = sb("h", [P, NT, D])
        self.hT = sb("hT", [P, NTOK + 2 * T])
        self.W = sb("W", [P, weights.n])
        self.first_columns = weights.first_columns
        self.w_rest = nc.alloc_semaphore("w_rest")
        self.enc_layout = weights.enc_layout
        self.big_at = {**weights.routed.at, **weights.moe.at}
        self.big_n = {"routed": weights.routed.n, "moe": weights.moe.n}
        self.ident = sb("ident", [P, P])
        self.ident_bf = sb("ident_bf", [P, P], BF16)
        self.ones = sb("ones", [P, P])
        self.neg_half = sb("neg_half", [P, NT])
        self.eps = sb("eps", [P, TT])
        self.causal01 = sb("causal01", [P, T])
        self.masks = {m: sb(f"mask_{m}", [P, TT, T], BF16) for m in ("causal", "window")}

    def w(self, name):
        c, n, rows = self.at[name]
        return self.W[0:rows, c:c + n]

    def big(self, name):
        c, n, rows = self.big_at[name]
        return self.BIG[0:rows, c:c + n]

    def has(self, name):
        return name in self.at


def load_stage(nc, g):
    with Stage(nc, "load") as st:
        x_in, zero, made, w_in = st.sem("x_in"), st.sem("zero"), st.sem("made"), st.sem("w_in")
        with nc.Block() as block:
            @block.sync
            def _(sp):
                sp.dma_start(g.x[:], g.a["x"].rearrange("b (t p) d -> p (b t) d", p=P)).then_inc(x_in, 16)
                n, first = g.W.shape[1], g.first_columns
                sp.dma_start(g.W[:, 0:first], g.a["weights"][:, 0:first]).then_inc(w_in, 16)
                half = (first + n) // 2
                sp.dma_start(g.W[:, first:half], g.a["weights"][:, first:half]).then_inc(g.w_rest, 16)
                sp.dma_start(g.W[:, half:n], g.a["weights"][:, half:n]).then_inc(g.w_rest, 16)
                sp.wait_ge(x_in, 16)
                sp.wait_ge(w_in, 16)

            @block.gpsimd
            def _(pool):
                pool.memset(g.ident[:], 0.0).then_inc(zero, 1)
                pool.memset(g.ident_bf[:], 0.0).then_inc(zero, 1)
                pool.memset(g.masks["causal"][:], 0.0).then_inc(zero, 1)
                pool.memset(g.masks["window"][:], 0.0).then_inc(zero, 1)
                pool.memset(g.ones[:], 1.0)
                pool.memset(g.neg_half[:], -0.5)
                pool.memset(g.eps[:], LN_EPS)
                pool.memset(g.hT[:, NTOK:], 0.0)
                pool.memset(g.causal01[:], 1.0).then_inc(zero, 1)
                pool.wait_ge(zero, 5)
                pool.affine_select(out=g.causal01[:], in_=g.causal01[:], compare_op=ALU.is_ge, fill=0.0,
                                   base=0, pattern=[[1, T]], channel_multiplier=-1)
                for m in (g.ident, g.ident_bf):
                    pool.affine_select(out=m[:], in_=m[:], compare_op=ALU.not_equal, fill=1.0, base=0,
                                       pattern=[[-1, P]], channel_multiplier=1)
                for m in ("causal", "window"):
                    pool.affine_select(out=g.masks[m][:], in_=g.masks[m][:], compare_op=ALU.is_ge, fill=NEG,
                                       base=0, pattern=[[P, TT], [-1, T]], channel_multiplier=1).then_inc(made, 1)
                pool.wait_ge(made, 2)
                m = g.masks["window"]
                pool.affine_select(out=m[:], in_=m[:], compare_op=ALU.is_ge, fill=NEG,
                                   base=63, pattern=[[-P, TT], [1, T]], channel_multiplier=-1)


def wait_stage(nc, g):
    with nc.Block() as block:
        @block.sync
        def _(sp):
            sp.wait_ge(g.w_rest, 32)
    nc.all_engine_barrier()


def load_big_stage(nc, g, which, iota, n, stack):
    g.BIG = stack.enter_context(nc.sbuf_tensor(f"big{n}", [P, g.big_n[which]], F32))
    g.iota_free = stack.enter_context(nc.sbuf_tensor(f"iota{n}", [P, iota], F32))
    with Stage(nc, f"load_big{n}") as st:
        loaded = st.sem("loaded")
        with nc.Block() as block:
            @block.sync
            def _(sp):
                width = g.big_n[which]
                half = width // 2
                sp.dma_start(g.BIG[:, 0:half], g.a[which][:, 0:half]).then_inc(loaded, 16)
                sp.dma_start(g.BIG[:, half:width], g.a[which][:, half:width]).then_inc(loaded, 16)
                sp.wait_ge(loaded, 32)

            @block.gpsimd
            def _(pool):
                pool.iota(g.iota_free[:], pattern=[[1, iota]], base=0, channel_multiplier=0,
                          allow_small_or_imprecise_dtypes=True)


def store_stage(nc, g):
    with Stage(nc, "store") as st:
        out_done = st.sem("out_done")
        with nc.Block() as block:
            @block.sync
            def _(sp):
                sp.dma_start(g.a["out"].rearrange("b (t p) d -> p (b t) d", p=P), g.x[:]).then_inc(out_done, 16)
                sp.wait_ge(out_done, 16)


LAYERS = ["L0_attn_a", "L0_ffn", "L0_attn_b", "L0_ffn", "L1_attn_a", "L1_ffn", "L1_attn_b", "L1_ffn",
          "L2_attn_a", "L2_ffn", "L2_attn_b", "L2_ffn", "L3_attn_a", "L3_ffn", "L3_attn_b", "L3_ffn"]


def build_program(nc, weights, a, layers=range(16)):
    with ExitStack() as stack:
        g = Globals(nc, stack, weights, a)
        load_stage(nc, g)
        if layers[0] != 0:
            wait_stage(nc, g)
        big = ExitStack()
        for n in layers:
            if n == min({1, 3} & set(layers), default=None):
                load_big_stage(nc, g, "routed", P, n, big)
            if n == min({9, 11} & set(layers), default=None):
                load_big_stage(nc, g, "moe", MOE_E * MOE_CAP, n, big)
            layer_norm_stage(nc, g, f"ln{n}")
            name = LAYERS[n]
            if name == "L0_attn_a":
                mamba_stage(nc, g, f"s{n}")
            elif name == "L0_ffn":
                routed_attention_stage(nc, g, f"s{n}")
            elif name == "L0_attn_b":
                attention_stage(nc, g, f"s{n}", "L0b_", 8, 8 ** -0.5, mask="causal")
            elif name == "L2_attn_b":
                attention_stage(nc, g, f"s{n}", "L2b_", 8, 128 ** -0.5)
            elif name == "L1_attn_b":
                linear_attention_stage(nc, g, f"s{n}")
            elif name == "L1_attn_a":
                alibi_attention_stage(nc, g, f"s{n}")
            elif name == "L3_attn_a":
                attention_stage(nc, g, f"s{n}", "L3a_", 64, 64 ** -0.5)
            elif name == "L1_ffn":
                channel_mix_stage(nc, g, f"s{n}")
            elif name == "L2_attn_a":
                kernel_attention_stage(nc, g, f"s{n}")
            elif name == "L2_ffn":
                moe_stage(nc, g, f"s{n}")
            elif name == "L3_ffn":
                encoder_stage(nc, g, f"s{n}")
            elif name == "L3_attn_b":
                attention_stage(nc, g, f"s{n}", "L3b_", 8, 8 ** -0.5, mask="window")
            if n == 0:
                wait_stage(nc, g)
            if n in (3, 11):
                big.close()
                big = ExitStack()
        big.close()
        store_stage(nc, g)



def head_chunks(w, hd):
    hs = 32 if hd <= 32 else 64
    out = np.zeros((w.shape[1], w.shape[0] // hd, hs), w.dtype)
    out[:, :, :hd] = w.T.reshape(w.shape[1], -1, hd)
    return out.reshape(w.shape[1], -1)


def head_rows(w, hd):
    hs = 32 if hd <= 32 else 64
    out = np.zeros((w.shape[0] // hd, hs, w.shape[1]), w.dtype)
    out[:, :hd] = w.reshape(-1, hd, w.shape[1])
    return out.reshape(-1, P, w.shape[1]).transpose(1, 0, 2).reshape(P, -1)


def head_columns(b, hd):
    hs = 32 if hd <= 32 else 64
    out = np.zeros((b.shape[0] // hd, hs), b.dtype)
    out[:, :hd] = b.reshape(-1, hd)
    return out.reshape(-1, P).T


def pack(i):
    W = Weights()
    W.add("m_in_w", i["L0_attn_a_in_proj_w"].T)
    W.add("m_in_b", i["L0_attn_a_in_proj_b"].reshape(4, P).T)
    W.add("m_conv_w", i["L0_attn_a_conv_w"].reshape(2, P, 4).transpose(1, 0, 2).reshape(P, 8))
    W.add("m_conv_b", i["L0_attn_a_conv_b"].reshape(2, P).T)
    xw = np.zeros((P, 2, 80), np.float32)
    xp = i["L0_attn_a_x_proj_w"].reshape(-1, 2, P).transpose(2, 1, 0)
    xw[:, :, 0:DT_RANK] = xp[:, :, 0:DT_RANK]
    xw[:, :, 32:32 + STATE] = xp[:, :, DT_RANK:DT_RANK + STATE]
    xw[:, :, 64:64 + STATE] = xp[:, :, DT_RANK + STATE:]
    W.add("m_x_w", xw.reshape(P, -1))
    W.add("m_dt_w", i["L0_attn_a_dt_proj_w"].T)
    W.add("m_dt_b", i["L0_attn_a_dt_proj_b"].reshape(2, P).T)
    W.add("m_a_log", i["L0_attn_a_A_log"].reshape(2, P, STATE).transpose(1, 0, 2).reshape(P, -1))
    W.add("m_d", i["L0_attn_a_D_param"].reshape(2, P).T)
    W.add("m_out_w", i["L0_attn_a_out_proj_w"].T.reshape(2, P, D).transpose(1, 0, 2).reshape(P, -1))
    W.add("m_out_b", i["L0_attn_a_out_proj_b"][None])
    W.first_columns = W.n
    w, b = i["L0_attn_b_W"], i["L0_attn_b_b"]
    W.add("L0b_wq", head_chunks(w[:D], 8))
    W.add("L0b_wk", head_chunks(w[D:2 * D], 8))
    W.add("L0b_wv", w[2 * D:].T)
    W.add("L0b_wo", head_rows(np.eye(D, dtype=w.dtype), 8))
    W.add("L0b_bq", head_columns(b[:D], 8))
    W.add("L0b_bk", head_columns(b[D:2 * D], 8))
    W.add("L0b_bv", b[None, 2 * D:])
    W.add("L2b_wq", head_chunks(i["L2_attn_b_Wq"].T, 8))
    W.add("L2b_wk", head_chunks(i["L2_attn_b_Wk"].T, 8))
    W.add("L2b_wv", i["L2_attn_b_Wk"])
    W.add("L2b_wo", head_rows(np.eye(D, dtype=w.dtype), 8))
    W.add("L2b_bq", head_columns(i["L2_attn_b_bq"], 8))
    W.add("L2b_bk", head_columns(i["L2_attn_b_bk"], 8))
    W.add("L2b_bv", i["L2_attn_b_bk"][None])
    W.add("L3b_wq", head_chunks(i["L3_attn_b_Wq"], 8))
    W.add("L3b_wk", head_chunks(i["L3_attn_b_Wk"], 8))
    W.add("L3b_wv", i["L3_attn_b_Wv"].T)
    W.add("L3b_wo", head_rows(i["L3_attn_b_Wo"].T, 8))
    W.add("L3a_wq", head_chunks(i["L3_attn_a_Wq"], 64))
    W.add("L3a_wk", head_chunks(i["L3_attn_a_Wk"], 64))
    W.add("L3a_wv", i["L3_attn_a_Wv"].T)
    W.add("L3a_wo", head_rows(i["L3_attn_a_Wo"].T, 64))
    W.add("L3a_bq", head_columns(i["L3_attn_a_bq"], 64))
    W.add("L3a_bk", head_columns(i["L3_attn_a_bk"], 64))
    W.add("L3a_bv", i["L3_attn_a_bv"][None])
    w = i["L1_attn_b_w_attn"]
    W.add("L1b_wq", head_chunks(w[:D], 8))
    W.add("L1b_wk", head_chunks(w[D:2 * D], 8))
    W.add("L1b_wv", w[2 * D:].T)
    W.add("L1b_wo", i["L1_attn_b_w_proj"].T)
    W.add("L1a_wqk", i["L1_attn_a_W_qk"])
    W.add("L1a_wv", i["L1_attn_a_W_v"].T)
    W.add("L1a_slope", np.broadcast_to(i["L1_attn_a_alibi_slope"][None], (P, 1)))
    W.add("L3a_bo", np.broadcast_to(i["L3_attn_a_bo"][None], (P, D)))
    for n in "rkv":
        W.add(f"L1f_w{n}", i[f"L1_ffn_W_{n}"].T)
    W.add("L1f_mu", np.stack([i["L1_ffn_mu_r"], i["L1_ffn_mu_k"]], 1))
    W.add("L2a_wqk", np.concatenate([i["L2_attn_a_Wq"].T, i["L2_attn_a_Wk"].T], 1))
    W.add("L2a_bqk", np.stack([i["L2_attn_a_bq"], i["L2_attn_a_bk"]], 1))
    W.add("L2a_wv", i["L2_attn_a_Wv"].T)
    W.add("L2a_bv", i["L2_attn_a_bv"][None])
    W.add("L2a_wo", i["L2_attn_a_Wo"].T)
    W.add("L2a_bo", np.broadcast_to(i["L2_attn_a_bo"][None], (P, D)))
    r = np.zeros((16, 8, 16, 8), np.float32)
    blocks = np.zeros((16, 8, 16, 8), np.float32)
    for h in range(16):
        r[h, :, h] = i["L2_attn_a_R"]
        blocks[h, :, h] = 1.0
    W.add("L2a_rblk", r.reshape(P, P))
    W.add("L2a_blocks", blocks.reshape(P, P))
    nhalf = np.zeros((16, 8, 16, 8), np.float32)
    for h in range(16):
        nhalf[h, :, h] = -0.5
    W.add("L2a_nhalf", nhalf.reshape(P, P))
    W.add("L2a_headof", np.ascontiguousarray(blocks.reshape(P, 16, 8)[:, :, 0]))
    W.add("moe_rw", i["L2_ffn_router_w"])
    W.add("moe_rb", np.broadcast_to(i["L2_ffn_router_b"][None], (P, MOE_E)))
    W.add("moe_iota", np.broadcast_to(np.arange(MOE_E, dtype=np.float32)[None], (P, MOE_E)))
    keep = np.ones((P, MOE_E, NT), np.float32)
    keep[:, :, 0] = 0.0
    W.add("moe_keep", keep.reshape(P, -1))
    W.add("moe_rowid", (np.arange(P)[:, None] + P * np.arange(MOE_E + 2)[None]).astype(np.float32))
    M = W.moe = Weights()
    M.add("moe_w1", i["L2_ffn_w1"].transpose(1, 0, 2).reshape(D, -1))
    M.add("moe_w2", i["L2_ffn_w2"].reshape(MOE_E * 4, P, D).transpose(1, 0, 2).reshape(P, -1))
    M.add("moe_b1", i["L2_ffn_b1"].reshape(MOE_E * 4, P).T)
    M.add("moe_b2", i["L2_ffn_b2"].reshape(1, -1))
    M.add("moe_ow1", i["L2_ffn_ow1"])
    M.add("moe_ow2", i["L2_ffn_ow2"].reshape(4, P, D).transpose(1, 0, 2).reshape(P, -1))
    M.add("moe_ob1", i["L2_ffn_ob1"].reshape(4, P).T)
    M.add("moe_ob2", i["L2_ffn_ob2"][None])
    R = W.routed = Weights()
    R.add("r_wq", i["L0_ffn_w_q"].transpose(2, 0, 1).reshape(D, -1))
    wkv = i["L0_ffn_w_kv"].reshape(4, 2, 4, 2, 64, D)
    R.add("r_wk", wkv[:, 0].transpose(4, 0, 1, 2, 3).reshape(D, -1))
    R.add("r_wv", wkv[:, 1].transpose(4, 0, 2, 1, 3).reshape(D, -1))
    R.add("r_wo", i["L0_ffn_w_out"].transpose(2, 0, 1).reshape(4, P, 4, D).transpose(1, 2, 0, 3).reshape(P, -1))
    R.add("r_nk", i["L0_ffn_null_kv"][0].reshape(4, 4, P).transpose(2, 0, 1).reshape(P, -1))
    nv = np.zeros((4, 2, 4, 4, 2, 64), np.float32)
    for h in range(8):
        nv[h // 2, h % 2, :, h // 2, h % 2] = i["L0_ffn_null_kv"][1, :, h, 0]
    R.add("r_nv", nv.reshape(8, -1))
    W.add("r_router", np.concatenate([i["L0_ffn_w_qr"], i["L0_ffn_w_kvr"]], 0).T)
    W.add("r_null", np.broadcast_to(i["L0_ffn_null_token"][0], (P, D)))
    W.add("r_iskv", np.tile([0.0] * 4 + [1.0] * 4, B).astype(np.float32)[:, None])
    W.add("enc_gate_w", i["L3_ffn_gate_w"].T)
    W.add("enc_gate_b", np.broadcast_to(i["L3_ffn_gate_b"][None], (B, 4)))
    W.add("enc_iota", np.broadcast_to(np.arange(4, dtype=np.float32)[None], (B, 4)))
    experts = [encoder_weights(i, e) for e in range(4)]
    W.enc_layout = (experts[0][0].at, experts[0][0].n, experts[0][1].at, experts[0][1].n)
    W.enc_a = np.stack([e[0].packed() for e in experts])
    W.enc_b = np.stack([e[1].packed() for e in experts])
    return W


def encoder_weights(i, e):
    A, Bw = Weights(), Weights()
    p = {n: i["L3_ffn_" + n][e] for n in ("in_proj_w", "in_proj_b", "out_proj_w", "out_proj_b", "lin1_w",
                                          "lin1_b", "lin2_w", "lin2_b", "ln1_w", "ln1_b", "ln2_w", "ln2_b")}
    w, b = p["in_proj_w"], p["in_proj_b"]
    A.add("wq", head_chunks(w[:D], 8))
    A.add("wk", head_chunks(w[D:2 * D], 8))
    A.add("wv", w[2 * D:].T)
    A.add("bq", head_columns(b[:D], 8))
    A.add("bk", head_columns(b[D:2 * D], 8))
    A.add("bv", b[None, 2 * D:])
    Bw.add("wo", head_rows(p["out_proj_w"].T, 8))
    Bw.add("w1", p["lin1_w"].T)
    Bw.add("w2", p["lin2_w"].T.reshape(4, P, D).transpose(1, 0, 2).reshape(P, -1))
    Bw.add("b1", p["lin1_b"].reshape(4, P).T)
    for to, of in (("ob", "out_proj_b"), ("b2", "lin2_b"), ("n1w", "ln1_w"), ("n1b", "ln1_b"),
                   ("n2w", "ln2_w"), ("n2b", "ln2_b")):
        Bw.add(to, np.broadcast_to(p[of][None], (P, D)))
    return A, Bw


def kernel(**inputs):
    import concourse.bacc as _bacc
    from concourse.bass_utils import run_bass_kernel_spmd as _run

    nc = _bacc.Bacc("TRN2", target_bir_lowering=False, num_devices=1)
    weights = pack({k: np.asarray(v) for k, v in inputs.items()})
    arrays = {"x": np.ascontiguousarray(inputs["L0_attn_a_x"]), "weights": weights.packed(),
              "enc_a": weights.enc_a, "enc_b": weights.enc_b,
              "routed": weights.routed.packed(), "moe": weights.moe.packed()}
    a = {n: nc.dram_tensor(n, v.shape, mybir.dt.from_np(v.dtype), kind="ExternalInput").ap()
         for n, v in arrays.items()}
    a["out"] = nc.dram_tensor("out", (B, T, D), F32, kind="ExternalOutput").ap()
    build_program(nc, weights, a)
    r = _run(nc, [arrays], core_ids=[0])
    return r.results[0]["out"]
```
